# Optimizing a Trainium2 kernel written in Bass

```python
import numpy as np
import jax
import jax.numpy as jnp

def _softmax(x, axis=-1):
    return jax.nn.softmax(x, axis=axis)

def _gelu(x):
    return jax.nn.gelu(x, approximate=True)

def _silu(x):
    return jax.nn.silu(x)

def _sigmoid(x):
    return jax.nn.sigmoid(x)

def _layernorm(x, axis=-1, eps=1e-05):
    m = jnp.mean(x, axis=axis, keepdims=True)
    v = jnp.var(x, axis=axis, keepdims=True)
    return (x - m) / jnp.sqrt(v + eps)

def _scatter_add(tgt, idx, src, axis=0):
    return tgt.at[idx].add(src)

def _segment_sum(src, seg, n):
    return jax.ops.segment_sum(src, seg, n)
kernel_name = 'mk_seq_preln_d1_jaxref_r8_37d413'

def setup_inputs(seed: int=0):
    np.random.seed(seed)
    _w = jnp.asarray

    def _L0_attn_setup():
        import jax, jax.numpy as jnp
        import numpy as np
        from jax import lax
        D_MODEL, D_STATE, EXPAND, K = (128, 16, 2, 4)
        D_INNER = D_MODEL * EXPAND
        B, L = (2, 256)

        def _selective_ssm(x, A_log, D_skip, W_delta, b_delta, W_B, W_C):
            A = -jnp.exp(A_log)
            delta = jax.nn.softplus(x @ W_delta + b_delta)
            Bm = x @ W_B
            Cm = x @ W_C
            h0 = jnp.zeros((x.shape[0], A.shape[0], A.shape[1]), x.dtype)

            def step(h, inp):
                d_t, x_t, B_t, C_t = inp
                dA = jnp.exp(d_t[..., None] * A)
                h = dA * h + (d_t * x_t)[..., None] * B_t[:, None, :]
                y_t = jnp.einsum('bdn,bn->bd', h, C_t)
                return (h, y_t)
            xs = (delta.transpose(1, 0, 2), x.transpose(1, 0, 2), Bm.transpose(1, 0, 2), Cm.transpose(1, 0, 2))
            _, ys = lax.scan(step, h0, xs)
            return ys.transpose(1, 0, 2) + x * D_skip
        key = jax.random.key(seed)
        ks = jax.random.split(key, 16)
        s = lambda fan_in: 1.0 / np.sqrt(fan_in)
        inp = {'x': jax.random.normal(ks[0], (B, L, D_MODEL), jnp.float32), 'W_in': jax.random.normal(ks[1], (D_MODEL, D_INNER), jnp.float32) * s(D_MODEL), 'b_in': jnp.zeros((D_INNER,), jnp.float32), 'W_gate': jax.random.normal(ks[2], (D_MODEL, D_INNER), jnp.float32) * s(D_MODEL), 'b_gate': jnp.zeros((D_INNER,), jnp.float32), 'conv_w': jax.random.normal(ks[3], (D_INNER, 1, K), jnp.float32) * s(K), 'conv_b': jnp.zeros((D_INNER,), jnp.float32), 'A_log': jnp.log(jnp.broadcast_to(jnp.arange(1, D_STATE + 1, dtype=jnp.float32), (D_INNER, D_STATE))), 'D_skip': jnp.ones((D_INNER,), jnp.float32), 'W_delta': jax.random.normal(ks[4], (D_INNER, D_INNER), jnp.float32) * s(D_INNER), 'b_delta': jnp.zeros((D_INNER,), jnp.float32), 'W_B': jax.random.normal(ks[5], (D_INNER, D_STATE), jnp.float32) * s(D_INNER), 'W_C': jax.random.normal(ks[6], (D_INNER, D_STATE), jnp.float32) * s(D_INNER), 'W_out': jax.random.normal(ks[7], (D_INNER, D_MODEL), jnp.float32) * s(D_INNER), 'b_out': jnp.zeros((D_MODEL,), jnp.float32)}
        return inp
    _L0_attn_in = _L0_attn_setup()

    def _L0_ffn_setup():
        import jax, jax.numpy as jnp
        import numpy as np
        DIM = 128
        DEPTH = 6
        HEADS = 16
        DIM_HEAD = 64
        WINDOW = 32
        INNER = HEADS * DIM_HEAD
        DIM_INNER = int(DIM * 4 * 2 / 3)
        QK_SCALE = 8.0

        def shift_tokens(t):
            a, s = jnp.split(t, 2, -1)
            s = jnp.pad(s, ((0, 0), (1, 0), (0, 0)))[:, :-1]
            return jnp.concatenate([a, s], -1)

        def l2norm(t):
            return t / jnp.maximum(jnp.linalg.norm(t, axis=-1, keepdims=True), 1e-12)

        def rotate_half(x):
            x1, x2 = jnp.split(x, 2, -1)
            return jnp.concatenate([-x2, x1], -1)

        def rotary_tables(n):
            half = jnp.arange(0, DIM_HEAD, 2, dtype=jnp.float32)
            inv_freq = 1.0 / 10000.0 ** (half / DIM_HEAD)
            t = jnp.arange(n, dtype=jnp.float32)
            freqs = t[:, None] * inv_freq[None, :]
            freqs = jnp.concatenate([freqs, freqs], -1)
            base_scale = (half + 0.4 * DIM_HEAD) / (1.4 * DIM_HEAD)
            power = (t - n // 2) / (WINDOW // 2)
            scale = base_scale[None, :] ** power[:, None]
            scale = jnp.concatenate([scale, scale], -1)
            return (freqs, scale)

        def local_attention(q, k, v):
            b, h, n, d = q.shape
            w = WINDOW
            nw = n // w
            bq = q.reshape(b, h, nw, w, d)
            bk = k.reshape(b, h, nw, w, d)
            bv = v.reshape(b, h, nw, w, d)

            def look(t):
                p = jnp.pad(t, ((0, 0), (0, 0), (1, 0), (0, 0), (0, 0)))
                return jnp.concatenate([p[:, :, :nw], p[:, :, 1:]], axis=3)
            bk2, bv2 = (look(bk), look(bv))
            seq = jnp.arange(n).reshape(nw, w)
            seq_p = jnp.pad(seq, ((1, 0), (0, 0)), constant_values=-1)
            jt = jnp.concatenate([seq_p[:nw], seq_p[1:]], axis=1)
            it = seq[:, :, None]
            jb = jt[:, None, :]
            mask = (it < jb) | (it > jb + w) | (jb == -1)
            sim = jnp.einsum('bhwie,bhwje->bhwij', bq, bk2) * QK_SCALE
            sim = jnp.where(mask, -jnp.finfo(sim.dtype).max, sim)
            attn = jax.nn.softmax(sim, -1)
            out = jnp.einsum('bhwij,bhwje->bhwie', attn, bv2)
            return out.reshape(b, h, n, d)

        def attn_layer(x, Wqkv, qs, ksc, Wo):
            b, n, _ = x.shape
            qkv = x @ Wqkv
            q, k, v = jnp.split(qkv, 3, -1)
            sh = lambda t: t.reshape(b, n, HEADS, DIM_HEAD).transpose(0, 2, 1, 3)
            q, k, v = (sh(q), sh(k), sh(v))
            q = l2norm(q) * qs
            k = l2norm(k) * ksc
            freqs, scale = rotary_tables(n)
            cos, sin = (jnp.cos(freqs), jnp.sin(freqs))
            q = q * cos * scale + rotate_half(q) * sin * scale
            inv = 1.0 / scale
            k = k * cos * inv + rotate_half(k) * sin * inv
            out = local_attention(q, k, v)
            out = out.transpose(0, 2, 1, 3).reshape(b, n, INNER)
            return out @ Wo

        def ffn_layer(x, g, bln, W1, b1, W2, b2):
            mu = x.mean(-1, keepdims=True)
            var = ((x - mu) ** 2).mean(-1, keepdims=True)
            xn = (x - mu) / jnp.sqrt(var + 1e-05) * g + bln
            hg = xn @ W1 + b1
            a, gate = jnp.split(hg, 2, -1)
            return a * jax.nn.gelu(gate, approximate=False) @ W2 + b2
        key = jax.random.key(seed)
        ks = jax.random.split(key, 8)
        B, N = (2, 256)
        init = lambda k, shape: jax.random.normal(k, shape, jnp.float32) * 0.02
        return {'x': jax.random.normal(ks[0], (B, N, DIM), jnp.float32), 'Wqkv': init(ks[1], (DEPTH, DIM, 3 * INNER)), 'q_scale': jnp.ones((DEPTH, DIM_HEAD), jnp.float32), 'k_scale': jnp.ones((DEPTH, DIM_HEAD), jnp.float32), 'Wo': init(ks[2], (DEPTH, INNER, DIM)), 'ln_g': jnp.ones((DEPTH, DIM), jnp.float32), 'ln_b': jnp.zeros((DEPTH, DIM), jnp.float32), 'W1': init(ks[3], (DEPTH, DIM, 2 * DIM_INNER)), 'b1': jnp.zeros((DEPTH, 2 * DIM_INNER), jnp.float32), 'W2': init(ks[4], (DEPTH, DIM_INNER, DIM)), 'b2': jnp.zeros((DEPTH, DIM), jnp.float32)}
    _L0_ffn_in = _L0_ffn_setup()
    _d = {'L0_attn_x': _L0_attn_in['x'], 'L0_attn_W_in': _L0_attn_in['W_in'], 'L0_attn_b_in': _L0_attn_in['b_in'], 'L0_attn_W_gate': _L0_attn_in['W_gate'], 'L0_attn_b_gate': _L0_attn_in['b_gate'], 'L0_attn_conv_w': _L0_attn_in['conv_w'], 'L0_attn_conv_b': _L0_attn_in['conv_b'], 'L0_attn_A_log': _L0_attn_in['A_log'], 'L0_attn_D_skip': _L0_attn_in['D_skip'], 'L0_attn_W_delta': _L0_attn_in['W_delta'], 'L0_attn_b_delta': _L0_attn_in['b_delta'], 'L0_attn_W_B': _L0_attn_in['W_B'], 'L0_attn_W_C': _L0_attn_in['W_C'], 'L0_attn_W_out': _L0_attn_in['W_out'], 'L0_attn_b_out': _L0_attn_in['b_out'], 'L0_ffn_Wqkv': _L0_ffn_in['Wqkv'], 'L0_ffn_q_scale': _L0_ffn_in['q_scale'], 'L0_ffn_k_scale': _L0_ffn_in['k_scale'], 'L0_ffn_Wo': _L0_ffn_in['Wo'], 'L0_ffn_ln_g': _L0_ffn_in['ln_g'], 'L0_ffn_ln_b': _L0_ffn_in['ln_b'], 'L0_ffn_W1': _L0_ffn_in['W1'], 'L0_ffn_b1': _L0_ffn_in['b1'], 'L0_ffn_W2': _L0_ffn_in['W2'], 'L0_ffn_b2': _L0_ffn_in['b2']}
    _x0 = _d['L0_attn_x']
    _d['L0_attn_x'] = jax.random.normal(jax.random.fold_in(jax.random.key(seed), 1), (16, 256, 128), dtype=_x0.dtype)
    del _x0
    return _d

def reference(L0_attn_x, L0_attn_W_in, L0_attn_b_in, L0_attn_W_gate, L0_attn_b_gate, L0_attn_conv_w, L0_attn_conv_b, L0_attn_A_log, L0_attn_D_skip, L0_attn_W_delta, L0_attn_b_delta, L0_attn_W_B, L0_attn_W_C, L0_attn_W_out, L0_attn_b_out, L0_ffn_Wqkv, L0_ffn_q_scale, L0_ffn_k_scale, L0_ffn_Wo, L0_ffn_ln_g, L0_ffn_ln_b, L0_ffn_W1, L0_ffn_b1, L0_ffn_W2, L0_ffn_b2):

    def _L0_attn_ref(x, W_in, b_in, W_gate, b_gate, conv_w, conv_b, A_log, D_skip, W_delta, b_delta, W_B, W_C, W_out, b_out):
        import jax, jax.numpy as jnp
        import numpy as np
        from jax import lax
        D_MODEL, D_STATE, EXPAND, K = (128, 16, 2, 4)
        D_INNER = D_MODEL * EXPAND
        B, L = (2, 256)

        def _selective_ssm(x, A_log, D_skip, W_delta, b_delta, W_B, W_C):
            A = -jnp.exp(A_log)
            delta = jax.nn.softplus(x @ W_delta + b_delta)
            Bm = x @ W_B
            Cm = x @ W_C
            h0 = jnp.zeros((x.shape[0], A.shape[0], A.shape[1]), x.dtype)

            def step(h, inp):
                d_t, x_t, B_t, C_t = inp
                dA = jnp.exp(d_t[..., None] * A)
                h = dA * h + (d_t * x_t)[..., None] * B_t[:, None, :]
                y_t = jnp.einsum('bdn,bn->bd', h, C_t)
                return (h, y_t)
            xs = (delta.transpose(1, 0, 2), x.transpose(1, 0, 2), Bm.transpose(1, 0, 2), Cm.transpose(1, 0, 2))
            _, ys = lax.scan(step, h0, xs)
            return ys.transpose(1, 0, 2) + x * D_skip
        xz = x @ W_in + b_in
        x_gate = x @ W_gate + b_gate
        x_conv = lax.conv_general_dilated(xz.transpose(0, 2, 1), conv_w, window_strides=(1,), padding=[(K - 1, 0)], dimension_numbers=('NCH', 'OIH', 'NCH'), feature_group_count=D_INNER)
        x_conv = x_conv.transpose(0, 2, 1) + conv_b
        act = jax.nn.silu(x_conv)
        ssm_out = _selective_ssm(act, A_log, D_skip, W_delta, b_delta, W_B, W_C)
        gated = ssm_out * jax.nn.silu(x_gate)
        return gated @ W_out + b_out

    def _L0_ffn_ref(x, Wqkv, q_scale, k_scale, Wo, ln_g, ln_b, W1, b1, W2, b2):
        import jax, jax.numpy as jnp
        import numpy as np
        DIM = 128
        DEPTH = 6
        HEADS = 16
        DIM_HEAD = 64
        WINDOW = 32
        INNER = HEADS * DIM_HEAD
        DIM_INNER = int(DIM * 4 * 2 / 3)
        QK_SCALE = 8.0

        def shift_tokens(t):
            a, s = jnp.split(t, 2, -1)
            s = jnp.pad(s, ((0, 0), (1, 0), (0, 0)))[:, :-1]
            return jnp.concatenate([a, s], -1)

        def l2norm(t):
            return t / jnp.maximum(jnp.linalg.norm(t, axis=-1, keepdims=True), 1e-12)

        def rotate_half(x):
            x1, x2 = jnp.split(x, 2, -1)
            return jnp.concatenate([-x2, x1], -1)

        def rotary_tables(n):
            half = jnp.arange(0, DIM_HEAD, 2, dtype=jnp.float32)
            inv_freq = 1.0 / 10000.0 ** (half / DIM_HEAD)
            t = jnp.arange(n, dtype=jnp.float32)
            freqs = t[:, None] * inv_freq[None, :]
            freqs = jnp.concatenate([freqs, freqs], -1)
            base_scale = (half + 0.4 * DIM_HEAD) / (1.4 * DIM_HEAD)
            power = (t - n // 2) / (WINDOW // 2)
            scale = base_scale[None, :] ** power[:, None]
            scale = jnp.concatenate([scale, scale], -1)
            return (freqs, scale)

        def local_attention(q, k, v):
            b, h, n, d = q.shape
            w = WINDOW
            nw = n // w
            bq = q.reshape(b, h, nw, w, d)
            bk = k.reshape(b, h, nw, w, d)
            bv = v.reshape(b, h, nw, w, d)

            def look(t):
                p = jnp.pad(t, ((0, 0), (0, 0), (1, 0), (0, 0), (0, 0)))
                return jnp.concatenate([p[:, :, :nw], p[:, :, 1:]], axis=3)
            bk2, bv2 = (look(bk), look(bv))
            seq = jnp.arange(n).reshape(nw, w)
            seq_p = jnp.pad(seq, ((1, 0), (0, 0)), constant_values=-1)
            jt = jnp.concatenate([seq_p[:nw], seq_p[1:]], axis=1)
            it = seq[:, :, None]
            jb = jt[:, None, :]
            mask = (it < jb) | (it > jb + w) | (jb == -1)
            sim = jnp.einsum('bhwie,bhwje->bhwij', bq, bk2) * QK_SCALE
            sim = jnp.where(mask, -jnp.finfo(sim.dtype).max, sim)
            attn = jax.nn.softmax(sim, -1)
            out = jnp.einsum('bhwij,bhwje->bhwie', attn, bv2)
            return out.reshape(b, h, n, d)

        def attn_layer(x, Wqkv, qs, ksc, Wo):
            b, n, _ = x.shape
            qkv = x @ Wqkv
            q, k, v = jnp.split(qkv, 3, -1)
            sh = lambda t: t.reshape(b, n, HEADS, DIM_HEAD).transpose(0, 2, 1, 3)
            q, k, v = (sh(q), sh(k), sh(v))
            q = l2norm(q) * qs
            k = l2norm(k) * ksc
            freqs, scale = rotary_tables(n)
            cos, sin = (jnp.cos(freqs), jnp.sin(freqs))
            q = q * cos * scale + rotate_half(q) * sin * scale
            inv = 1.0 / scale
            k = k * cos * inv + rotate_half(k) * sin * inv
            out = local_attention(q, k, v)
            out = out.transpose(0, 2, 1, 3).reshape(b, n, INNER)
            return out @ Wo

        def ffn_layer(x, g, bln, W1, b1, W2, b2):
            mu = x.mean(-1, keepdims=True)
            var = ((x - mu) ** 2).mean(-1, keepdims=True)
            xn = (x - mu) / jnp.sqrt(var + 1e-05) * g + bln
            hg = xn @ W1 + b1
            a, gate = jnp.split(hg, 2, -1)
            return a * jax.nn.gelu(gate, approximate=False) @ W2 + b2
        for i in range(DEPTH):
            x = attn_layer(shift_tokens(x), Wqkv[i], q_scale[i], k_scale[i], Wo[i]) + x
            x = ffn_layer(shift_tokens(x), ln_g[i], ln_b[i], W1[i], b1[i], W2[i], b2[i]) + x
        return x
    x = L0_attn_x
    x = x + _L0_attn_ref(_layernorm(x, axis=-1), L0_attn_W_in, L0_attn_b_in, L0_attn_W_gate, L0_attn_b_gate, L0_attn_conv_w, L0_attn_conv_b, L0_attn_A_log, L0_attn_D_skip, L0_attn_W_delta, L0_attn_b_delta, L0_attn_W_B, L0_attn_W_C, L0_attn_W_out, L0_attn_b_out)
    x = x + _L0_ffn_ref(_layernorm(x, axis=-1), L0_ffn_Wqkv, L0_ffn_q_scale, L0_ffn_k_scale, L0_ffn_Wo, L0_ffn_ln_g, L0_ffn_ln_b, L0_ffn_W1, L0_ffn_b1, L0_ffn_W2, L0_ffn_b2)
    return x

_drawn_inputs = setup_inputs


def setup_inputs(seed=0):
    import zlib

    import numpy as np

    out = dict(_drawn_inputs(seed))
    spreads = {'L0_attn_b_in': (0.0, 0.1),
     'L0_attn_b_gate': (0.0, 0.1),
     'L0_attn_conv_b': (0.0, 0.1),
     'L0_attn_D_skip': (1.0, 0.2),
     'L0_attn_b_delta': (0.0, 0.325),
     'L0_attn_b_out': (0.0, 0.1),
     'L0_ffn_q_scale': (1.0, 0.6),
     'L0_ffn_k_scale': (1.0, 0.6),
     'L0_ffn_ln_g': (1.0, 0.6),
     'L0_ffn_ln_b': (0.0, 0.8),
     'L0_ffn_b1': (0.0, 0.8),
     'L0_ffn_b2': (0.0, 0.1)}
    factors = {'L0_ffn_W1': 3.884, 'L0_ffn_W2': 3.823}
    for name, (base, spread) in spreads.items():
        noise = np.random.default_rng([zlib.crc32(name.encode()), seed]).standard_normal(out[name].shape)
        drawn = base * np.exp(spread * noise) if base else spread * noise
        out[name] = jnp.asarray(drawn.astype(out[name].dtype))
    for name, factor in factors.items():
        out[name] = (out[name] * factor).astype(out[name].dtype)
    return out
```

```python
import concourse.bass as bass
from concourse import mybir
from contextlib import ExitStack

BATCH, SEQ, DIM = 16, 256, 128
TOKENS = BATCH * SEQ
P = 128
GROUP = 512
GROUPS = TOKENS // GROUP
SEQ_PER_GROUP = GROUP // SEQ
CHUNKS = SEQ // P
D_INNER, D_STATE, CONV = 256, 16, 4
MT = D_INNER // P
DEPTH, HEADS, HEAD, WINDOW = 6, 16, 64, 32
INNER = HEADS * HEAD
HALF = HEAD // 2
PAIRS = HEADS // 2
HID = int(DIM * 4 * 2 / 3)
HT = [(m * P, min(P, HID - m * P)) for m in range((HID + P - 1) // P)]
NHT = len(HT)
KEYS_B = P + WINDOW
FIRST_B = P - WINDOW
QKV_BANKS = 3
NP_BUF = 4

ORDER = [(0, 0), (0, 2), (0, 1), (0, 3), (0, 4), (0, 5), (1, 0), (1, 2), (1, 1), (1, 3), (1, 4), (1, 5)]
UNITS = len(ORDER)
QK = [n for n, (c, j) in enumerate(ORDER) if j < 4]
VU = [n for n, (c, j) in enumerate(ORDER) if j >= 4]
NQK = len(QK)
TR_AT = {un + 2: n for n, un in enumerate(QK)}
R_AT = {un + 1: n for n, un in enumerate(QK)}
SLOT_UNITS = [[0, 1], [2], [3, 4], [5], [6, 7], [8], [9, 10], [11]]

LN_SCALE = float(2 ** 32)
NORM_FLOOR = 1e-24
LN_EPS = 1e-5
MASKED = -3.0e38
EXP_LN_SET = "natural_log_exp_and_others"


def build(nc, t, out):
    f32, bf16 = mybir.dt.float32, mybir.dt.bfloat16
    ALU, ACT, AX = mybir.AluOpType, mybir.ActivationFunctionType, mybir.AxisListType
    ctx = ExitStack()
    with ctx:
        def sb(name, shape, dt=f32):
            return ctx.enter_context(nc.sbuf_tensor(name, shape, dt))

        credit = {}

        def sem(name, credits=0):
            s = ctx.enter_context(nc.semaphore(name))
            credit[name] = credits
            return (s, credits)

        def item(e, s, n):
            e.wait_ge(s[0], n + (1 + s[1]))

        def slot(e, s, n):
            e.wait_ge(s[0], n + 1)

        def give_credits(e, sems):
            for s in sems:
                e.sem_inc(s[0], s[1])

        ds = bass.ds

        x1T = sb("x1T", [P, TOKENS])
        xT = sb("xT", [P, TOKENS])
        xnT = sb("xnT", [P, TOKENS])
        ident = sb("ident", [P, P])
        ident16 = sb("ident16", [P, P], bf16)
        meanw = sb("meanw", [P, P])
        mask_a = sb("mask_a", [P, P], bf16)
        mask_b = sb("mask_b", [P, KEYS_B], bf16)
        base_q = sb("base_q", [P, CHUNKS, 2, HEAD])
        base_k = sb("base_k", [P, CHUNKS, 2, HEAD])
        tab_q = sb("tab_q", [P, CHUNKS, 2, HEAD])
        tab_k = sb("tab_k", [P, CHUNKS, 2, HEAD])
        scale_q = sb("scale_q", [P, DEPTH, HEAD])
        scale_k = sb("scale_k", [P, DEPTH, HEAD])
        NPAR = 3 + 2 * NHT
        lpar_all = sb("lpar_all", [P, DEPTH, NPAR])
        lpar = sb("lpar", [P, NPAR])
        eps = sb("eps", [P, 1])
        wqkv = sb("wqkv", [P, 3 * INNER])
        wo = sb("wo", [P, PAIRS, DIM])
        w1 = sb("w1", [P, 2 * HID])
        w2 = sb("w2", [P, NHT, DIM])
        xs = [sb(f"xs{u}", [P, SEQ]) for u in range(2)]
        xs2 = [sb(f"xs2_{u}", [P, SEQ_PER_GROUP, SEQ]) for u in range(2)]
        hid_last = [sb(f"hid_last{u}", [P, GROUP]) for u in range(2)]
        ssq = [sb(f"ssq{u}", [P, 8]) for u in range(2)]
        ssqc = [sb(f"ssqc{u}", [P, 8]) for u in range(2)]
        lnv = [sb(f"lnv{u}", [P, 8]) for u in range(2)]
        rq = [sb(f"rq{u}", [P, CHUNKS, HEADS]) for u in range(2)]
        rk = [sb(f"rk{u}", [P, 8]) for u in range(2)]
        mx = [sb(f"mx{n}", [P, 4]) for n in range(NP_BUF)]
        nbias = [sb(f"nbias{n}", [P, 4]) for n in range(NP_BUF)]
        rsum = [sb(f"rsum{n}", [P, 4]) for n in range(NP_BUF)]
        rinv = [sb(f"rinv{n}", [P, 4]) for n in range(NP_BUF)]

        ARENA = 28992
        arena = sb("arena", [P, ARENA])
        at = [0]

        def cut(cols):
            a = arena[:, at[0]:at[0] + cols]
            at[0] += cols
            assert at[0] <= ARENA, at[0]
            return a

        kT = [cut(PAIRS * 2 * SEQ).rearrange("p (a h t) -> p a h t", a=PAIRS, h=2) for _ in range(2)]
        pB = [cut(2 * SEQ).rearrange("p (h t) -> p h t", h=2) for _ in range(NP_BUF)]
        pA = [cut(2 * P).rearrange("p (h t) -> p h t", h=2) for _ in range(NP_BUF)]
        ffn_at = at[0]
        qT = [cut(PAIRS * SEQ).rearrange("p (a t) -> p a t", a=PAIRS) for _ in range(2)]
        vv = [cut(CHUNKS * INNER).rearrange("p (c n) -> p c n", c=CHUNKS) for _ in range(2)]
        oT = [xnT[:, u * INNER * 2:(u + 1) * INNER * 2].rearrange("p (a t) -> p a t", a=PAIRS) for u in range(2)]
        tq = [cut(2 * 512).rearrange("p (s h e) -> p s h e", s=2, h=8) for _ in range(2)]
        tk = [cut(2 * 512).rearrange("p (s h e) -> p s h e", s=2, h=8) for _ in range(2)]
        sq = [cut(512) for _ in range(2)]
        ks = [cut(512) for _ in range(2)]
        pT = [[cut(P + WINDOW + P) for _ in range(2)] for _ in range(2)]
        at[0] = ffn_at
        xc = [cut(GROUP) for _ in range(2)]
        sq2 = [cut(GROUP) for _ in range(2)]
        lg = [cut(GROUP) for _ in range(2)]
        rstd = [cut(GROUP) for _ in range(2)]
        aff = [cut(GROUP) for _ in range(2)]
        gl = [cut(GROUP) for _ in range(NHT)]
        hid = [[cut(GROUP) for _ in range(NHT - 1)] + [hid_last[u][:, :]] for u in range(2)]
        xtok = [cut(GROUP).rearrange("p (c f) -> p c f", f=DIM) for _ in range(2)]
        fin = [cut(GROUP) for _ in range(2)]
        ffn_end = at[0]
        at[0] = 0
        act = [cut(TOKENS) for _ in range(MT)]
        NDA, NH_BUF = 3, 3
        dA = [cut(GROUP) for _ in range(NDA)]
        xz = [cut(SEQ_PER_GROUP * (SEQ + CONV - 1)).rearrange("p (s t) -> p s t", s=SEQ_PER_GROUP) for _ in range(MT)]
        assert at[0] <= ffn_at
        at[0] = ffn_at
        cacc, zabs, zexp, zlog, zpos, delta, dx, gated = ([cut(GROUP) for _ in range(MT)] for _ in range(8))
        dbx, hst, hc = ([cut(GROUP) for _ in range(NH_BUF)] for _ in range(3))
        r1 = cut(GROUP)
        r2 = cut(GROUP)
        bc_parts = cut(GROUP // 2).bitcast(bf16)
        assert at[0] >= ffn_end
        w_in = cut(D_INNER)
        w_gate = cut(D_INNER)
        w_delta = cut(MT * D_INNER).rearrange("p (k n) -> p k n", k=MT)
        w_bc = cut(MT * P).rearrange("p (k n) -> p k n", k=MT)
        w_out = cut(MT * DIM).rearrange("p (k n) -> p k n", k=MT)
        conv_w = cut(MT * CONV).rearrange("p (m k) -> p m k", m=MT)
        mpar = cut(8 * MT).rearrange("p (m k) -> p m k", m=MT)
        a_neg = cut(MT * D_STATE).rearrange("p (m n) -> p m n", m=MT)
        sel = cut(2 * D_STATE * P // 2).bitcast(bf16).rearrange("p (n m) -> p n m", n=2 * D_STATE)
        sgate = [xT, xnT]

        bank = [ctx.enter_context(nc.psum_tensor(f"bank{i}", [P, 512], f32)) for i in range(8)]
        QKB, TRB, SAB, SBB, PTB, OB = bank[0:3], bank[3], bank[4], bank[5], bank[6], bank[7]

        const_in = sem("const_in")
        lpar_in = sem("lpar_in")
        cleared = sem("cleared")
        m_cleared = sem("m_cleared")
        x_in = [sem(f"x_in{u}", 0) for u in range(2)]
        x_turned = sem("x_turned", 2)
        x_kept = sem("x_kept", 2)
        ln_in = sem("ln_in")
        ln_mean = sem("ln_mean")
        ln_xc = sem("ln_xc", 2)
        ln_sq = sem("ln_sq")
        ln_var = sem("ln_var")
        ln_log = sem("ln_log", 2)
        ln_rstd = sem("ln_rstd")
        ln_aff = sem("ln_aff")
        ln_out = sem("ln_out", 2)
        in_done = sem("in_done")
        in_used = [sem(f"in_used{n}", 1) for n in range(2 * MT)]
        conv_step = sem("conv_step")
        conv_done = sem("conv_done", MT)
        act_done = sem("act_done", MT)
        sg_done = sem("sg_done")
        a_done = sem("a_done")
        d_done = sem("d_done")
        z_abs = sem("z_abs")
        z_exp = sem("z_exp")
        z_log = sem("z_log")
        z_pos = sem("z_pos", MT)
        delta_done = sem("delta_done")
        dx_done = sem("dx_done")
        bc_done = sem("bc_done")
        bc_step = sem("bc_step")
        bc_split = sem("bc_split", 1)
        b_ready = sem("b_ready")
        c_ready = sem("c_ready")
        dA_done = sem("dA_done")
        dbx_done = sem("dbx_done", 2 * MT)
        scan_done = sem("scan_done", NDA)
        hc_done = sem("hc_done", 2 * MT)
        y_step = sem("y_step", NH_BUF)
        y_skip = sem("y_skip", MT)
        g_done = sem("g_done")
        mo_done = sem("mo_done", 1)
        mo_used = sem("mo_used", 1)
        wqkv_in = sem("wqkv_in")
        wo_in = sem("wo_in")
        w1_in = sem("w1_in")
        w2_in = sem("w2_in")
        tabs_done = sem("tabs_done")
        xs_ready = sem("xs_ready")
        proj_done = sem("proj_done", 2 * UNITS)
        sq_ready = sem("sq_ready")
        sq_reduced = sem("sq_reduced", 2)
        ssq_ready = sem("ssq_ready")
        ln_done = sem("ln_done")
        r_done = sem("r_done")
        rope_q = sem("rope_q", 1)
        rope_k = sem("rope_k", 1)
        v_ready = sem("v_ready", 2)
        k_summed = sem("k_summed", 2)
        k_scaled = sem("k_scaled")
        tr_done = sem("tr_done", 4)
        tr_act = sem("tr_act", 1)
        tr_dve = sem("tr_dve", 1)
        sA_done = sem("sA_done")
        sB_done = sem("sB_done", 2 * PAIRS)
        mx_step = sem("mx_step")
        nb_ready = sem("nb_ready")
        expA = sem("expA", 2)
        expB = sem("expB", 2)
        rinv_ready = sem("rinv_ready")
        normed = sem("normed")
        pt_done = sem("pt_done", 2 * NP_BUF)
        pt_evac = sem("pt_evac", 1)
        pv_done = sem("pv_done", 2 * PAIRS)
        o_evac = sem("o_evac", 1)
        wo_done = sem("wo_done", 2)
        x_added = sem("x_added", 1)
        ag_done = sem("ag_done")
        gelu_done = sem("gelu_done")
        hid_done = sem("hid_done", NHT)
        y_done = sem("y_done", 2)
        x_next = sem("x_next", 2)
        f_sum = sem("f_sum")
        f_turned = sem("f_turned", 2)
        f_ready = sem("f_ready", 2)
        f_out = [sem(f"f_out{u}") for u in range(2)]

        block = ctx.enter_context(nc.Block())

        def pair_loop(e, first, last, body):
            with e.Fori(first, last) as i:
                body(i)

        def swapped(a):
            return a.rearrange("p h (s e) -> p h s e", s=2)[:, :, ::-1, :]

        B_IN, B_GATE, CONV_B, B_DELTA, D_SK, B_OUT = range(6)

        @block.sync
        def _(sp):
            small = [
                (ident[:], t["ident"]), (ident16[:], t["ident16"]), (mask_a[:], t["mask_a"]), (mask_b[:], t["mask_b"]),
                (base_q[:], t["rope_q"]), (base_k[:], t["rope_k"]), (sel, t["sel"]),
                (w_in, t["L0_attn_W_in"]), (w_gate, t["L0_attn_W_gate"]),
                (w_delta, t["L0_attn_W_delta"].rearrange("(k p) n -> p k n", p=P)),
                (w_out, t["L0_attn_W_out"].rearrange("(k p) n -> p k n", p=P)),
                (conv_w, t["L0_attn_conv_w"].rearrange("(m p) o k -> p m (o k)", p=P)),
                (a_neg, t["L0_attn_A_log"].rearrange("(m p) n -> p m n", p=P)),
                (mpar[:, 0, B_OUT:B_OUT + 1], t["L0_attn_b_out"].rearrange("(p o) -> p o", o=1)),
            ]
            for col, name in ((B_IN, "b_in"), (B_GATE, "b_gate"), (CONV_B, "conv_b"), (B_DELTA, "b_delta"), (D_SK, "D_skip")):
                small.append((mpar[:, :, col], t[f"L0_attn_{name}"].rearrange("(m p) -> p m", p=P)))
            for copy in range(4):
                w = w_bc[:, :, 32 * copy:32 * copy + 32]
                small.append((w[:, :, 0:D_STATE], t["L0_attn_W_B"].rearrange("(k p) n -> p k n", p=P)))
                small.append((w[:, :, D_STATE:2 * D_STATE], t["L0_attn_W_C"].rearrange("(k p) n -> p k n", p=P)))
            with nc.allow_non_contiguous_dma("small parameters, once"):
                for dst, src in small:
                    sp.dma_start(dst, src).then_inc(const_in[0], 16)
            x_rows = t["L0_attn_x"].rearrange("s n f -> (s n) f")

            def load_pair(i):
                for u in range(2):
                    slot(sp, x_turned, i * 2 + u)
                    sp.dma_start(xtok[u], x_rows[ds((i * 2 + u) * GROUP, GROUP), :].rearrange("(c p) f -> p c f", p=P)) \
                        .then_inc(x_in[u][0], 16)
            pair_loop(sp, 0, GROUPS // 2, load_pair)

            vectors = [(lpar_all[:, :, 0], t["L0_ffn_ln_g"]), (lpar_all[:, :, 1], t["L0_ffn_ln_b"]),
                       (lpar_all[:, :, 2], t["L0_ffn_b2"])]
            for m, (h0, hn) in enumerate(HT):
                vectors.append((lpar_all[0:hn, :, 3 + m], t["L0_ffn_b1"][:, h0:h0 + hn]))
                vectors.append((lpar_all[0:hn, :, 3 + NHT + m], t["L0_ffn_b1"][:, HID + h0:HID + h0 + hn]))
            sp.wait_ge(cleared[0], 1)
            with nc.allow_non_contiguous_dma("small parameters, once"):
                for dst, src in vectors:
                    sp.dma_start(dst, src.rearrange("l p -> p l")).then_inc(lpar_in[0], 16)
                for dst, src in ((scale_q, t["L0_ffn_q_scale"]), (scale_k, t["L0_ffn_k_scale"])):
                    sp.dma_start(dst[:], src.unsqueeze(0).to_broadcast([P, DEPTH, HEAD])).then_inc(lpar_in[0], 16)

            def load_layer_front(l):
                sp.dma_start(wqkv[:], t["L0_ffn_Wqkv"][ds(l, 1), :, :].rearrange("o p n -> p (o n)")).then_inc(wqkv_in[0], 16)
                sp.dma_start(wo[:], t["L0_ffn_Wo"][ds(l, 1), :, :].rearrange("o (a p) n -> p (o a) n", p=P)).then_inc(wo_in[0], 16)

            def load_layer_back(l):
                sp.dma_start(w1[:], t["L0_ffn_W1"][ds(l, 1), :, :].rearrange("o p n -> p (o n)")).then_inc(w1_in[0], 16)
                sp.dma_start(w2[:, 0:NHT - 1, :], t["L0_ffn_W2"][ds(l, 1), 0:(NHT - 1) * P, :].rearrange("o (a p) n -> p (o a) n", p=P)) \
                    .then_inc(w2_in[0], 16)
                h0, hn = HT[-1]
                sp.dma_start(w2[0:hn, NHT - 1:NHT, :], t["L0_ffn_W2"][ds(l, 1), h0:HID, :].rearrange("o p n -> p o n")).then_inc(w2_in[0], 16)

            load_layer_front(0)
            load_layer_back(0)
            with sp.Fori(1, DEPTH) as l:
                sp.wait_ge(wo_done[0], l * BATCH + wo_done[1])
                load_layer_front(l)
                sp.wait_ge(y_done[0], l * GROUPS + y_done[1])
                load_layer_back(l)

            out_rows = out.rearrange("s n f -> (s n) f")

            def store_pair(i):
                for u in range(2):
                    item(sp, f_ready, i * 2 + u)
                    sp.dma_start(out_rows[ds((i * 2 + u) * GROUP, GROUP), :].rearrange("(c p) f -> p c f", p=P), xtok[u]) \
                        .then_inc(f_out[u][0], 16)
            pair_loop(sp, 0, GROUPS // 2, store_pair)
            for u in range(2):
                sp.wait_ge(f_out[u][0], 16 * (GROUPS // 2))

        N_CONST = 16 * (14 + 5 + 8)
        N_LPAR = 16 * (3 + 2 * NHT + 2)

        @block.gpsimd
        def _(pool):
            give_credits(pool, [k_summed])
            nc.gpsimd.memset(meanw[:], 1.0 / P)
            nc.gpsimd.memset(lpar_all[:], 0.0)
            nc.gpsimd.memset(eps[:], LN_EPS)
            nc.gpsimd.memset(w2[:, NHT - 1, :], 0.0)
            for u in range(2):
                nc.gpsimd.memset(hid_last[u][:], 0.0)
                nc.gpsimd.memset(xs[u][:, 0:1], 0.0)
            for m in range(MT):
                nc.gpsimd.memset(xz[m][:, :, 0:CONV - 1], 0.0)
            for n in range(NDA):
                last = nc.gpsimd.memset(dA[n].rearrange("p (s t) -> p s t", t=SEQ)[:, :, 0:1], 0.0)
            last.then_inc(cleared[0], 1)

            item(pool, mo_used, GROUPS - 1)
            for u in range(2):
                nc.gpsimd.memset(kT[u], 0.0)
                item(pool, ln_out, 2 * GROUPS - 1)
                nc.gpsimd.memset(xs2[u][:, :, 0:1], 0.0)
            for n in range(NP_BUF):
                last = nc.gpsimd.memset(pB[n][:, :, 0:FIRST_B], 0.0)
            last.then_inc(cleared[0], 1)

            def k_unit(B, qn):
                ki = qn // 2
                b = ki % 2
                item(pool, rope_k, B * (NQK // 2) + ki)
                slot(pool, tr_done, B * NQK + qn)
                k2 = ks[b].rearrange("p (h e) -> p h e", h=8)
                nc.gpsimd.tensor_tensor(k2, tk[b][:, 0], tk[b][:, 1], ALU.add).then_inc(k_summed[0], 1)
                item(pool, k_summed, B * (NQK // 2) + ki)
                item(pool, r_done, B * NQK + qn)
                nc.gpsimd.tensor_tensor(k2, k2, rk[b][:, :].unsqueeze(2).to_broadcast([P, 8, HEAD]), ALU.mult).then_inc(k_scaled[0], 1)

            def normalise(s, n):
                item(pool, rinv_ready, s)
                nc.gpsimd.tensor_tensor(pA[n], pA[n], rinv[n][:, 0:2].unsqueeze(2).to_broadcast([P, 2, P]), ALU.mult) \
                    .then_inc(normed[0], 1)
                pb = pB[n][:, :, FIRST_B:SEQ]
                nc.gpsimd.tensor_tensor(pb, pb, rinv[n][:, 2:4].unsqueeze(2).to_broadcast([P, 2, KEYS_B]), ALU.mult) \
                    .then_inc(normed[0], 1)

            def units(B, uns):
                for un in uns:
                    if un in QK and ORDER[un][1] >= 2:
                        k_unit(B, QK.index(un))

            def two_sequences(l, i, first=False, last=False):
                for u in range(2):
                    for p in range(PAIRS):
                        k = u * PAIRS + p
                        s = l * (BATCH * PAIRS) + i * (2 * PAIRS) + (k - 1)
                        if not (first and k < 1):
                            normalise(s, (k - 1) % NP_BUF)
                        if not (last and u == 1):
                            units(l * BATCH + i * 2 + (u + 1), SLOT_UNITS[p])

            with pool.Fori(0, DEPTH) as l:
                units(l * BATCH, range(UNITS))
                two_sequences(l, 0, first=True)
                with pool.Fori(1, BATCH // 2 - 1) as i:
                    two_sequences(l, i)
                two_sequences(l, BATCH // 2 - 1, last=True)
                normalise(l * (BATCH * PAIRS) + (BATCH * PAIRS - 1), (BATCH * PAIRS - 1) % NP_BUF)

        @block.scalar
        def _(act_e):
            A = nc.scalar.activation
            give_credits(act_e, [ln_log, act_done, f_ready, v_ready, tr_act, expA, expB, o_evac] + in_used)
            act_e.wait_ge(const_in[0], N_CONST)
            act_e.wait_ge(cleared[0], 1)
            act_e.preload_act_table_set(EXP_LN_SET)
            A(a_neg, a_neg, ACT.Exp).then_inc(a_done[0], 1)

            def ln_pair(g0):
                for u in range(2):
                    item(act_e, ln_xc, g0 + u)
                    A(sq2[u], xc[u], ACT.Square).then_inc(ln_sq[0], 1)
                for u in range(2):
                    item(act_e, ln_var, g0 + u)
                    slot(act_e, ln_out, g0 + u)
                    A(lg[u], bank[2 + u][:], ACT.Ln, bias=eps[:, 0:1]).then_inc(ln_log[0], 1)
                    item(act_e, ln_log, g0 + u)
                    A(rstd[u], lg[u], ACT.Exp, scale=-0.5).then_inc(ln_rstd[0], 1)

            pair_loop(act_e, 0, GROUPS // 2, lambda i: ln_pair(i * 2))

            def mamba_in(g):
                for m in range(MT):
                    item(act_e, in_done, g * (2 * MT) + m)
                    slot(act_e, conv_done, g * MT + m)
                    A(xz[m][:, :, CONV - 1:], bank[m].rearrange("p (s t) -> p s t", t=SEQ), ACT.Identity,
                      bias=mpar[:, m, B_IN:B_IN + 1]).then_inc(in_used[m][0], 1)
                for m in range(MT):
                    item(act_e, in_done, g * (2 * MT) + (MT + m))
                    A(sgate[m][:, ds(g * GROUP, GROUP)], bank[MT + m][:], ACT.Silu, bias=mpar[:, m, B_GATE:B_GATE + 1]) \
                        .then_inc(in_used[MT + m][0], 1)
                for m in range(MT):
                    item(act_e, conv_done, g * MT + m)
                    A(act[m][:, ds(g * GROUP, GROUP)], cacc[m], ACT.Silu).then_inc(act_done[0], 1)

            act_e.preload_act_table(ACT.Silu)
            pair_loop(act_e, 0, GROUPS, mamba_in)
            act_e.preload_act_table_set(EXP_LN_SET)

            def scan_group(g):
                for m in range(MT):
                    item(act_e, d_done, g * MT + m)
                    A(zabs[m], bank[6 + m][:], ACT.Abs, bias=mpar[:, m, B_DELTA:B_DELTA + 1]).then_inc(z_abs[0], 1)
                for m in range(MT):
                    item(act_e, z_abs, g * MT + m)
                    A(zexp[m], zabs[m], ACT.Exp, scale=-1.0).then_inc(z_exp[0], 1)
                for m in range(MT):
                    item(act_e, z_exp, g * MT + m)
                    A(zlog[m], zexp[m], ACT.Ln, bias=1.0).then_inc(z_log[0], 1)
                for k in range(D_STATE * MT):
                    n, m = divmod(k, MT)
                    b = k % NDA
                    if k < MT:
                        item(act_e, delta_done, g * MT + m)
                    act_e.wait_ge(scan_done[0], g * (D_STATE * MT) + (k + 1 if k >= NDA else NDA))
                    d3 = delta[m].rearrange("p (s t) -> p s t", t=SEQ)
                    a3 = dA[b].rearrange("p (s t) -> p s t", t=SEQ)
                    A(a3[:, :, 1:], d3[:, :, 1:], ACT.Exp, scale=a_neg[:, m, n:n + 1]).then_inc(dA_done[0], 1)

            item(act_e, a_done, 1)
            pair_loop(act_e, 0, GROUPS, scan_group)
            pair_loop(act_e, 0, GROUPS // 2, lambda i: ln_pair(i * 2 + GROUPS))

            def norms(B, u, qn):
                c, j = ORDER[QK[qn]]
                item(act_e, ssq_ready, B * NQK + qn)
                A(lnv[qn % 2][:], ssqc[qn % 2][:], ACT.Ln, scale=LN_SCALE).then_inc(ln_done[0], 1)
                item(act_e, ln_done, B * NQK + qn)
                dst = rq[u][:, c, 8 * j:8 * j + 8] if j < 2 else rk[j % 2][:]
                A(dst, lnv[qn % 2][:], ACT.Exp, scale=-0.5).then_inc(r_done[0], 1)

            def evacuate(B, u, qn):
                c, j = ORDER[QK[qn]]
                item(act_e, tr_done, B * NQK + qn)
                act_e.wait_ge(sB_done[0], B * PAIRS + PAIRS)
                src = TRB.rearrange("p (a t) -> p a t", a=4)
                if j < 2:
                    A(qT[u][:, 4 * j:4 * j + 4, c * P:c * P + P], src, ACT.Copy).then_inc(tr_act[0], 1)
                else:
                    A(kT[u][64:P, 4 * (j - 2):4 * (j - 2) + 4, 1, c * P:c * P + P], src[64:P], ACT.Copy).then_inc(tr_act[0], 1)

            def units(B, u, uns):
                for un in uns:
                    c, j = ORDER[un]
                    item(act_e, proj_done, B * UNITS + un)
                    if un in QK:
                        qn = QK.index(un)
                        slot(act_e, sq_reduced, B * NQK + qn)
                        A(sq[qn % 2], QKB[un % QKV_BANKS][:], ACT.Square).then_inc(sq_ready[0], 1)
                    else:
                        act_e.wait_ge(pv_done[0], B * PAIRS + PAIRS)
                        A(vv[u][:, c, 512 * (j - 4):512 * (j - 4) + 512], QKB[un % QKV_BANKS][:], ACT.Copy).then_inc(v_ready[0], 1)
                    if un in R_AT:
                        norms(B, u, R_AT[un])
                    if un in TR_AT:
                        evacuate(B, u, TR_AT[un])

            def exps(s, n, u, p, blk):
                item(act_e, nb_ready, s * 2 + blk)
                if blk == 0:
                    act_e.wait_ge(pt_done[0], s * 2 + 2)
                for h in range(2):
                    if blk == 0:
                        src, dst, done = SAB[:, h * P:h * P + P], pA[n][:, h, :], expA
                    else:
                        src, dst, done = SBB[:, h * KEYS_B:(h + 1) * KEYS_B], pB[n][:, h, FIRST_B:SEQ], expB
                    A(dst, src, ACT.Exp, bias=nbias[n][:, 2 * blk + h:2 * blk + h + 1],
                      scale=rq[u][:, blk, 2 * p + h:2 * p + h + 1],
                      accum_out=rsum[n][:, 2 * blk + h:2 * blk + h + 1]).then_inc(done[0], 1)

            def out_evac(s, B, u, p):
                item(act_e, pv_done, s)
                slot(act_e, wo_done, B)
                A(oT[u][:, p, :], OB[:, 0:SEQ], ACT.Copy).then_inc(o_evac[0], 1)

            def two_sequences(l, i, first=False, last=False):
                for u in range(2):
                    for p in range(PAIRS):
                        k = u * PAIRS + p
                        s = l * (BATCH * PAIRS) + i * (2 * PAIRS) + k
                        for blk in range(2):
                            exps(s, k % NP_BUF, u, p, blk)
                        if not (last and u == 1):
                            units(l * BATCH + i * 2 + (u + 1), 1 - u, SLOT_UNITS[p])
                        if not (first and k < 3):
                            kk = (k - 3) % (2 * PAIRS)
                            out_evac(l * (BATCH * PAIRS) + i * (2 * PAIRS) + (k - 3),
                                     l * BATCH + i * 2 + (k - 3) // PAIRS, kk // PAIRS, kk % PAIRS)

            def gelu_group(g, u):
                for m, (h0, hn) in enumerate(HT):
                    item(act_e, ag_done, g * NHT + m)
                    A(gl[m][0:hn], bank[NHT + m][0:hn, :], ACT.Gelu, bias=lpar[0:hn, 3 + NHT + m:4 + NHT + m]).then_inc(gelu_done[0], 1)

            act_e.wait_ge(cleared[0], 2)
            with act_e.Fori(0, DEPTH) as l:
                act_e.preload_act_table_set(EXP_LN_SET)
                units(l * BATCH, 0, range(UNITS))
                two_sequences(l, 0, first=True)
                with act_e.Fori(1, BATCH // 2 - 1) as i:
                    two_sequences(l, i)
                two_sequences(l, BATCH // 2 - 1, last=True)
                for k in range(PAIRS - 3, PAIRS):
                    out_evac(l * (BATCH * PAIRS) + (BATCH - 1) * PAIRS + k, l * BATCH + (BATCH - 1), 1, k)
                with act_e.Fori(0, GROUPS // 2) as i:
                    ln_pair(l * GROUPS + i * 2 + 2 * GROUPS)
                act_e.preload_act_table(ACT.Gelu)
                with act_e.Fori(0, GROUPS // 2) as i:
                    for u in range(2):
                        gelu_group(l * GROUPS + i * 2 + u, u)

            def finish(i):
                for u in range(2):
                    item(act_e, f_turned, i * 2 + u)
                    act_e.wait_ge(f_out[u][0], i * 16) if not isinstance(i, int) or i else None
                    A(xtok[u], bank[u].rearrange("p (c f) -> p c f", f=DIM), ACT.Copy).then_inc(f_ready[0], 1)
            finish(0)
            pair_loop(act_e, 1, GROUPS // 2, finish)

        @block.vector
        def _(dve):
            V = nc.vector
            give_credits(dve, [x_kept, ln_xc, ln_out, z_pos, bc_split, dbx_done, scan_done, hc_done, y_skip, mo_used,
                               sq_reduced, rope_q, rope_k, tr_dve, pt_evac, x_added, hid_done, x_next, conv_done])
            dve.wait_ge(const_in[0], N_CONST)
            dve.wait_ge(cleared[0], 1)

            def keep(i):
                for u in range(2):
                    item(dve, x_turned, i * 2 + u)
                    V.tensor_copy(x1T[:, ds((i * 2 + u) * GROUP, GROUP)], bank[u][:]).then_inc(x_kept[0], 1)
            pair_loop(dve, 0, GROUPS // 2, keep)

            def ln_pair(g0, stage, finish):
                for u in range(2):
                    stage(u).then_inc(ln_in[0], 1)
                for u in range(2):
                    item(dve, ln_mean, g0 + u)
                    V.tensor_tensor(xc[u], xs2[u].rearrange("p s t -> p (s t)"), bank[u][:], ALU.subtract).then_inc(ln_xc[0], 1)
                for u in range(2):
                    item(dve, ln_rstd, g0 + u)
                    finish(u).then_inc(ln_out[0], 1)

            def plain_norm(g0, dst):
                def body(i):
                    ln_pair(i * 2 + g0,
                            lambda u: V.tensor_copy(xs2[u].rearrange("p s t -> p (s t)"), x1T[:, ds((i * 2 + u) * GROUP, GROUP)]),
                            lambda u: V.tensor_tensor(dst[:, ds((i * 2 + u) * GROUP, GROUP)], xc[u], rstd[u], ALU.mult))
                pair_loop(dve, 0, GROUPS // 2, body)

            item(dve, x_kept, GROUPS - 1)
            plain_norm(0, xnT)

            item(dve, a_done, 0)
            V.tensor_scalar(a_neg, a_neg, -1.0, None, ALU.mult).then_inc(a_done[0], 1)

            def conv_group(g):
                for m in range(MT):
                    item(dve, in_used[m], g)
                    slot(dve, act_done, g * MT + m)
                    c3 = cacc[m].rearrange("p (s t) -> p s t", t=SEQ)
                    V.tensor_scalar(c3, xz[m][:, :, CONV - 1:], conv_w[:, m, CONV - 1:CONV], mpar[:, m, CONV_B:CONV_B + 1],
                                    ALU.mult, ALU.add).then_inc(conv_step[0], 1)
                for tap in range(CONV - 2, -1, -1):
                    for m in range(MT):
                        step = (CONV - 2 - tap) * MT + m
                        item(dve, conv_step, g * ((CONV - 1) * MT) + step)
                        c3 = cacc[m].rearrange("p (s t) -> p s t", t=SEQ)
                        op = V.scalar_tensor_tensor(out=c3, in0=xz[m][:, :, tap:tap + SEQ], scalar=conv_w[:, m, tap:tap + 1],
                                                    in1=c3, op0=ALU.mult, op1=ALU.add)
                        op.then_inc(conv_step[0] if tap else conv_done[0], 1)
            pair_loop(dve, 0, GROUPS, conv_group)

            def scan_group(g):
                cols = ds(g * GROUP, GROUP)
                for m in range(MT):
                    item(dve, z_abs, g * MT + m)
                    V.tensor_scalar(zpos[m], bank[6 + m][:], mpar[:, m, B_DELTA:B_DELTA + 1], 0.0, ALU.add, ALU.max).then_inc(z_pos[0], 1)
                item(dve, bc_done, g)
                V.tensor_copy(bc_parts, bank[6][:]).then_inc(bc_step[0], 1)
                for m in range(MT):
                    item(dve, z_log, g * MT + m)
                    item(dve, z_pos, g * MT + m)
                    V.tensor_tensor(delta[m], zpos[m], zlog[m], ALU.add).then_inc(delta_done[0], 1)
                item(dve, bc_step, g * 4)
                V.tensor_tensor(r1, bank[6][:], bc_parts, ALU.subtract).then_inc(bc_step[0], 1)
                for m in range(MT):
                    item(dve, delta_done, g * MT + m)
                    V.tensor_tensor(dx[m], delta[m], act[m][:, cols], ALU.mult).then_inc(dx_done[0], 1)
                item(dve, bc_step, g * 4 + 1)
                V.tensor_copy(bc_parts[32:64], r1[32:64])
                V.tensor_copy(bc_parts[64:P], r1[64:P]).then_inc(bc_step[0], 1)
                item(dve, bc_step, g * 4 + 2)
                V.tensor_tensor(r2[64:96], r1[64:96], bc_parts[64:96], ALU.subtract).then_inc(bc_step[0], 1)
                item(dve, bc_step, g * 4 + 3)
                V.tensor_copy(bc_parts[64:96], r2[64:96]).then_inc(bc_split[0], 1)
                steps = D_STATE * MT
                for k in range(steps + 2):
                    if k < steps:
                        n, m = divmod(k, MT)
                        if k < MT:
                            item(dve, dx_done, g * MT + m)
                        item(dve, b_ready, g * D_STATE + n)
                        V.tensor_tensor(dbx[k % NH_BUF], dx[m], bank[n % 2][:], ALU.mult).then_inc(dbx_done[0], 1)
                    if 0 <= k - 1 < steps:
                        q = k - 1
                        item(dve, dA_done, g * steps + q)
                        item(dve, dbx_done, g * steps + q)
                        V.tensor_tensor_scan(hst[q % NH_BUF], dA[q % NDA], dbx[q % NH_BUF], 0.0, ALU.mult, ALU.add).then_inc(scan_done[0], 1)
                    if 0 <= k - 2:
                        q = k - 2
                        n = q // MT
                        item(dve, c_ready, g * D_STATE + n)
                        item(dve, scan_done, g * steps + q)
                        dve.wait_ge(y_step[0], g * steps + (q + 1 if q >= NH_BUF else NH_BUF))
                        V.tensor_tensor(hc[q % NH_BUF], hst[q % NH_BUF], bank[2 + n % 2][:], ALU.mult).then_inc(hc_done[0], 1)
                for m in range(MT):
                    item(dve, y_step, g * steps + (steps - MT + m))
                    V.scalar_tensor_tensor(out=zpos[m], in0=act[m][:, cols], scalar=mpar[:, m, D_SK:D_SK + 1], in1=bank[4 + m][:],
                                           op0=ALU.mult, op1=ALU.add).then_inc(y_skip[0], 1)
                slot(dve, mo_done, g)
                for m in range(MT):
                    item(dve, y_skip, g * MT + m)
                    V.tensor_tensor(gated[m], zpos[m], sgate[m][:, cols], ALU.mult).then_inc(g_done[0], 1)
                item(dve, mo_done, g)
                V.scalar_tensor_tensor(out=x1T[:, cols], in0=bank[7][:], scalar=mpar[:, 0, B_OUT:B_OUT + 1], in1=x1T[:, cols],
                                       op0=ALU.add, op1=ALU.add).then_inc(mo_used[0], 1)
            pair_loop(dve, 0, GROUPS, scan_group)

            item(dve, mo_used, GROUPS - 1)
            plain_norm(GROUPS, xT)

            def layer_tables(l):
                for c in range(CHUNKS):
                    for tab, base, sc in ((tab_q, base_q, scale_q), (tab_k, base_k, scale_k)):
                        V.tensor_tensor(tab[:, c], base[:, c], sc[:, ds(l, 1), :].to_broadcast([P, 2, HEAD]), ALU.mult) \
                            .then_inc(tabs_done[0], 1)
                V.tensor_copy(lpar[:], lpar_all[:, ds(l, 1), :].rearrange("p o n -> p (o n)")).then_inc(tabs_done[0], 1)

            def stage_x(B, u, col):
                dve.wait_ge(proj_done[0], B * UNITS + UNITS)
                V.tensor_copy(xs[u][0:64, :], xT[0:64, ds(col, SEQ)])
                V.tensor_copy(xs[u][64:P, 1:SEQ], xT[64:P, ds(col, SEQ - 1)]).then_inc(xs_ready[0], 1)

            def evacuate(B, u, qn):
                c, j = ORDER[QK[qn]]
                if j < 2:
                    return
                item(dve, tr_done, B * NQK + qn)
                dve.wait_ge(sB_done[0], B * PAIRS + PAIRS)
                V.tensor_copy(kT[u][0:64, 4 * (j - 2):4 * (j - 2) + 4, 0, c * P:c * P + P],
                              TRB.rearrange("p (a t) -> p a t", a=4)[0:64]).then_inc(tr_dve[0], 1)

            def units(B, u, uns):
                for un in uns:
                    c, j = ORDER[un]
                    if un in QK:
                        qn = QK.index(un)
                        item(dve, sq_ready, B * NQK + qn)
                        V.tensor_reduce(ssq[qn % 2][:], sq[qn % 2].rearrange("p (h e) -> p h e", h=8), op=ALU.add, axis=AX.X) \
                            .then_inc(sq_reduced[0], 1)
                        tab, dst, done = (tab_q, tq[j % 2], rope_q) if j < 2 else (tab_k, tk[j % 2], rope_k)
                        if j < 2:
                            slot(dve, tr_done, B * NQK + qn)
                        else:
                            slot(dve, k_summed, B * (NQK // 2) + qn // 2)
                        src = QKB[un % QKV_BANKS].rearrange("p (h e) -> p h e", h=8)
                        V.tensor_tensor(dst[:, 0], src, tab[:, c, 0:1, :].to_broadcast([P, 8, HEAD]), ALU.mult)
                        V.tensor_tensor(swapped(dst[:, 1]), src.rearrange("p h (s e) -> p h s e", s=2),
                                        tab[:, c, 1:2, :].rearrange("p o (s e) -> p o s e", s=2).to_broadcast([P, 8, 2, HALF]),
                                        ALU.mult).then_inc(done[0], 1)
                        item(dve, sq_reduced, B * NQK + qn)
                        V.tensor_scalar(ssqc[qn % 2][:], ssq[qn % 2][:], NORM_FLOOR, None, ALU.max).then_inc(ssq_ready[0], 1)
                    if un in TR_AT:
                        evacuate(B, u, TR_AT[un])

            def maxima(s, n, u, p, blk):
                bank_, keys, done = (SAB, P, sA_done) if blk == 0 else (SBB, KEYS_B, sB_done)
                item(dve, done, s)
                V.reduce_max(mx[n][:, 2 * blk:2 * blk + 2], bank_[:, 0:2 * keys].rearrange("p (h t) -> p h t", h=2), AX.X).then_inc(mx_step[0], 1)

            def biases(s, n, u, p, blk):
                item(dve, mx_step, s * 2 + blk)
                V.scalar_tensor_tensor(out=nbias[n][:, 2 * blk:2 * blk + 2], in0=mx[n][:, 2 * blk:2 * blk + 2], scalar=-1.0,
                                       in1=rq[u][:, blk, 2 * p:2 * p + 2], op0=ALU.mult, op1=ALU.mult).then_inc(nb_ready[0], 1)

            def probs_evac(s, b, h):
                item(dve, pt_done, s * 2 + h)
                dve.wait_ge(pv_done[0], s + (2 * PAIRS - 1))
                V.tensor_copy(pT[b][h], PTB[:, 0:P + WINDOW + P]).then_inc(pt_evac[0], 1)

            def add_x(B, col):
                item(dve, wo_done, B)
                V.tensor_tensor(xT[:, ds(col, SEQ)], OB[:, 0:SEQ], xT[:, ds(col, SEQ)], ALU.add).then_inc(x_added[0], 1)

            def two_sequences(l, i, first=False, last=False):
                for u in range(2):
                    B = l * BATCH + i * 2 + u
                    if not (last and u == 1):
                        stage_x(B + 1, 1 - u, i * (2 * SEQ) + (u + 1) * SEQ)
                    for p in range(PAIRS):
                        k = u * PAIRS + p
                        s = l * (BATCH * PAIRS) + i * (2 * PAIRS) + k
                        n = k % NP_BUF
                        if k == 0:
                            item(dve, r_done, (l * BATCH + i * 2) * NQK + (NQK - 1))
                        if k == PAIRS:
                            item(dve, r_done, (l * BATCH + i * 2) * NQK + (2 * NQK - 1))
                        if not (first and k < 2):
                            probs_evac(s + -2, k % 2, 0)
                        maxima(s, n, u, p, 0)
                        maxima(s, n, u, p, 1)
                        biases(s, n, u, p, 0)
                        biases(s, n, u, p, 1)
                        if not (first and k < 2):
                            probs_evac(s + -2, k % 2, 1)
                        if not (last and u == 1):
                            units(B + 1, 1 - u, SLOT_UNITS[p])
                        if p == 3 and not (first and u == 0):
                            add_x(B + -1, i * (2 * SEQ) + (u - 1) * SEQ)
                        item(dve, expA, s * 2 + 1)
                        item(dve, expB, s * 2 + 1)
                        V.reciprocal(rinv[n][:], rsum[n][:]).then_inc(rinv_ready[0], 1)

            dve.wait_ge(lpar_in[0], N_LPAR)
            dve.wait_ge(cleared[0], 2)
            item(dve, ln_out, 2 * GROUPS - 1)
            with dve.Fori(0, DEPTH) as l:
                layer_tables(l)
                item(dve, tabs_done, l * (2 * CHUNKS + 1) + 2 * CHUNKS)
                stage_x(l * BATCH, 0, 0)
                units(l * BATCH, 0, range(UNITS))
                two_sequences(l, 0, first=True)
                with dve.Fori(1, BATCH // 2 - 1) as i:
                    two_sequences(l, i)
                two_sequences(l, BATCH // 2 - 1, last=True)
                for s in range(BATCH * PAIRS - 2, BATCH * PAIRS):
                    for h in range(2):
                        probs_evac(l * (BATCH * PAIRS) + s, s % 2, h)
                add_x(l * BATCH + (BATCH - 1), (BATCH - 1) * SEQ)

                with dve.Fori(0, GROUPS // 2) as i:
                    item(dve, x_added, l * BATCH + (BATCH - 1))
                    def stage(u):
                        x3 = xT[:, ds((i * 2 + u) * GROUP, GROUP)].rearrange("p (s t) -> p s t", t=SEQ)
                        V.tensor_copy(xs2[u][0:64], x3[0:64])
                        return V.tensor_copy(xs2[u][64:P, :, 1:SEQ], x3[64:P, :, 0:SEQ - 1])

                    def finish(u):
                        V.scalar_tensor_tensor(out=aff[u], in0=xc[u], scalar=lpar[:, 0:1], in1=rstd[u], op0=ALU.mult, op1=ALU.mult) \
                            .then_inc(ln_aff[0], 1)
                        item(dve, ln_aff, l * GROUPS + i * 2 + u)
                        return V.tensor_scalar(xnT[:, ds((i * 2 + u) * GROUP, GROUP)], aff[u], lpar[:, 1:2], None, ALU.add)
                    ln_pair(l * GROUPS + i * 2 + 2 * GROUPS, stage, finish)

                with dve.Fori(0, GROUPS // 2) as i:
                    for u in range(2):
                        g = l * GROUPS + i * 2 + u
                        slot(dve, y_done, g)
                        for m, (h0, hn) in enumerate(HT):
                            item(dve, gelu_done, g * NHT + m)
                            V.scalar_tensor_tensor(out=hid[u][m][0:hn], in0=bank[m][0:hn, :], scalar=lpar[0:hn, 3 + m:4 + m],
                                                   in1=gl[m][0:hn], op0=ALU.add, op1=ALU.mult).then_inc(hid_done[0], 1)
                        item(dve, y_done, g)
                        cols = ds((i * 2 + u) * GROUP, GROUP)
                        V.scalar_tensor_tensor(out=xT[:, cols], in0=bank[2 * NHT + u][:], scalar=lpar[:, 2:3], in1=xT[:, cols],
                                               op0=ALU.add, op1=ALU.add).then_inc(x_next[0], 1)
                item(dve, x_next, l * GROUPS + (GROUPS - 1))

            def finish(i):
                for u in range(2):
                    cols = ds((i * 2 + u) * GROUP, GROUP)
                    slot(dve, f_turned, i * 2 + u)
                    V.tensor_tensor(fin[u], x1T[:, cols], xT[:, cols], ALU.add).then_inc(f_sum[0], 1)
            pair_loop(dve, 0, GROUPS // 2, finish)

        @block.tensor
        def _(pe):
            give_credits(pe, [x_turned, y_step, mo_done, proj_done, tr_done, sB_done, pt_done, pv_done, wo_done, y_done, f_turned])
            MM = nc.tensor.matmul

            def turn(out_, in_, **kw):
                k = in_.shape[0]
                return MM(out_, lhsT=in_, rhs=ident[0:k, 0:k], is_transpose=True, **kw)

            pe.wait_ge(const_in[0], N_CONST)
            pe.wait_ge(cleared[0], 1)

            def load_pair(i):
                for u in range(2):
                    pe.wait_ge(x_in[u][0], i * 16 + 16)
                    slot(pe, x_kept, i * 2 + u)
                    for c in range(GROUP // P):
                        last = turn(bank[u][:, c * P:(c + 1) * P], xtok[u][:, c, :], start=True, stop=True)
                    last.then_inc(x_turned[0], 1)
            pair_loop(pe, 0, GROUPS // 2, load_pair)

            def ln_pair(g0):
                for u in range(2):
                    item(pe, ln_in, g0 + u)
                    slot(pe, ln_xc, g0 + u)
                    MM(bank[u][:], lhsT=meanw[:], rhs=xs2[u].rearrange("p s t -> p (s t)"), start=True, stop=True).then_inc(ln_mean[0], 1)
                for u in range(2):
                    item(pe, ln_sq, g0 + u)
                    slot(pe, ln_log, g0 + u)
                    MM(bank[2 + u][:], lhsT=meanw[:], rhs=sq2[u], start=True, stop=True).then_inc(ln_var[0], 1)

            item(pe, x_kept, GROUPS - 1)
            pair_loop(pe, 0, GROUPS // 2, lambda i: ln_pair(i * 2))

            def mamba_in(g):
                rhs = xnT[:, ds(g * GROUP, GROUP)]
                for n in range(2 * MT):
                    slot(pe, in_used[n], g)
                    w = (w_in, w_gate)[n // MT]
                    m = n % MT
                    MM(bank[n][:], lhsT=w[:, m * P:(m + 1) * P], rhs=rhs, start=True, stop=True).then_inc(in_done[0], 1)

            item(pe, ln_out, GROUPS - 1)
            pair_loop(pe, 0, GROUPS, mamba_in)

            def scan_group(g):
                cols = ds(g * GROUP, GROUP)
                for m in range(MT):
                    if m == 0:
                        slot(pe, bc_split, g)
                    else:
                        slot(pe, mo_used, g)
                    for k in range(MT):
                        last = MM(bank[6 + m][:], lhsT=w_delta[:, k, m * P:(m + 1) * P], rhs=act[k][:, cols], start=k == 0, stop=k == MT - 1)
                    last.then_inc(d_done[0], 1)
                item(pe, z_pos, g * MT)
                for k in range(MT):
                    last = MM(bank[6][:], lhsT=w_bc[:, k, :], rhs=act[k][:, cols], start=k == 0, stop=k == MT - 1)
                last.then_inc(bc_done[0], 1)
                item(pe, bc_split, g)
                steps = D_STATE * MT

                def spread(n):
                    pe.wait_ge(dbx_done[0], g * steps + (n + 1) * MT)
                    MM(bank[n % 2][:], lhsT=sel[:, n, :], rhs=bc_parts, start=True, stop=True).then_inc(b_ready[0], 1)
                    pe.wait_ge(hc_done[0], g * steps + (n + 1) * MT)
                    MM(bank[2 + n % 2][:], lhsT=sel[:, D_STATE + n, :], rhs=bc_parts, start=True, stop=True).then_inc(c_ready[0], 1)

                spread(0)
                for m in range(MT):
                    slot(pe, y_skip, g * MT + m)
                for n in range(D_STATE):
                    if n + 1 < D_STATE:
                        spread(n + 1)
                    for m in range(MT):
                        k = n * MT + m
                        item(pe, hc_done, g * steps + k)
                        MM(bank[4 + m][:], lhsT=ident[:], rhs=hc[k % NH_BUF], start=n == 0, stop=n == D_STATE - 1).then_inc(y_step[0], 1)
                for m in range(MT):
                    item(pe, g_done, g * MT + m)
                    last = MM(bank[7][:], lhsT=w_out[:, m, :], rhs=gated[m], start=m == 0, stop=m == MT - 1)
                last.then_inc(mo_done[0], 1)

            item(pe, act_done, GROUPS * MT - 1)
            for n in range(2 * MT):
                item(pe, in_used[n], GROUPS - 1)
            pair_loop(pe, 0, GROUPS, scan_group)
            item(pe, mo_used, GROUPS - 1)
            pair_loop(pe, 0, GROUPS // 2, lambda i: ln_pair(i * 2 + GROUPS))
            item(pe, ln_out, 2 * GROUPS - 1)

            def bank_free(B, un):
                prev = un - QKV_BANKS
                back = 0
                if prev < 0:
                    prev, back = prev + UNITS, 1
                if prev in QK:
                    qn = QK.index(prev)
                    s = rope_q if ORDER[prev][1] < 2 else rope_k
                    pe.wait_ge(s[0], B * (NQK // 2) + (qn // 2 - back * (NQK // 2) + 1 + s[1]))
                else:
                    pe.wait_ge(v_ready[0], B * len(VU) + (VU.index(prev) - back * len(VU) + 1 + v_ready[1]))

            def transposes(B, qn):
                c, j = ORDER[QK[qn]]
                slot(pe, tr_act, B * NQK + qn)
                if j < 2:
                    slot(pe, tr_dve, B * (NQK // 2) + qn // 2)
                    item(pe, rope_q, B * (NQK // 2) + qn // 2)
                    for a in range(4):
                        turn(TRB[:, a * P:(a + 1) * P], tq[j][:, 0, 2 * a:2 * a + 2, :].rearrange("p h e -> p (h e)"), start=True, stop=False)
                        last = turn(TRB[:, a * P:(a + 1) * P], tq[j][:, 1, 2 * a:2 * a + 2, :].rearrange("p h e -> p (h e)"), start=False, stop=True)
                else:
                    item(pe, k_scaled, B * (NQK // 2) + qn // 2)
                    for a in range(4):
                        last = turn(TRB[:, a * P:(a + 1) * P], ks[j % 2][:, a * P:(a + 1) * P], start=True, stop=True)
                last.then_inc(tr_done[0], 1)

            def units(B, u, uns):
                for un in uns:
                    c, j = ORDER[un]
                    if un == 0:
                        item(pe, xs_ready, B)
                    bank_free(B, un)
                    MM(QKB[un % QKV_BANKS][:], lhsT=xs[u][:, c * P:(c + 1) * P], rhs=wqkv[:, j * 512:(j + 1) * 512],
                       start=True, stop=True).then_inc(proj_done[0], 1)
                    if un in TR_AT:
                        transposes(B, TR_AT[un])

            def scores(s, B, u, p):
                c, j = 1, p // 4
                if p % 4 == 0:
                    pe.wait_ge(tr_act[0], B * NQK + (NQK - 2 + 2 * j + tr_act[1]))
                    pe.wait_ge(tr_dve[0], B * (NQK // 2) + (NQK // 2 - 1 + j + tr_dve[1]))
                for bank_, first, keys, mask, free, done, q0 in (
                        (SAB, 0, P, mask_a, expA, sA_done, 0), (SBB, FIRST_B, KEYS_B, mask_b, expB, sB_done, P)):
                    pe.wait_ge(free[0], s * 2 + 2)
                    dst = bank_[:, 0:2 * keys]
                    MM(dst, lhsT=ident16[:], rhs=mask[:, :].unsqueeze(1).to_broadcast([P, 2, keys]), start=True, stop=False)
                    MM(dst, lhsT=qT[u][:, p, q0:q0 + P], rhs=kT[u][:, p, :, first:first + keys], start=False, stop=True) \
                        .then_inc(done[0], 1)

            def probs_turn(s, n, h):
                slot(pe, pt_evac, s * 2 + h)
                if h == 0:
                    item(pe, normed, s * 2 + 1)
                turn(PTB[:, 0:P], pA[n][:, h, :], start=True, stop=True)
                turn(PTB[:, P:P + WINDOW], pB[n][0:WINDOW, h, 0:P], start=True, stop=True)
                turn(PTB[:, P + WINDOW:2 * P + WINDOW], pB[n][:, h, P:SEQ], start=True, stop=True).then_inc(pt_done[0], 1)

            def values(s, B, u, p, b):
                item(pe, pt_evac, s * 2 + 1)
                slot(pe, o_evac, s)
                if p == 0:
                    slot(pe, x_added, B)
                    item(pe, v_ready, B * len(VU) + (len(VU) - 1))
                for c, q0, t0, n in ((0, 0, 0, P + WINDOW), (1, P, P + WINDOW, P)):
                    for h in range(2):
                        col = (2 * p + h) * HEAD
                        last = MM(OB[64 * h:64 * h + 64, q0:q0 + n], lhsT=vv[u][:, c, col:col + HEAD], rhs=pT[b][h][:, t0:t0 + n],
                                  start=c == 0, stop=c == 1, skip_group_check=True)
                last.then_inc(pv_done[0], 1)

            def project(B, u):
                item(pe, o_evac, B * PAIRS + (PAIRS - 1))
                for a in range(PAIRS):
                    last = MM(OB[:, 0:SEQ], lhsT=wo[:, a, :], rhs=oT[u][:, a, :], start=a == 0, stop=a == PAIRS - 1)
                last.then_inc(wo_done[0], 1)

            def two_sequences(l, i, first=False, last=False):
                for u in range(2):
                    B = l * BATCH + i * 2 + u
                    for p in range(PAIRS):
                        k = u * PAIRS + p
                        s = l * (BATCH * PAIRS) + i * (2 * PAIRS) + k
                        if not (first and k < 2):
                            probs_turn(s + -2, (k - 2) % NP_BUF, 0)
                        scores(s, B, u, p)
                        if not (first and k < 2):
                            probs_turn(s + -2, (k - 2) % NP_BUF, 1)
                        if not (last and u == 1):
                            units(B + 1, 1 - u, SLOT_UNITS[p])
                        if p == 3 and not (first and u == 0):
                            project(B + -1, 1 - u)
                        if not (first and k < 3):
                            kk = (k - 3) % (2 * PAIRS)
                            values(s + -3, l * BATCH + i * 2 + (k - 3) // PAIRS, kk // PAIRS, kk % PAIRS, (k - 3) % 2)

            with pe.Fori(0, DEPTH) as l:
                pe.wait_ge(wqkv_in[0], l * 16 + 16)
                units(l * BATCH, 0, range(UNITS))
                pe.wait_ge(wo_in[0], l * 16 + 16)
                two_sequences(l, 0, first=True)
                with pe.Fori(1, BATCH // 2 - 1) as i:
                    two_sequences(l, i)
                two_sequences(l, BATCH // 2 - 1, last=True)
                LAST = BATCH * PAIRS
                for s in range(LAST, LAST + 3):
                    if s - 2 < LAST:
                        probs_turn(l * LAST + (s - 2), (s - 2) % NP_BUF, 0)
                        probs_turn(l * LAST + (s - 2), (s - 2) % NP_BUF, 1)
                    values(l * LAST + (s - 3), l * BATCH + (BATCH - 1), 1, (s - 3) % PAIRS, (s - 3) % 2)
                project(l * BATCH + (BATCH - 1), 1)

                with pe.Fori(0, GROUPS // 2) as i:
                    ln_pair(l * GROUPS + i * 2 + 2 * GROUPS)

                with pe.Fori(0, GROUPS // 2) as i:
                    pe.wait_ge(w1_in[0], l * 16 + 16)
                    pe.wait_ge(w2_in[0], l * 32 + 32)
                    item(pe, ln_out, l * GROUPS + (3 * GROUPS - 1))

                    def up(u, m):
                        g = l * GROUPS + i * 2 + u
                        h0, hn = HT[m]
                        rhs = xnT[:, ds((i * 2 + u) * GROUP, GROUP)]
                        slot(pe, hid_done, g * NHT + m)
                        MM(bank[m][0:hn, :], lhsT=w1[:, h0:h0 + hn], rhs=rhs, start=True, stop=True)
                        MM(bank[NHT + m][0:hn, :], lhsT=w1[:, HID + h0:HID + h0 + hn], rhs=rhs, start=True, stop=True) \
                            .then_inc(ag_done[0], 1)

                    def down(u):
                        g = l * GROUPS + i * 2 + u
                        slot(pe, x_next, g)
                        for m in range(NHT):
                            item(pe, hid_done, g * NHT + m)
                            last = MM(bank[2 * NHT + u][:], lhsT=w2[:, m, :], rhs=hid[u][m], start=m == 0, stop=m == NHT - 1)
                        last.then_inc(y_done[0], 1)

                    for m in range(NHT):
                        up(0, m)
                    up(1, 0)
                    down(0)
                    for m in range(1, NHT):
                        up(1, m)
                    down(1)

            def finish(i):
                for u in range(2):
                    item(pe, f_sum, i * 2 + u)
                    slot(pe, f_ready, i * 2 + u)
                    for c in range(GROUP // P):
                        last = turn(bank[u][:, c * P:(c + 1) * P], fin[u][:, c * P:(c + 1) * P], start=True, stop=True)
                    last.then_inc(f_turned[0], 1)
            pair_loop(pe, 0, GROUPS // 2, finish)


_NAMES = ['L0_attn_x', 'L0_attn_W_in', 'L0_attn_b_in', 'L0_attn_W_gate', 'L0_attn_b_gate', 'L0_attn_conv_w',
          'L0_attn_conv_b', 'L0_attn_A_log', 'L0_attn_D_skip', 'L0_attn_W_delta', 'L0_attn_b_delta', 'L0_attn_W_B',
          'L0_attn_W_C', 'L0_attn_W_out', 'L0_attn_b_out', 'L0_ffn_Wqkv', 'L0_ffn_q_scale', 'L0_ffn_k_scale',
          'L0_ffn_Wo', 'L0_ffn_ln_g', 'L0_ffn_ln_b', 'L0_ffn_W1', 'L0_ffn_b1', 'L0_ffn_W2', 'L0_ffn_b2']


def constants():
    import numpy as np
    bf = mybir.dt.np(mybir.dt.bfloat16)
    f = np.float32
    out = {"ident": np.eye(P, dtype=f), "ident16": np.eye(P).astype(bf)}
    i, k = np.arange(P)[:, None], np.arange(P)[None, :]
    out["mask_a"] = np.where((k <= i) & (k >= i - WINDOW), 0.0, MASKED).astype(bf)
    i, k = i + P, np.arange(FIRST_B, SEQ)[None, :]
    out["mask_b"] = np.where((k <= i) & (k >= i - WINDOW), 0.0, MASKED).astype(bf)
    sel = np.zeros((P, 2 * D_STATE, P))
    for n in range(2 * D_STATE):
        sel[[n, 32 + n, 64 + n], n, :] = 1.0
    out["sel"] = sel.astype(bf)
    half = np.arange(0, HEAD, 2, dtype=f)
    inv_freq = (f(1.0) / np.power(f(10000.0), half / f(HEAD))).astype(f)
    pos = np.arange(SEQ, dtype=f)
    freqs = (pos[:, None] * inv_freq[None, :]).astype(f)
    freqs = np.concatenate([freqs, freqs], -1).astype(np.float64)
    base = ((half + f(0.4 * HEAD)) / f(1.4 * HEAD)).astype(f)
    power = ((pos - SEQ // 2) / f(WINDOW // 2)).astype(f)
    scale = np.power(base[None, :].astype(np.float64), power[:, None].astype(np.float64))
    scale = np.concatenate([scale, scale], -1)
    sign = np.where(np.arange(HEAD) < HALF, 1.0, -1.0)[None, :]
    for name, sc in (("rope_q", scale * 8.0), ("rope_k", 1.0 / scale)):
        tab = np.stack([np.cos(freqs) * sc, np.sin(freqs) * sc * sign], 1) * 2.0 ** 16
        out[name] = np.ascontiguousarray(tab.reshape(CHUNKS, P, 2, HEAD).transpose(1, 0, 2, 3)).astype(f)
    return out


def kernel(**inputs):
    import numpy as np
    import concourse.bacc as bacc
    from concourse.bass_utils import run_bass_kernel_spmd

    nc = bacc.Bacc("TRN2", target_bir_lowering=False, num_devices=1)
    arrays, aps = {}, {}
    given = {n: np.ascontiguousarray(inputs[n]) for n in _NAMES}
    given.update(constants())
    for name, a in given.items():
        arrays["in_" + name] = a
        aps[name] = nc.dram_tensor("in_" + name, a.shape, mybir.dt.from_np(a.dtype), kind="ExternalInput").ap()
    out = nc.dram_tensor("out", (BATCH, SEQ, DIM), mybir.dt.float32, kind="ExternalOutput").ap()
    build(nc, aps, out)
    r = run_bass_kernel_spmd(nc, [arrays], core_ids=[0])
    return r.results[0]["out"]
```

```python
import concourse.bass as bass
from concourse import mybir
from contextlib import ExitStack

BATCH, SEQ, DIM = 16, 256, 128
TOKENS = BATCH * SEQ
P = 128
GROUP = 512
GROUPS = TOKENS // GROUP
SEQ_PER_GROUP = GROUP // SEQ
CHUNKS = SEQ // P
D_INNER, D_STATE, CONV = 256, 16, 4
MT = D_INNER // P
DEPTH, HEADS, HEAD, WINDOW = 6, 16, 64, 32
INNER = HEADS * HEAD
HALF = HEAD // 2
PAIRS = HEADS // 2
HID = int(DIM * 4 * 2 / 3)
HT = [(m * P, min(P, HID - m * P)) for m in range((HID + P - 1) // P)]
NHT = len(HT)
KEYS_B = P + WINDOW
FIRST_B = P - WINDOW
NP_BUF = 4

SLOTS = 2 * PAIRS
QK_UNITS = [(0, 0), (0, 2), (1, 0), (1, 2), (0, 1), (0, 3), (1, 1), (1, 3)]
NQK = len(QK_UNITS)
V_UNITS = [(0, 4), (1, 4), (0, 5), (1, 5)]
NV = len(V_UNITS)
V_FIRST = 4
NWO = PAIRS // 2
WO_FIRST = 5
LAG_NORMALISE, LAG_TURN, LAG_VALUES, LAG_OUT = 1, 2, 3, 4
LAG_ROPE, LAG_NORM, LAG_UNIT_TURN, LAG_UNIT_OUT = 1, 2, 3, 4
DRAIN = WO_FIRST + 2 * (NWO - 1) + 1 - PAIRS + 1


def pair_at(l, i, k, lag, first, last):
    t = k - lag
    if (first and t < 0) or (last and t >= SLOTS):
        return None
    return l * (BATCH * PAIRS) + i * SLOTS + t, l * BATCH + i * 2 + t // PAIRS, t // PAIRS % 2, t % PAIRS, t


def unit_at(l, i, k, lag, first, last):
    t = k - lag
    if (first and t < -PAIRS) or (last and t >= PAIRS):
        return None
    return l * BATCH + i * 2 + (t // PAIRS + 1), (t // PAIRS + 1) % 2, t % PAIRS


def v_at(l, i, k, lag, first, last):
    t = k - V_FIRST - lag
    if t % 2 or (first and t < -PAIRS) or (last and t >= PAIRS):
        return None
    return l * BATCH + i * 2 + (t // PAIRS + 1), (t // PAIRS + 1) % 2, t % PAIRS // 2


def wo_at(l, i, k, lag, first, last):
    t = k - WO_FIRST - lag
    if t % 2 or (first and t < 0) or (last and t >= SLOTS):
        return None
    return l * BATCH + i * 2 + t // PAIRS, i * 2 + t // PAIRS, t // PAIRS % 2, t % PAIRS // 2, not (last and t >= PAIRS)


def attention_slots(e, l, body):
    for k in range(-PAIRS, SLOTS):
        body(l, 0, k, True, False)
    with e.Fori(1, BATCH // 2 - 1) as i:
        for k in range(SLOTS):
            body(l, i, k, False, False)
    for k in range(SLOTS + DRAIN):
        body(l, BATCH // 2 - 1, k, False, True)


LN_SCALE = float(2 ** 32)
NORM_FLOOR = 1e-24
LN_EPS = 1e-5
MASKED = -3.0e38
EXP_LN_SET = "natural_log_exp_and_others"


def build(nc, t, out):
    f32, bf16 = mybir.dt.float32, mybir.dt.bfloat16
    ALU, ACT, AX = mybir.AluOpType, mybir.ActivationFunctionType, mybir.AxisListType
    ctx = ExitStack()
    with ctx:
        def sb(name, shape, dt=f32):
            return ctx.enter_context(nc.sbuf_tensor(name, shape, dt))

        credit = {}

        def sem(name, credits=0):
            s = ctx.enter_context(nc.semaphore(name))
            credit[name] = credits
            return (s, credits)

        def item(e, s, n):
            e.wait_ge(s[0], n + (1 + s[1]))

        def slot(e, s, n):
            e.wait_ge(s[0], n + 1)

        def give_credits(e, sems):
            for s in sems:
                e.sem_inc(s[0], s[1])

        ds = bass.ds

        x1T = sb("x1T", [P, TOKENS])
        xT = sb("xT", [P, TOKENS])
        xnT = sb("xnT", [P, TOKENS])
        ident = sb("ident", [P, P])
        ident16 = sb("ident16", [P, P], bf16)
        meanw = sb("meanw", [P, P])
        mask_a = sb("mask_a", [P, P], bf16)
        mask_b = sb("mask_b", [P, KEYS_B], bf16)
        base_q = sb("base_q", [P, CHUNKS, 2, HEAD])
        base_k = sb("base_k", [P, CHUNKS, 2, HEAD])
        tab_q = sb("tab_q", [P, CHUNKS, 2, HEAD])
        tab_k = sb("tab_k", [P, CHUNKS, 2, HEAD])
        scale_q = sb("scale_q", [P, DEPTH, HEAD])
        scale_k = sb("scale_k", [P, DEPTH, HEAD])
        NPAR = 3 + 2 * NHT
        lpar_all = sb("lpar_all", [P, DEPTH, NPAR])
        lpar = sb("lpar", [P, NPAR])
        eps = sb("eps", [P, 1])
        wqkv = sb("wqkv", [P, 3 * INNER])
        wo = sb("wo", [P, PAIRS, DIM])
        w1 = sb("w1", [P, 2 * HID])
        w2 = sb("w2", [P, NHT, DIM])
        xs = [sb(f"xs{u}", [P, SEQ]) for u in range(2)]
        xs2 = [sb(f"xs2_{u}", [P, SEQ_PER_GROUP, SEQ]) for u in range(2)]
        hid_last = [sb(f"hid_last{u}", [P, GROUP]) for u in range(2)]
        ssq = [sb(f"ssq{u}", [P, 8]) for u in range(2)]
        ssqc = [sb(f"ssqc{u}", [P, 8]) for u in range(2)]
        lnv = [sb(f"lnv{u}", [P, 8]) for u in range(2)]
        rq = [sb(f"rq{u}", [P, CHUNKS, HEADS]) for u in range(2)]
        rk = [sb(f"rk{u}", [P, 8]) for u in range(2)]
        mx = [sb(f"mx{n}", [P, 4]) for n in range(NP_BUF)]
        nbias = [sb(f"nbias{n}", [P, 4]) for n in range(NP_BUF)]
        rsum = [sb(f"rsum{n}", [P, 4]) for n in range(NP_BUF)]
        rinv = [sb(f"rinv{n}", [P, 4]) for n in range(NP_BUF)]

        ARENA = 28992
        arena = sb("arena", [P, ARENA])
        at = [0]

        def cut(cols):
            a = arena[:, at[0]:at[0] + cols]
            at[0] += cols
            assert at[0] <= ARENA, at[0]
            return a

        kT = [cut(PAIRS * 2 * SEQ).rearrange("p (a h t) -> p a h t", a=PAIRS, h=2) for _ in range(2)]
        pB = [cut(2 * SEQ).rearrange("p (h t) -> p h t", h=2) for _ in range(NP_BUF)]
        pA = [cut(2 * P).rearrange("p (h t) -> p h t", h=2) for _ in range(NP_BUF)]
        ffn_at = at[0]
        qT = [cut(PAIRS * SEQ).rearrange("p (a t) -> p a t", a=PAIRS) for _ in range(2)]
        vv = [cut(CHUNKS * INNER).rearrange("p (c n) -> p c n", c=CHUNKS) for _ in range(2)]
        oT = [xnT[:, u * INNER * 2:(u + 1) * INNER * 2].rearrange("p (a t) -> p a t", a=PAIRS) for u in range(2)]
        tq = [cut(2 * 512).rearrange("p (s h e) -> p s h e", s=2, h=8) for _ in range(2)]
        tk = [cut(2 * 512).rearrange("p (s h e) -> p s h e", s=2, h=8) for _ in range(2)]
        sq = [cut(512) for _ in range(2)]
        ks = [cut(512) for _ in range(2)]
        pT = [[cut(P + WINDOW + P) for _ in range(2)] for _ in range(2)]
        at[0] = ffn_at
        xc = [cut(GROUP) for _ in range(2)]
        sq2 = [cut(GROUP) for _ in range(2)]
        lg = [cut(GROUP) for _ in range(2)]
        rstd = [cut(GROUP) for _ in range(2)]
        aff = [cut(GROUP) for _ in range(2)]
        gl = [cut(GROUP) for _ in range(NHT)]
        hid = [[cut(GROUP) for _ in range(NHT - 1)] + [hid_last[u][:, :]] for u in range(2)]
        xtok = [cut(GROUP).rearrange("p (c f) -> p c f", f=DIM) for _ in range(2)]
        fin = [cut(GROUP) for _ in range(2)]
        ffn_end = at[0]
        at[0] = 0
        act = [cut(TOKENS) for _ in range(MT)]
        NDA, NH_BUF, NHC = 3, 3, 4
        dA = [cut(GROUP) for _ in range(NDA)]
        xz = [cut(SEQ_PER_GROUP * (SEQ + CONV - 1)).rearrange("p (s t) -> p s t", s=SEQ_PER_GROUP) for _ in range(MT)]
        assert at[0] <= ffn_at
        at[0] = ffn_at
        cacc, zabs, zexp, zlog, zpos, delta, dx, gated = ([cut(GROUP) for _ in range(MT)] for _ in range(8))
        dbx, hst = ([cut(GROUP) for _ in range(NH_BUF)] for _ in range(2))
        hc = cacc + [cut(GROUP) for _ in range(NHC - MT)]
        r1 = cut(GROUP)
        r2 = cut(GROUP)
        bc_parts = cut(GROUP // 2).bitcast(bf16)
        assert at[0] >= ffn_end
        w_in = cut(D_INNER)
        w_gate = cut(D_INNER)
        w_delta = cut(MT * D_INNER).rearrange("p (k n) -> p k n", k=MT)
        w_bc = cut(MT * P).rearrange("p (k n) -> p k n", k=MT)
        w_out = cut(MT * DIM).rearrange("p (k n) -> p k n", k=MT)
        conv_w = cut(MT * CONV).rearrange("p (m k) -> p m k", m=MT)
        mpar = cut(8 * MT).rearrange("p (m k) -> p m k", m=MT)
        a_neg = cut(MT * D_STATE).rearrange("p (m n) -> p m n", m=MT)
        sel = cut(2 * D_STATE * P // 2).bitcast(bf16).rearrange("p (n m) -> p n m", n=2 * D_STATE)
        sgate = [xT, xnT]

        bank = [ctx.enter_context(nc.psum_tensor(f"bank{i}", [P, 512], f32)) for i in range(8)]
        QB, KB, VOB, TRB, SAB, SBB, PTB, OB = bank[0], bank[1], bank[2], bank[3], bank[4], bank[5], bank[6], bank[7]

        const_in = sem("const_in")
        lpar_in = sem("lpar_in")
        cleared = sem("cleared")
        m_cleared = sem("m_cleared")
        x_in = [sem(f"x_in{u}", 0) for u in range(2)]
        x_turned = sem("x_turned", 2)
        x_kept = sem("x_kept", 2)
        ln_in = sem("ln_in")
        ln_mean = sem("ln_mean")
        ln_xc = sem("ln_xc", 2)
        ln_sq = sem("ln_sq")
        ln_var = sem("ln_var")
        ln_log = sem("ln_log", 2)
        ln_rstd = sem("ln_rstd")
        ln_aff = sem("ln_aff")
        ln_out = sem("ln_out", 2)
        in_done = sem("in_done")
        in_used = [sem(f"in_used{n}", 1) for n in range(2 * MT)]
        conv_step = sem("conv_step")
        conv_done = sem("conv_done", MT)
        act_done = sem("act_done", MT)
        sg_done = sem("sg_done")
        a_done = sem("a_done")
        d_done = sem("d_done")
        z_abs = sem("z_abs")
        z_exp = sem("z_exp")
        z_log = sem("z_log")
        z_pos = sem("z_pos", MT)
        delta_done = sem("delta_done")
        dx_done = sem("dx_done")
        bc_done = sem("bc_done")
        bc_step = sem("bc_step")
        bc_split = sem("bc_split", 1)
        b_ready = sem("b_ready")
        c_ready = sem("c_ready")
        dA_done = sem("dA_done")
        dbx_done = sem("dbx_done", 2 * MT)
        scan_done = sem("scan_done", NDA)
        hc_done = sem("hc_done", 2 * MT)
        y_step = sem("y_step", NHC)
        y_skip = sem("y_skip", MT)
        g_done = sem("g_done")
        mo_done = sem("mo_done", 1)
        mo_used = sem("mo_used", 1)
        wqkv_in = sem("wqkv_in")
        wo_in = sem("wo_in")
        w1_in = sem("w1_in")
        w2_in = sem("w2_in")
        tabs_done = sem("tabs_done")
        xs_ready = sem("xs_ready")
        proj_done = sem("proj_done")
        vproj_done = sem("vproj_done", 2 * NV)
        sq_ready = sem("sq_ready")
        sq_reduced = sem("sq_reduced", 2)
        ssq_ready = sem("ssq_ready")
        ln_done = sem("ln_done")
        r_done = sem("r_done")
        rope_q = sem("rope_q", 1)
        rope_k = sem("rope_k", 1)
        v_ready = sem("v_ready", 1)
        k_summed = sem("k_summed", 2)
        k_scaled = sem("k_scaled")
        tr_done = sem("tr_done", 4)
        tr_act = sem("tr_act", 1)
        tr_dve = sem("tr_dve", 1)
        sA_done = sem("sA_done")
        sB_done = sem("sB_done", 2 * PAIRS)
        mx_step = sem("mx_step")
        nb_ready = sem("nb_ready")
        expA = sem("expA", 2)
        expB = sem("expB", 2)
        rinv_ready = sem("rinv_ready")
        normed = sem("normed")
        pt_done = sem("pt_done", 2 * NP_BUF)
        pt_evac = sem("pt_evac", 1)
        pv_done = sem("pv_done", 2 * PAIRS)
        o_evac = sem("o_evac", 1)
        wo_done = sem("wo_done", 2 * NWO)
        x_added = sem("x_added", NWO + 1)
        ag_done = sem("ag_done")
        gelu_done = sem("gelu_done")
        hid_done = sem("hid_done", NHT)
        y_done = sem("y_done", 2)
        x_next = sem("x_next", 2)
        f_sum = sem("f_sum")
        f_turned = sem("f_turned", 2)
        f_ready = sem("f_ready", 2)
        f_out = [sem(f"f_out{u}") for u in range(2)]

        block = ctx.enter_context(nc.Block())

        def pair_loop(e, first, last, body):
            with e.Fori(first, last) as i:
                body(i)

        def swapped(a):
            return a.rearrange("p h (s e) -> p h s e", s=2)[:, :, ::-1, :]

        B_IN, B_GATE, CONV_B, B_DELTA, D_SK, B_OUT = range(6)

        @block.sync
        def _(sp):
            small = [
                (ident[:], t["ident"]), (ident16[:], t["ident16"]), (mask_a[:], t["mask_a"]), (mask_b[:], t["mask_b"]),
                (base_q[:], t["rope_q"]), (base_k[:], t["rope_k"]), (sel, t["sel"]),
                (w_in, t["L0_attn_W_in"]), (w_gate, t["L0_attn_W_gate"]),
                (w_delta, t["L0_attn_W_delta"].rearrange("(k p) n -> p k n", p=P)),
                (w_out, t["L0_attn_W_out"].rearrange("(k p) n -> p k n", p=P)),
                (conv_w, t["L0_attn_conv_w"].rearrange("(m p) o k -> p m (o k)", p=P)),
                (a_neg, t["L0_attn_A_log"].rearrange("(m p) n -> p m n", p=P)),
                (mpar[:, 0, B_OUT:B_OUT + 1], t["L0_attn_b_out"].rearrange("(p o) -> p o", o=1)),
            ]
            for col, name in ((B_IN, "b_in"), (B_GATE, "b_gate"), (CONV_B, "conv_b"), (B_DELTA, "b_delta"), (D_SK, "D_skip")):
                small.append((mpar[:, :, col], t[f"L0_attn_{name}"].rearrange("(m p) -> p m", p=P)))
            for copy in range(4):
                w = w_bc[:, :, 32 * copy:32 * copy + 32]
                small.append((w[:, :, 0:D_STATE], t["L0_attn_W_B"].rearrange("(k p) n -> p k n", p=P)))
                small.append((w[:, :, D_STATE:2 * D_STATE], t["L0_attn_W_C"].rearrange("(k p) n -> p k n", p=P)))
            with nc.allow_non_contiguous_dma("small parameters, once"):
                for dst, src in small:
                    sp.dma_start(dst, src).then_inc(const_in[0], 16)
            x_rows = t["L0_attn_x"].rearrange("s n f -> (s n) f")

            def load_pair(i):
                for u in range(2):
                    slot(sp, x_turned, i * 2 + u)
                    sp.dma_start(xtok[u], x_rows[ds((i * 2 + u) * GROUP, GROUP), :].rearrange("(c p) f -> p c f", p=P)) \
                        .then_inc(x_in[u][0], 16)
            pair_loop(sp, 0, GROUPS // 2, load_pair)

            vectors = [(lpar_all[:, :, 0], t["L0_ffn_ln_g"]), (lpar_all[:, :, 1], t["L0_ffn_ln_b"]),
                       (lpar_all[:, :, 2], t["L0_ffn_b2"])]
            for m, (h0, hn) in enumerate(HT):
                vectors.append((lpar_all[0:hn, :, 3 + m], t["L0_ffn_b1"][:, h0:h0 + hn]))
                vectors.append((lpar_all[0:hn, :, 3 + NHT + m], t["L0_ffn_b1"][:, HID + h0:HID + h0 + hn]))
            sp.wait_ge(cleared[0], 1)
            with nc.allow_non_contiguous_dma("small parameters, once"):
                for dst, src in vectors:
                    sp.dma_start(dst, src.rearrange("l p -> p l")).then_inc(lpar_in[0], 16)
                for dst, src in ((scale_q, t["L0_ffn_q_scale"]), (scale_k, t["L0_ffn_k_scale"])):
                    sp.dma_start(dst[:], src.unsqueeze(0).to_broadcast([P, DEPTH, HEAD])).then_inc(lpar_in[0], 16)

            def load_layer_front(l):
                sp.dma_start(wqkv[:], t["L0_ffn_Wqkv"][ds(l, 1), :, :].rearrange("o p n -> p (o n)")).then_inc(wqkv_in[0], 16)
                sp.dma_start(wo[:], t["L0_ffn_Wo"][ds(l, 1), :, :].rearrange("o (a p) n -> p (o a) n", p=P)).then_inc(wo_in[0], 16)

            def load_layer_back(l):
                sp.dma_start(w1[:], t["L0_ffn_W1"][ds(l, 1), :, :].rearrange("o p n -> p (o n)")).then_inc(w1_in[0], 16)
                sp.dma_start(w2[:, 0:NHT - 1, :], t["L0_ffn_W2"][ds(l, 1), 0:(NHT - 1) * P, :].rearrange("o (a p) n -> p (o a) n", p=P)) \
                    .then_inc(w2_in[0], 16)
                h0, hn = HT[-1]
                sp.dma_start(w2[0:hn, NHT - 1:NHT, :], t["L0_ffn_W2"][ds(l, 1), h0:HID, :].rearrange("o p n -> p o n")).then_inc(w2_in[0], 16)

            load_layer_front(0)
            load_layer_back(0)
            with sp.Fori(1, DEPTH) as l:
                sp.wait_ge(wo_done[0], l * (BATCH * NWO) + wo_done[1])
                load_layer_front(l)
                sp.wait_ge(y_done[0], l * GROUPS + y_done[1])
                load_layer_back(l)

            out_rows = out.rearrange("s n f -> (s n) f")

            def store_pair(i):
                for u in range(2):
                    item(sp, f_ready, i * 2 + u)
                    sp.dma_start(out_rows[ds((i * 2 + u) * GROUP, GROUP), :].rearrange("(c p) f -> p c f", p=P), xtok[u]) \
                        .then_inc(f_out[u][0], 16)
            pair_loop(sp, 0, GROUPS // 2, store_pair)
            for u in range(2):
                sp.wait_ge(f_out[u][0], 16 * (GROUPS // 2))

        N_CONST = 16 * (14 + 5 + 8)
        N_LPAR = 16 * (3 + 2 * NHT + 2)

        @block.gpsimd
        def _(pool):
            give_credits(pool, [k_summed])
            nc.gpsimd.memset(meanw[:], 1.0 / P)
            nc.gpsimd.memset(lpar_all[:], 0.0)
            nc.gpsimd.memset(eps[:], LN_EPS)
            nc.gpsimd.memset(w2[:, NHT - 1, :], 0.0)
            for u in range(2):
                nc.gpsimd.memset(hid_last[u][:], 0.0)
                nc.gpsimd.memset(xs[u][:, 0:1], 0.0)
            for m in range(MT):
                nc.gpsimd.memset(xz[m][:, :, 0:CONV - 1], 0.0)
            for n in range(NDA):
                last = nc.gpsimd.memset(dA[n].rearrange("p (s t) -> p s t", t=SEQ)[:, :, 0:1], 0.0)
            last.then_inc(cleared[0], 1)

            item(pool, mo_used, GROUPS - 1)
            for u in range(2):
                nc.gpsimd.memset(kT[u], 0.0)
                item(pool, ln_out, 2 * GROUPS - 1)
                nc.gpsimd.memset(xs2[u][:, :, 0:1], 0.0)
            for n in range(NP_BUF):
                last = nc.gpsimd.memset(pB[n][:, :, 0:FIRST_B], 0.0)
            last.then_inc(cleared[0], 1)

            def k_unit(B, qn):
                ki = qn // 2
                b = ki % 2
                item(pool, rope_k, B * (NQK // 2) + ki)
                slot(pool, tr_done, B * NQK + qn)
                k2 = ks[b].rearrange("p (h e) -> p h e", h=8)
                nc.gpsimd.tensor_tensor(k2, tk[b][:, 0], tk[b][:, 1], ALU.add).then_inc(k_summed[0], 1)
                item(pool, k_summed, B * (NQK // 2) + ki)
                item(pool, r_done, B * NQK + qn)
                nc.gpsimd.tensor_tensor(k2, k2, rk[b][:, :].unsqueeze(2).to_broadcast([P, 8, HEAD]), ALU.mult).then_inc(k_scaled[0], 1)

            def normalise(s, n):
                item(pool, rinv_ready, s)
                nc.gpsimd.tensor_tensor(pA[n], pA[n], rinv[n][:, 0:2].unsqueeze(2).to_broadcast([P, 2, P]), ALU.mult) \
                    .then_inc(normed[0], 1)
                pb = pB[n][:, :, FIRST_B:SEQ]
                nc.gpsimd.tensor_tensor(pb, pb, rinv[n][:, 2:4].unsqueeze(2).to_broadcast([P, 2, KEYS_B]), ALU.mult) \
                    .then_inc(normed[0], 1)

            def attention_slot(l, i, k, first, last):
                at_ = pair_at(l, i, k, LAG_NORMALISE, first, last)
                if at_:
                    normalise(at_[0], at_[4] % NP_BUF)
                at_ = unit_at(l, i, k, LAG_NORM, first, last)
                if at_ and at_[2] % 2:
                    k_unit(at_[0], at_[2])

            with pool.Fori(0, DEPTH) as l:
                attention_slots(pool, l, attention_slot)

        @block.scalar
        def _(act_e):
            A = nc.scalar.activation
            give_credits(act_e, [ln_log, act_done, f_ready, v_ready, tr_act, expA, expB, o_evac] + in_used)
            act_e.wait_ge(const_in[0], N_CONST)
            act_e.wait_ge(cleared[0], 1)
            act_e.preload_act_table_set(EXP_LN_SET)
            A(a_neg, a_neg, ACT.Exp).then_inc(a_done[0], 1)

            def ln_pair(g0):
                for u in range(2):
                    item(act_e, ln_xc, g0 + u)
                    A(sq2[u], xc[u], ACT.Square).then_inc(ln_sq[0], 1)
                for u in range(2):
                    item(act_e, ln_var, g0 + u)
                    slot(act_e, ln_out, g0 + u)
                    A(lg[u], bank[2 + u][:], ACT.Ln, bias=eps[:, 0:1]).then_inc(ln_log[0], 1)
                    item(act_e, ln_log, g0 + u)
                    A(rstd[u], lg[u], ACT.Exp, scale=-0.5).then_inc(ln_rstd[0], 1)

            pair_loop(act_e, 0, GROUPS // 2, lambda i: ln_pair(i * 2))

            def mamba_in(g):
                for m in range(MT):
                    item(act_e, in_done, g * (2 * MT) + m)
                    slot(act_e, conv_done, g * MT + m)
                    A(xz[m][:, :, CONV - 1:], bank[m].rearrange("p (s t) -> p s t", t=SEQ), ACT.Identity,
                      bias=mpar[:, m, B_IN:B_IN + 1]).then_inc(in_used[m][0], 1)
                for m in range(MT):
                    item(act_e, in_done, g * (2 * MT) + (MT + m))
                    A(sgate[m][:, ds(g * GROUP, GROUP)], bank[MT + m][:], ACT.Silu, bias=mpar[:, m, B_GATE:B_GATE + 1]) \
                        .then_inc(in_used[MT + m][0], 1)
                for m in range(MT):
                    item(act_e, conv_done, g * MT + m)
                    A(act[m][:, ds(g * GROUP, GROUP)], cacc[m], ACT.Silu).then_inc(act_done[0], 1)

            act_e.preload_act_table(ACT.Silu)
            pair_loop(act_e, 0, GROUPS, mamba_in)
            act_e.preload_act_table_set(EXP_LN_SET)

            def scan_group(g):
                for m in range(MT):
                    item(act_e, d_done, g * MT + m)
                    A(zabs[m], bank[6 + m][:], ACT.Abs, bias=mpar[:, m, B_DELTA:B_DELTA + 1]).then_inc(z_abs[0], 1)
                for m in range(MT):
                    item(act_e, z_abs, g * MT + m)
                    A(zexp[m], zabs[m], ACT.Exp, scale=-1.0).then_inc(z_exp[0], 1)
                for m in range(MT):
                    item(act_e, z_exp, g * MT + m)
                    A(zlog[m], zexp[m], ACT.Ln, bias=1.0).then_inc(z_log[0], 1)
                for k in range(D_STATE * MT):
                    n, m = divmod(k, MT)
                    b = k % NDA
                    if k < MT:
                        item(act_e, delta_done, g * MT + m)
                    act_e.wait_ge(scan_done[0], g * (D_STATE * MT) + (k + 1 if k >= NDA else NDA))
                    d3 = delta[m].rearrange("p (s t) -> p s t", t=SEQ)
                    a3 = dA[b].rearrange("p (s t) -> p s t", t=SEQ)
                    A(a3[:, :, 1:], d3[:, :, 1:], ACT.Exp, scale=a_neg[:, m, n:n + 1]).then_inc(dA_done[0], 1)

            item(act_e, a_done, 1)
            pair_loop(act_e, 0, GROUPS, scan_group)
            pair_loop(act_e, 0, GROUPS // 2, lambda i: ln_pair(i * 2 + GROUPS))

            def norms(B, u, qn):
                c, j = QK_UNITS[qn]
                item(act_e, ssq_ready, B * NQK + qn)
                A(lnv[qn % 2][:], ssqc[qn % 2][:], ACT.Ln, scale=LN_SCALE).then_inc(ln_done[0], 1)
                item(act_e, ln_done, B * NQK + qn)
                dst = rq[u][:, c, 8 * j:8 * j + 8] if j < 2 else rk[qn // 2 % 2][:]
                A(dst, lnv[qn % 2][:], ACT.Exp, scale=-0.5).then_inc(r_done[0], 1)

            def evacuate(B, u, qn):
                c, j = QK_UNITS[qn]
                item(act_e, tr_done, B * NQK + qn)
                act_e.wait_ge(sB_done[0], B * PAIRS + PAIRS)
                src = TRB.rearrange("p (a t) -> p a t", a=4)
                if j < 2:
                    A(qT[u][:, 4 * j:4 * j + 4, c * P:c * P + P], src, ACT.Copy).then_inc(tr_act[0], 1)
                else:
                    A(kT[u][64:P, 4 * (j - 2):4 * (j - 2) + 4, 1, c * P:c * P + P], src[64:P], ACT.Copy).then_inc(tr_act[0], 1)

            def squares(B, u, qn):
                item(act_e, proj_done, B * NQK + qn)
                slot(act_e, sq_reduced, B * NQK + qn)
                A(sq[qn % 2], (QB, KB)[qn % 2][:], ACT.Square).then_inc(sq_ready[0], 1)

            def v_evac(B, u, vn):
                c, j = V_UNITS[vn]
                item(act_e, vproj_done, B * NV + vn)
                act_e.wait_ge(pv_done[0], B * PAIRS + PAIRS)
                A(vv[u][:, c, 512 * (j - 4):512 * (j - 4) + 512], VOB[:], ACT.Copy).then_inc(v_ready[0], 1)

            def exps(s, n, u, p, blk):
                item(act_e, nb_ready, s * 2 + blk)
                if blk == 0:
                    act_e.wait_ge(pt_done[0], s * 2 + 2)
                for h in range(2):
                    if blk == 0:
                        src, dst, done = SAB[:, h * P:h * P + P], pA[n][:, h, :], expA
                    else:
                        src, dst, done = SBB[:, h * KEYS_B:(h + 1) * KEYS_B], pB[n][:, h, FIRST_B:SEQ], expB
                    A(dst, src, ACT.Exp, bias=nbias[n][:, 2 * blk + h:2 * blk + h + 1],
                      scale=rq[u][:, blk, 2 * p + h:2 * p + h + 1],
                      accum_out=rsum[n][:, 2 * blk + h:2 * blk + h + 1]).then_inc(done[0], 1)

            def out_evac(s, B, u, p):
                item(act_e, pv_done, s)
                act_e.wait_ge(wo_done[0], B * NWO + NWO)
                A(oT[u][:, p, :], OB[:, 0:SEQ], ACT.Copy).then_inc(o_evac[0], 1)

            def attention_slot(l, i, k, first, last):
                at_ = pair_at(l, i, k, LAG_OUT, first, last)
                if at_:
                    out_evac(*at_[:4])
                at_ = v_at(l, i, k, 1, first, last)
                if at_:
                    v_evac(*at_)
                at_ = unit_at(l, i, k, LAG_UNIT_OUT, first, last)
                if at_:
                    evacuate(*at_)
                at_ = unit_at(l, i, k, LAG_NORM, first, last)
                if at_:
                    norms(*at_)
                at_ = pair_at(l, i, k, 0, first, last)
                if at_:
                    s, B, u, p, t_ = at_
                    for blk in range(2):
                        exps(s, t_ % NP_BUF, u, p, blk)
                at_ = unit_at(l, i, k, 0, first, last)
                if at_:
                    squares(*at_)

            def gelu_group(g, u):
                for m, (h0, hn) in enumerate(HT):
                    item(act_e, ag_done, g * NHT + m)
                    A(gl[m][0:hn], bank[NHT + m][0:hn, :], ACT.Gelu, bias=lpar[0:hn, 3 + NHT + m:4 + NHT + m]).then_inc(gelu_done[0], 1)

            act_e.wait_ge(cleared[0], 2)
            with act_e.Fori(0, DEPTH) as l:
                act_e.preload_act_table_set(EXP_LN_SET)
                attention_slots(act_e, l, attention_slot)
                with act_e.Fori(0, GROUPS // 2) as i:
                    ln_pair(l * GROUPS + i * 2 + 2 * GROUPS)
                act_e.preload_act_table(ACT.Gelu)
                with act_e.Fori(0, GROUPS // 2) as i:
                    for u in range(2):
                        gelu_group(l * GROUPS + i * 2 + u, u)

            def finish(i):
                for u in range(2):
                    item(act_e, f_turned, i * 2 + u)
                    act_e.wait_ge(f_out[u][0], i * 16) if not isinstance(i, int) or i else None
                    A(xtok[u], bank[u].rearrange("p (c f) -> p c f", f=DIM), ACT.Copy).then_inc(f_ready[0], 1)
            finish(0)
            pair_loop(act_e, 1, GROUPS // 2, finish)

        @block.vector
        def _(dve):
            V = nc.vector
            give_credits(dve, [x_kept, ln_xc, ln_out, z_pos, bc_split, dbx_done, scan_done, hc_done, y_skip, mo_used,
                               sq_reduced, rope_q, rope_k, tr_dve, pt_evac, x_added, hid_done, x_next, conv_done])
            dve.wait_ge(const_in[0], N_CONST)
            dve.wait_ge(cleared[0], 1)

            def keep(i):
                for u in range(2):
                    item(dve, x_turned, i * 2 + u)
                    V.tensor_copy(x1T[:, ds((i * 2 + u) * GROUP, GROUP)], bank[u][:]).then_inc(x_kept[0], 1)
            pair_loop(dve, 0, GROUPS // 2, keep)

            def ln_pair(g0, stage, finish):
                for u in range(2):
                    stage(u).then_inc(ln_in[0], 1)
                for u in range(2):
                    item(dve, ln_mean, g0 + u)
                    V.tensor_tensor(xc[u], xs2[u].rearrange("p s t -> p (s t)"), bank[u][:], ALU.subtract).then_inc(ln_xc[0], 1)
                for u in range(2):
                    item(dve, ln_rstd, g0 + u)
                    finish(u).then_inc(ln_out[0], 1)

            def plain_norm(g0, dst):
                def body(i):
                    ln_pair(i * 2 + g0,
                            lambda u: V.tensor_copy(xs2[u].rearrange("p s t -> p (s t)"), x1T[:, ds((i * 2 + u) * GROUP, GROUP)]),
                            lambda u: V.tensor_tensor(dst[:, ds((i * 2 + u) * GROUP, GROUP)], xc[u], rstd[u], ALU.mult))
                pair_loop(dve, 0, GROUPS // 2, body)

            item(dve, x_kept, GROUPS - 1)
            plain_norm(0, xnT)

            item(dve, a_done, 0)
            V.tensor_scalar(a_neg, a_neg, -1.0, None, ALU.mult).then_inc(a_done[0], 1)

            def conv_group(g):
                for m in range(MT):
                    item(dve, in_used[m], g)
                    slot(dve, act_done, g * MT + m)
                    c3 = cacc[m].rearrange("p (s t) -> p s t", t=SEQ)
                    V.tensor_scalar(c3, xz[m][:, :, CONV - 1:], conv_w[:, m, CONV - 1:CONV], mpar[:, m, CONV_B:CONV_B + 1],
                                    ALU.mult, ALU.add).then_inc(conv_step[0], 1)
                for tap in range(CONV - 2, -1, -1):
                    for m in range(MT):
                        step = (CONV - 2 - tap) * MT + m
                        item(dve, conv_step, g * ((CONV - 1) * MT) + step)
                        c3 = cacc[m].rearrange("p (s t) -> p s t", t=SEQ)
                        op = V.scalar_tensor_tensor(out=c3, in0=xz[m][:, :, tap:tap + SEQ], scalar=conv_w[:, m, tap:tap + 1],
                                                    in1=c3, op0=ALU.mult, op1=ALU.add)
                        op.then_inc(conv_step[0] if tap else conv_done[0], 1)
            pair_loop(dve, 0, GROUPS, conv_group)

            def scan_group(g):
                cols = ds(g * GROUP, GROUP)
                for m in range(MT):
                    item(dve, z_abs, g * MT + m)
                    V.tensor_scalar(zpos[m], bank[6 + m][:], mpar[:, m, B_DELTA:B_DELTA + 1], 0.0, ALU.add, ALU.max).then_inc(z_pos[0], 1)
                item(dve, bc_done, g)
                V.tensor_copy(bc_parts, bank[6][:]).then_inc(bc_step[0], 1)
                for m in range(MT):
                    item(dve, z_log, g * MT + m)
                    item(dve, z_pos, g * MT + m)
                    V.tensor_tensor(delta[m], zpos[m], zlog[m], ALU.add).then_inc(delta_done[0], 1)
                item(dve, bc_step, g * 4)
                V.tensor_tensor(r1, bank[6][:], bc_parts, ALU.subtract).then_inc(bc_step[0], 1)
                for m in range(MT):
                    item(dve, delta_done, g * MT + m)
                    V.tensor_tensor(dx[m], delta[m], act[m][:, cols], ALU.mult).then_inc(dx_done[0], 1)
                item(dve, bc_step, g * 4 + 1)
                V.tensor_copy(bc_parts[32:64], r1[32:64])
                V.tensor_copy(bc_parts[64:P], r1[64:P]).then_inc(bc_step[0], 1)
                item(dve, bc_step, g * 4 + 2)
                V.tensor_tensor(r2[64:96], r1[64:96], bc_parts[64:96], ALU.subtract).then_inc(bc_step[0], 1)
                item(dve, bc_step, g * 4 + 3)
                V.tensor_copy(bc_parts[64:96], r2[64:96]).then_inc(bc_split[0], 1)
                steps = D_STATE * MT
                for k in range(steps + 2):
                    if k < steps:
                        n, m = divmod(k, MT)
                        if k < MT:
                            item(dve, dx_done, g * MT + m)
                        item(dve, b_ready, g * D_STATE + n)
                        V.tensor_tensor(dbx[k % NH_BUF], dx[m], bank[n % 2][:], ALU.mult).then_inc(dbx_done[0], 1)
                    if 0 <= k - 1 < steps:
                        q = k - 1
                        item(dve, dA_done, g * steps + q)
                        item(dve, dbx_done, g * steps + q)
                        V.tensor_tensor_scan(hst[q % NH_BUF], dA[q % NDA], dbx[q % NH_BUF], 0.0, ALU.mult, ALU.add).then_inc(scan_done[0], 1)
                    if 0 <= k - 2:
                        q = k - 2
                        n = q // MT
                        item(dve, c_ready, g * D_STATE + n)
                        item(dve, scan_done, g * steps + q)
                        slot(dve, y_step, g * steps + q)
                        V.tensor_tensor(hc[q % NHC], hst[q % NH_BUF], bank[2 + n % 2][:], ALU.mult).then_inc(hc_done[0], 1)
                for m in range(MT):
                    item(dve, y_step, g * steps + (steps - MT + m))
                    V.scalar_tensor_tensor(out=zpos[m], in0=act[m][:, cols], scalar=mpar[:, m, D_SK:D_SK + 1], in1=bank[4 + m][:],
                                           op0=ALU.mult, op1=ALU.add).then_inc(y_skip[0], 1)
                slot(dve, mo_done, g)
                for m in range(MT):
                    item(dve, y_skip, g * MT + m)
                    V.tensor_tensor(gated[m], zpos[m], sgate[m][:, cols], ALU.mult).then_inc(g_done[0], 1)
                item(dve, mo_done, g)
                V.scalar_tensor_tensor(out=x1T[:, cols], in0=bank[7][:], scalar=mpar[:, 0, B_OUT:B_OUT + 1], in1=x1T[:, cols],
                                       op0=ALU.add, op1=ALU.add).then_inc(mo_used[0], 1)
            pair_loop(dve, 0, GROUPS, scan_group)

            item(dve, mo_used, GROUPS - 1)
            plain_norm(GROUPS, xT)

            def layer_tables(l):
                for c in range(CHUNKS):
                    for tab, base, sc in ((tab_q, base_q, scale_q), (tab_k, base_k, scale_k)):
                        V.tensor_tensor(tab[:, c], base[:, c], sc[:, ds(l, 1), :].to_broadcast([P, 2, HEAD]), ALU.mult) \
                            .then_inc(tabs_done[0], 1)
                V.tensor_copy(lpar[:], lpar_all[:, ds(l, 1), :].rearrange("p o n -> p (o n)")).then_inc(tabs_done[0], 1)

            def stage_x(B, u, col):
                dve.wait_ge(vproj_done[0], B * NV + NV)
                V.tensor_copy(xs[u][0:64, :], xT[0:64, ds(col, SEQ)])
                V.tensor_copy(xs[u][64:P, 1:SEQ], xT[64:P, ds(col, SEQ - 1)]).then_inc(xs_ready[0], 1)

            def evacuate(B, u, qn):
                c, j = QK_UNITS[qn]
                if j < 2:
                    return
                item(dve, tr_done, B * NQK + qn)
                dve.wait_ge(sB_done[0], B * PAIRS + PAIRS)
                V.tensor_copy(kT[u][0:64, 4 * (j - 2):4 * (j - 2) + 4, 0, c * P:c * P + P],
                              TRB.rearrange("p (a t) -> p a t", a=4)[0:64]).then_inc(tr_dve[0], 1)

            def rope(B, u, qn):
                c, j = QK_UNITS[qn]
                item(dve, sq_ready, B * NQK + qn)
                V.tensor_reduce(ssq[qn % 2][:], sq[qn % 2].rearrange("p (h e) -> p h e", h=8), op=ALU.add, axis=AX.X) \
                    .then_inc(sq_reduced[0], 1)
                b = qn // 2 % 2
                tab, dst, done = (tab_q, tq[b], rope_q) if j < 2 else (tab_k, tk[b], rope_k)
                if j < 2:
                    slot(dve, tr_done, B * NQK + qn)
                else:
                    slot(dve, k_summed, B * (NQK // 2) + qn // 2)
                src = (QB, KB)[qn % 2].rearrange("p (h e) -> p h e", h=8)
                V.tensor_tensor(dst[:, 0], src, tab[:, c, 0:1, :].to_broadcast([P, 8, HEAD]), ALU.mult)
                V.tensor_tensor(swapped(dst[:, 1]), src.rearrange("p h (s e) -> p h s e", s=2),
                                tab[:, c, 1:2, :].rearrange("p o (s e) -> p o s e", s=2).to_broadcast([P, 8, 2, HALF]),
                                ALU.mult).then_inc(done[0], 1)
                item(dve, sq_reduced, B * NQK + qn)
                V.tensor_scalar(ssqc[qn % 2][:], ssq[qn % 2][:], NORM_FLOOR, None, ALU.max).then_inc(ssq_ready[0], 1)

            def maxima(s, n, u, p, blk):
                bank_, keys, done = (SAB, P, sA_done) if blk == 0 else (SBB, KEYS_B, sB_done)
                item(dve, done, s)
                V.reduce_max(mx[n][:, 2 * blk:2 * blk + 2], bank_[:, 0:2 * keys].rearrange("p (h t) -> p h t", h=2), AX.X).then_inc(mx_step[0], 1)

            def biases(s, n, u, p, blk):
                item(dve, mx_step, s * 2 + blk)
                V.scalar_tensor_tensor(out=nbias[n][:, 2 * blk:2 * blk + 2], in0=mx[n][:, 2 * blk:2 * blk + 2], scalar=-1.0,
                                       in1=rq[u][:, blk, 2 * p:2 * p + 2], op0=ALU.mult, op1=ALU.mult).then_inc(nb_ready[0], 1)

            def probs_evac(s, b, h):
                item(dve, pt_done, s * 2 + h)
                dve.wait_ge(pv_done[0], s + (2 * PAIRS - 1))
                V.tensor_copy(pT[b][h], PTB[:, 0:P + WINDOW + P]).then_inc(pt_evac[0], 1)

            def add_x(B, place, u, pc, more):
                item(dve, wo_done, B * NWO + pc)
                if pc:
                    item(dve, x_added, B * NWO + (pc - 1))
                cols = ds(place * SEQ, SEQ)
                V.tensor_tensor(xT[:, cols], VOB[:, 0:SEQ], xT[:, cols], ALU.add).then_inc(x_added[0], 1)

            def inverse(s, n):
                item(dve, expA, s * 2 + 1)
                item(dve, expB, s * 2 + 1)
                V.reciprocal(rinv[n][:], rsum[n][:]).then_inc(rinv_ready[0], 1)

            def attention_slot(l, i, k, first, last):
                at_ = pair_at(l, i, k, LAG_NORMALISE, first, last)
                if at_:
                    inverse(at_[0], at_[4] % NP_BUF)
                at_ = wo_at(l, i, k, 1, first, last)
                if at_:
                    add_x(*at_)
                at_ = unit_at(l, i, k, LAG_UNIT_OUT, first, last)
                if at_:
                    evacuate(*at_)
                at_ = pair_at(l, i, k, 0, first, last)
                if at_:
                    s, B, u, p, t_ = at_
                    if p % 4 == 0:
                        item(dve, r_done, B * NQK + (p + 2))
                    for blk in range(2):
                        maxima(s, t_ % NP_BUF, u, p, blk)
                    for blk in range(2):
                        biases(s, t_ % NP_BUF, u, p, blk)
                turned = pair_at(l, i, k, LAG_TURN, first, last)
                if turned:
                    probs_evac(turned[0], turned[4] % 2, 0)
                at_ = unit_at(l, i, k, LAG_ROPE, first, last)
                if at_:
                    rope(*at_)
                if turned:
                    probs_evac(turned[0], turned[4] % 2, 1)
                at_ = unit_at(l, i, k, -1, first, last)
                if at_ and at_[2] == 0:
                    stage_x(at_[0], at_[1], i * (2 * SEQ) + ((k + 1) // PAIRS + 1) * SEQ)

            dve.wait_ge(lpar_in[0], N_LPAR)
            dve.wait_ge(cleared[0], 2)
            item(dve, ln_out, 2 * GROUPS - 1)
            with dve.Fori(0, DEPTH) as l:
                layer_tables(l)
                item(dve, tabs_done, l * (2 * CHUNKS + 1) + 2 * CHUNKS)
                stage_x(l * BATCH, 0, 0)
                attention_slots(dve, l, attention_slot)

                with dve.Fori(0, GROUPS // 2) as i:
                    item(dve, x_added, l * (BATCH * NWO) + (BATCH * NWO - 1))
                    def stage(u):
                        x3 = xT[:, ds((i * 2 + u) * GROUP, GROUP)].rearrange("p (s t) -> p s t", t=SEQ)
                        V.tensor_copy(xs2[u][0:64], x3[0:64])
                        return V.tensor_copy(xs2[u][64:P, :, 1:SEQ], x3[64:P, :, 0:SEQ - 1])

                    def finish(u):
                        V.scalar_tensor_tensor(out=aff[u], in0=xc[u], scalar=lpar[:, 0:1], in1=rstd[u], op0=ALU.mult, op1=ALU.mult) \
                            .then_inc(ln_aff[0], 1)
                        item(dve, ln_aff, l * GROUPS + i * 2 + u)
                        return V.tensor_scalar(xnT[:, ds((i * 2 + u) * GROUP, GROUP)], aff[u], lpar[:, 1:2], None, ALU.add)
                    ln_pair(l * GROUPS + i * 2 + 2 * GROUPS, stage, finish)

                with dve.Fori(0, GROUPS // 2) as i:
                    for u in range(2):
                        g = l * GROUPS + i * 2 + u
                        slot(dve, y_done, g)
                        for m, (h0, hn) in enumerate(HT):
                            item(dve, gelu_done, g * NHT + m)
                            V.scalar_tensor_tensor(out=hid[u][m][0:hn], in0=bank[m][0:hn, :], scalar=lpar[0:hn, 3 + m:4 + m],
                                                   in1=gl[m][0:hn], op0=ALU.add, op1=ALU.mult).then_inc(hid_done[0], 1)
                        item(dve, y_done, g)
                        cols = ds((i * 2 + u) * GROUP, GROUP)
                        V.scalar_tensor_tensor(out=xT[:, cols], in0=bank[2 * NHT + u][:], scalar=lpar[:, 2:3], in1=xT[:, cols],
                                               op0=ALU.add, op1=ALU.add).then_inc(x_next[0], 1)
                item(dve, x_next, l * GROUPS + (GROUPS - 1))

            def finish(i):
                for u in range(2):
                    cols = ds((i * 2 + u) * GROUP, GROUP)
                    slot(dve, f_turned, i * 2 + u)
                    V.tensor_tensor(fin[u], x1T[:, cols], xT[:, cols], ALU.add).then_inc(f_sum[0], 1)
            pair_loop(dve, 0, GROUPS // 2, finish)

        @block.tensor
        def _(pe):
            give_credits(pe, [x_turned, y_step, mo_done, vproj_done, tr_done, sB_done, pt_done, pv_done, wo_done, y_done, f_turned])
            MM = nc.tensor.matmul

            def turn(out_, in_, **kw):
                k = in_.shape[0]
                return MM(out_, lhsT=in_, rhs=ident[0:k, 0:k], is_transpose=True, **kw)

            pe.wait_ge(const_in[0], N_CONST)
            pe.wait_ge(cleared[0], 1)

            def load_pair(i):
                for u in range(2):
                    pe.wait_ge(x_in[u][0], i * 16 + 16)
                    slot(pe, x_kept, i * 2 + u)
                    for c in range(GROUP // P):
                        last = turn(bank[u][:, c * P:(c + 1) * P], xtok[u][:, c, :], start=True, stop=True)
                    last.then_inc(x_turned[0], 1)
            pair_loop(pe, 0, GROUPS // 2, load_pair)

            def ln_pair(g0):
                for u in range(2):
                    item(pe, ln_in, g0 + u)
                    slot(pe, ln_xc, g0 + u)
                    MM(bank[u][:], lhsT=meanw[:], rhs=xs2[u].rearrange("p s t -> p (s t)"), start=True, stop=True).then_inc(ln_mean[0], 1)
                for u in range(2):
                    item(pe, ln_sq, g0 + u)
                    slot(pe, ln_log, g0 + u)
                    MM(bank[2 + u][:], lhsT=meanw[:], rhs=sq2[u], start=True, stop=True).then_inc(ln_var[0], 1)

            item(pe, x_kept, GROUPS - 1)
            pair_loop(pe, 0, GROUPS // 2, lambda i: ln_pair(i * 2))

            def mamba_in(g):
                rhs = xnT[:, ds(g * GROUP, GROUP)]
                for n in range(2 * MT):
                    slot(pe, in_used[n], g)
                    w = (w_in, w_gate)[n // MT]
                    m = n % MT
                    MM(bank[n][:], lhsT=w[:, m * P:(m + 1) * P], rhs=rhs, start=True, stop=True).then_inc(in_done[0], 1)

            item(pe, ln_out, GROUPS - 1)
            pair_loop(pe, 0, GROUPS, mamba_in)

            def scan_group(g):
                cols = ds(g * GROUP, GROUP)
                for m in range(MT):
                    if m == 0:
                        slot(pe, bc_split, g)
                    else:
                        slot(pe, mo_used, g)
                    for k in range(MT):
                        last = MM(bank[6 + m][:], lhsT=w_delta[:, k, m * P:(m + 1) * P], rhs=act[k][:, cols], start=k == 0, stop=k == MT - 1)
                    last.then_inc(d_done[0], 1)
                item(pe, z_pos, g * MT)
                for k in range(MT):
                    last = MM(bank[6][:], lhsT=w_bc[:, k, :], rhs=act[k][:, cols], start=k == 0, stop=k == MT - 1)
                last.then_inc(bc_done[0], 1)
                item(pe, bc_split, g)
                steps = D_STATE * MT

                def spread_b(n):
                    pe.wait_ge(dbx_done[0], g * steps + (n + 1) * MT)
                    MM(bank[n % 2][:], lhsT=sel[:, n, :], rhs=bc_parts, start=True, stop=True).then_inc(b_ready[0], 1)

                def spread_c(n):
                    pe.wait_ge(hc_done[0], g * steps + (n + 1) * MT)
                    MM(bank[2 + n % 2][:], lhsT=sel[:, D_STATE + n, :], rhs=bc_parts, start=True, stop=True).then_inc(c_ready[0], 1)

                spread_b(0)
                spread_c(0)
                for m in range(MT):
                    slot(pe, y_skip, g * MT + m)
                for n in range(D_STATE + 1):
                    if n + 1 < D_STATE:
                        spread_b(n + 1)
                    for m in range(MT):
                        k = (n - 1) * MT + m
                        if k >= 0:
                            item(pe, hc_done, g * steps + k)
                            MM(bank[4 + m][:], lhsT=ident[:], rhs=hc[k % NHC], start=n == 1, stop=n == D_STATE).then_inc(y_step[0], 1)
                    if n + 1 < D_STATE:
                        spread_c(n + 1)
                for m in range(MT):
                    item(pe, g_done, g * MT + m)
                    last = MM(bank[7][:], lhsT=w_out[:, m, :], rhs=gated[m], start=m == 0, stop=m == MT - 1)
                last.then_inc(mo_done[0], 1)

            item(pe, act_done, GROUPS * MT - 1)
            for n in range(2 * MT):
                item(pe, in_used[n], GROUPS - 1)
            pair_loop(pe, 0, GROUPS, scan_group)
            item(pe, mo_used, GROUPS - 1)
            pair_loop(pe, 0, GROUPS // 2, lambda i: ln_pair(i * 2 + GROUPS))
            item(pe, ln_out, 2 * GROUPS - 1)

            def transposes(B, u, qn):
                c, j = QK_UNITS[qn]
                b = qn // 2 % 2
                slot(pe, tr_act, B * NQK + qn)
                if j < 2:
                    slot(pe, tr_dve, B * (NQK // 2) + qn // 2)
                    item(pe, rope_q, B * (NQK // 2) + qn // 2)
                    for a in range(4):
                        turn(TRB[:, a * P:(a + 1) * P], tq[b][:, 0, 2 * a:2 * a + 2, :].rearrange("p h e -> p (h e)"), start=True, stop=False)
                        last = turn(TRB[:, a * P:(a + 1) * P], tq[b][:, 1, 2 * a:2 * a + 2, :].rearrange("p h e -> p (h e)"), start=False, stop=True)
                else:
                    item(pe, k_scaled, B * (NQK // 2) + qn // 2)
                    for a in range(4):
                        last = turn(TRB[:, a * P:(a + 1) * P], ks[b][:, a * P:(a + 1) * P], start=True, stop=True)
                last.then_inc(tr_done[0], 1)

            def unit(B, u, qn):
                c, j = QK_UNITS[qn]
                if qn == 0:
                    item(pe, xs_ready, B)
                slot(pe, rope_q if j < 2 else rope_k, B * (NQK // 2) + qn // 2)
                MM((QB, KB)[qn % 2][:], lhsT=xs[u][:, c * P:(c + 1) * P], rhs=wqkv[:, j * 512:(j + 1) * 512],
                   start=True, stop=True).then_inc(proj_done[0], 1)

            def v_unit(B, u, vn):
                c, j = V_UNITS[vn]
                slot(pe, v_ready, B * NV + vn)
                slot(pe, x_added, B * NWO + vn)
                MM(VOB[:], lhsT=xs[u][:, c * P:(c + 1) * P], rhs=wqkv[:, j * 512:(j + 1) * 512],
                   start=True, stop=True).then_inc(vproj_done[0], 1)

            def scores(s, B, u, p):
                if p % 4 == 0:
                    item(pe, tr_act, B * NQK + (p + 3))
                    item(pe, tr_dve, B * (NQK // 2) + (p // 2 + 1))
                for bank_, first, keys, mask, free, done, q0 in (
                        (SAB, 0, P, mask_a, expA, sA_done, 0), (SBB, FIRST_B, KEYS_B, mask_b, expB, sB_done, P)):
                    pe.wait_ge(free[0], s * 2 + 2)
                    dst = bank_[:, 0:2 * keys]
                    MM(dst, lhsT=ident16[:], rhs=mask[:, :].unsqueeze(1).to_broadcast([P, 2, keys]), start=True, stop=False)
                    MM(dst, lhsT=qT[u][:, p, q0:q0 + P], rhs=kT[u][:, p, :, first:first + keys], start=False, stop=True) \
                        .then_inc(done[0], 1)

            def probs_turn(s, n, h):
                slot(pe, pt_evac, s * 2 + h)
                if h == 0:
                    item(pe, normed, s * 2 + 1)
                turn(PTB[:, 0:P], pA[n][:, h, :], start=True, stop=True)
                turn(PTB[:, P:P + WINDOW], pB[n][0:WINDOW, h, 0:P], start=True, stop=True)
                turn(PTB[:, P + WINDOW:2 * P + WINDOW], pB[n][:, h, P:SEQ], start=True, stop=True).then_inc(pt_done[0], 1)

            def values(s, B, u, p, b):
                item(pe, pt_evac, s * 2 + 1)
                slot(pe, o_evac, s)
                if p % 4 == 0:
                    item(pe, v_ready, B * NV + (p // 4 * 2 + 1))
                for c, q0, t0, n in ((0, 0, 0, P + WINDOW), (1, P, P + WINDOW, P)):
                    for h in range(2):
                        col = (2 * p + h) * HEAD
                        last = MM(OB[64 * h:64 * h + 64, q0:q0 + n], lhsT=vv[u][:, c, col:col + HEAD], rhs=pT[b][h][:, t0:t0 + n],
                                  start=c == 0, stop=c == 1, skip_group_check=True)
                last.then_inc(pv_done[0], 1)

            def project(B, place, u, pc, more):
                item(pe, o_evac, B * PAIRS + (2 * pc + 1))
                pe.wait_ge(x_added[0], B * NWO + (pc + x_added[1]))
                if more:
                    item(pe, v_ready, B * NV + (NV + pc))
                for a in (2 * pc, 2 * pc + 1):
                    last = MM(VOB[:, 0:SEQ], lhsT=wo[:, a, :], rhs=oT[u][:, a, :], start=a % 2 == 0, stop=a % 2 == 1)
                last.then_inc(wo_done[0], 1)

            def attention_slot(l, i, k, first, last):
                at_ = pair_at(l, i, k, 0, first, last)
                if at_:
                    scores(*at_[:4])
                turned = pair_at(l, i, k, LAG_TURN, first, last)
                if turned:
                    probs_turn(turned[0], turned[4] % NP_BUF, 0)
                at_ = unit_at(l, i, k, 0, first, last)
                if at_:
                    unit(*at_)
                at_ = v_at(l, i, k, 0, first, last)
                if at_:
                    v_unit(*at_)
                at_ = wo_at(l, i, k, 0, first, last)
                if at_:
                    project(*at_)
                if turned:
                    probs_turn(turned[0], turned[4] % NP_BUF, 1)
                at_ = unit_at(l, i, k, LAG_UNIT_TURN, first, last)
                if at_:
                    transposes(*at_)
                at_ = pair_at(l, i, k, LAG_VALUES, first, last)
                if at_:
                    s, B, u, p, t_ = at_
                    values(s, B, u, p, t_ % 2)

            with pe.Fori(0, DEPTH) as l:
                pe.wait_ge(wqkv_in[0], l * 16 + 16)
                pe.wait_ge(wo_in[0], l * 16 + 16)
                attention_slots(pe, l, attention_slot)

                with pe.Fori(0, GROUPS // 2) as i:
                    ln_pair(l * GROUPS + i * 2 + 2 * GROUPS)

                with pe.Fori(0, GROUPS // 2) as i:
                    pe.wait_ge(w1_in[0], l * 16 + 16)
                    pe.wait_ge(w2_in[0], l * 32 + 32)
                    item(pe, ln_out, l * GROUPS + (3 * GROUPS - 1))

                    def up(u, m):
                        g = l * GROUPS + i * 2 + u
                        h0, hn = HT[m]
                        rhs = xnT[:, ds((i * 2 + u) * GROUP, GROUP)]
                        slot(pe, hid_done, g * NHT + m)
                        MM(bank[m][0:hn, :], lhsT=w1[:, h0:h0 + hn], rhs=rhs, start=True, stop=True)
                        MM(bank[NHT + m][0:hn, :], lhsT=w1[:, HID + h0:HID + h0 + hn], rhs=rhs, start=True, stop=True) \
                            .then_inc(ag_done[0], 1)

                    def down(u):
                        g = l * GROUPS + i * 2 + u
                        slot(pe, x_next, g)
                        for m in range(NHT):
                            item(pe, hid_done, g * NHT + m)
                            last = MM(bank[2 * NHT + u][:], lhsT=w2[:, m, :], rhs=hid[u][m], start=m == 0, stop=m == NHT - 1)
                        last.then_inc(y_done[0], 1)

                    for m in range(NHT):
                        up(0, m)
                    up(1, 0)
                    down(0)
                    for m in range(1, NHT):
                        up(1, m)
                    down(1)

            def finish(i):
                for u in range(2):
                    item(pe, f_sum, i * 2 + u)
                    slot(pe, f_ready, i * 2 + u)
                    for c in range(GROUP // P):
                        last = turn(bank[u][:, c * P:(c + 1) * P], fin[u][:, c * P:(c + 1) * P], start=True, stop=True)
                    last.then_inc(f_turned[0], 1)
            pair_loop(pe, 0, GROUPS // 2, finish)


_NAMES = ['L0_attn_x', 'L0_attn_W_in', 'L0_attn_b_in', 'L0_attn_W_gate', 'L0_attn_b_gate', 'L0_attn_conv_w',
          'L0_attn_conv_b', 'L0_attn_A_log', 'L0_attn_D_skip', 'L0_attn_W_delta', 'L0_attn_b_delta', 'L0_attn_W_B',
          'L0_attn_W_C', 'L0_attn_W_out', 'L0_attn_b_out', 'L0_ffn_Wqkv', 'L0_ffn_q_scale', 'L0_ffn_k_scale',
          'L0_ffn_Wo', 'L0_ffn_ln_g', 'L0_ffn_ln_b', 'L0_ffn_W1', 'L0_ffn_b1', 'L0_ffn_W2', 'L0_ffn_b2']


def constants():
    import numpy as np
    bf = mybir.dt.np(mybir.dt.bfloat16)
    f = np.float32
    out = {"ident": np.eye(P, dtype=f), "ident16": np.eye(P).astype(bf)}
    i, k = np.arange(P)[:, None], np.arange(P)[None, :]
    out["mask_a"] = np.where((k <= i) & (k >= i - WINDOW), 0.0, MASKED).astype(bf)
    i, k = i + P, np.arange(FIRST_B, SEQ)[None, :]
    out["mask_b"] = np.where((k <= i) & (k >= i - WINDOW), 0.0, MASKED).astype(bf)
    sel = np.zeros((P, 2 * D_STATE, P))
    for n in range(2 * D_STATE):
        sel[[n, 32 + n, 64 + n], n, :] = 1.0
    out["sel"] = sel.astype(bf)
    half = np.arange(0, HEAD, 2, dtype=f)
    inv_freq = (f(1.0) / np.power(f(10000.0), half / f(HEAD))).astype(f)
    pos = np.arange(SEQ, dtype=f)
    freqs = (pos[:, None] * inv_freq[None, :]).astype(f)
    freqs = np.concatenate([freqs, freqs], -1).astype(np.float64)
    base = ((half + f(0.4 * HEAD)) / f(1.4 * HEAD)).astype(f)
    power = ((pos - SEQ // 2) / f(WINDOW // 2)).astype(f)
    scale = np.power(base[None, :].astype(np.float64), power[:, None].astype(np.float64))
    scale = np.concatenate([scale, scale], -1)
    sign = np.where(np.arange(HEAD) < HALF, 1.0, -1.0)[None, :]
    for name, sc in (("rope_q", scale * 8.0), ("rope_k", 1.0 / scale)):
        tab = np.stack([np.cos(freqs) * sc, np.sin(freqs) * sc * sign], 1) * 2.0 ** 16
        out[name] = np.ascontiguousarray(tab.reshape(CHUNKS, P, 2, HEAD).transpose(1, 0, 2, 3)).astype(f)
    return out


def kernel(**inputs):
    import numpy as np
    import concourse.bacc as bacc
    from concourse.bass_utils import run_bass_kernel_spmd

    nc = bacc.Bacc("TRN2", target_bir_lowering=False, num_devices=1)
    arrays, aps = {}, {}
    given = {n: np.ascontiguousarray(inputs[n]) for n in _NAMES}
    given.update(constants())
    for name, a in given.items():
        arrays["in_" + name] = a
        aps[name] = nc.dram_tensor("in_" + name, a.shape, mybir.dt.from_np(a.dtype), kind="ExternalInput").ap()
    out = nc.dram_tensor("out", (BATCH, SEQ, DIM), mybir.dt.float32, kind="ExternalOutput").ap()
    build(nc, aps, out)
    r = run_bass_kernel_spmd(nc, [arrays], core_ids=[0])
    return r.results[0]["out"]
```

```python
import concourse.bass as bass
from concourse import mybir
from contextlib import ExitStack

BATCH, SEQ, DIM = 16, 256, 128
TOKENS = BATCH * SEQ
P = 128
GROUP = 512
GROUPS = TOKENS // GROUP
SEQ_PER_GROUP = GROUP // SEQ
CHUNKS = SEQ // P
D_INNER, D_STATE, CONV = 256, 16, 4
MT = D_INNER // P
DEPTH, HEADS, HEAD, WINDOW = 6, 16, 64, 32
INNER = HEADS * HEAD
HALF = HEAD // 2
PAIRS = HEADS // 2
HID = int(DIM * 4 * 2 / 3)
HT = [(m * P, min(P, HID - m * P)) for m in range((HID + P - 1) // P)]
NHT = len(HT)
KEYS_B = P + WINDOW
FIRST_B = P - WINDOW
NLN = 4
NP_BUF = 4

SLOTS = 2 * PAIRS
QK_UNITS = [(0, 0), (0, 2), (1, 0), (1, 2), (0, 1), (0, 3), (1, 1), (1, 3)]
NQK = len(QK_UNITS)
V_UNITS = [(0, 4), (1, 4), (0, 5), (1, 5)]
NV = len(V_UNITS)
V_FIRST = 6
NWO = PAIRS // 2
WO_FIRST = 5
LAG_NORMALISE, LAG_TURN, LAG_VALUES, LAG_OUT = 1, 2, 3, 4
LAG_ROPE, LAG_NORM, LAG_UNIT_TURN, LAG_UNIT_OUT = 1, 2, 3, 4
NORM_FIRST = 5
LAG_MEAN, LAG_VAR, LAG_RSTD, LAG_NORMED = 1, 2, 3, 4
DRAIN = NORM_FIRST + LAG_NORMED + 1


def pair_at(l, i, k, lag, first, last):
    t = k - lag
    if (first and t < 0) or (last and t >= SLOTS):
        return None
    return l * (BATCH * PAIRS) + i * SLOTS + t, l * BATCH + i * 2 + t // PAIRS, t // PAIRS % 2, t % PAIRS, t


def unit_at(l, i, k, lag, first, last):
    t = k - lag
    if (first and t < -PAIRS) or (last and t >= PAIRS):
        return None
    return l * BATCH + i * 2 + (t // PAIRS + 1), (t // PAIRS + 1) % 2, t % PAIRS


def v_at(l, i, k, lag, first, last):
    t = k - V_FIRST - lag
    if t % 2 or (first and t < -PAIRS) or (last and t >= PAIRS):
        return None
    return l * BATCH + i * 2 + (t // PAIRS + 1), (t // PAIRS + 1) % 2, t % PAIRS // 2


def wo_at(l, i, k, lag, first, last):
    t = k - WO_FIRST - lag
    if t % 2 or (first and t < 0) or (last and t >= SLOTS):
        return None
    return l * BATCH + i * 2 + t // PAIRS, i * 2 + t // PAIRS, t // PAIRS % 2, t % PAIRS // 2, not (last and t >= PAIRS)


def norm_at(l, i, k, lag, first, last):
    t = k - lag - NORM_FIRST - SLOTS
    if t % SLOTS or (first and t < 0):
        return None
    group = i + t // SLOTS
    return group, l * GROUPS + group + 2 * GROUPS, l * (BATCH * PAIRS) + i * SLOTS + min(k - LAG_VALUES - 1, SLOTS - 1)


def attention_slots(e, l, body):
    for k in range(-PAIRS, SLOTS):
        body(l, 0, k, True, False)
    with e.Fori(1, BATCH // 2 - 1) as i:
        for k in range(SLOTS):
            body(l, i, k, False, False)
    for k in range(SLOTS + DRAIN):
        body(l, BATCH // 2 - 1, k, False, True)


LN_SCALE = float(2 ** 32)
NORM_FLOOR = 1e-24
LN_EPS = 1e-5
MASKED = -3.0e38
EXP_LN_SET = "natural_log_exp_and_others"


def build(nc, t, out):
    f32, bf16 = mybir.dt.float32, mybir.dt.bfloat16
    ALU, ACT, AX = mybir.AluOpType, mybir.ActivationFunctionType, mybir.AxisListType
    ctx = ExitStack()
    with ctx:
        def sb(name, shape, dt=f32):
            return ctx.enter_context(nc.sbuf_tensor(name, shape, dt))

        credit = {}

        def sem(name, credits=0):
            s = ctx.enter_context(nc.semaphore(name))
            credit[name] = credits
            return (s, credits)

        def item(e, s, n):
            e.wait_ge(s[0], n + (1 + s[1]))

        def slot(e, s, n):
            e.wait_ge(s[0], n + 1)

        def give_credits(e, sems):
            for s in sems:
                e.sem_inc(s[0], s[1])

        ds = bass.ds

        x1T = sb("x1T", [P, TOKENS])
        xT = sb("xT", [P, TOKENS])
        xnT = sb("xnT", [P, TOKENS])
        ident = sb("ident", [P, P])
        ident16 = sb("ident16", [P, P], bf16)
        meanw = sb("meanw", [P, P])
        mask_a = sb("mask_a", [P, P], bf16)
        mask_b = sb("mask_b", [P, KEYS_B], bf16)
        base_q = sb("base_q", [P, CHUNKS, 2, HEAD])
        base_k = sb("base_k", [P, CHUNKS, 2, HEAD])
        tab_q = sb("tab_q", [P, CHUNKS, 2, HEAD])
        tab_k = sb("tab_k", [P, CHUNKS, 2, HEAD])
        scale_q = sb("scale_q", [P, DEPTH, HEAD])
        scale_k = sb("scale_k", [P, DEPTH, HEAD])
        NPAR = 3 + 2 * NHT
        lpar_all = sb("lpar_all", [P, DEPTH, NPAR])
        lpar = sb("lpar", [P, NPAR])
        eps = sb("eps", [P, 1])
        wqkv = sb("wqkv", [P, 3 * INNER])
        wo = sb("wo", [P, PAIRS, DIM])
        w1 = sb("w1", [P, 2 * HID])
        w2 = sb("w2", [P, NHT, DIM])
        xs = [sb(f"xs{u}", [P, SEQ]) for u in range(2)]
        xs2 = sb("xs2", [P, SEQ_PER_GROUP, SEQ])
        hid_last = [sb(f"hid_last{u}", [P, GROUP]) for u in range(2)]
        ssq = [sb(f"ssq{u}", [P, 8]) for u in range(2)]
        ssqc = [sb(f"ssqc{u}", [P, 8]) for u in range(2)]
        lnv = [sb(f"lnv{u}", [P, 8]) for u in range(2)]
        rq = [sb(f"rq{u}", [P, CHUNKS, HEADS]) for u in range(2)]
        rk = [sb(f"rk{u}", [P, 8]) for u in range(2)]
        mx = [sb(f"mx{n}", [P, 4]) for n in range(NP_BUF)]
        nbias = [sb(f"nbias{n}", [P, 4]) for n in range(NP_BUF)]
        rsum = [sb(f"rsum{n}", [P, 4]) for n in range(NP_BUF)]
        rinv = [sb(f"rinv{n}", [P, 4]) for n in range(NP_BUF)]

        ARENA = 28992
        arena = sb("arena", [P, ARENA])
        at = [0]

        def cut(cols):
            a = arena[:, at[0]:at[0] + cols]
            at[0] += cols
            assert at[0] <= ARENA, at[0]
            return a

        kT = cut(PAIRS * 2 * SEQ).rearrange("p (a h t) -> p a h t", a=PAIRS, h=2)
        pB = [cut(2 * SEQ).rearrange("p (h t) -> p h t", h=2) for _ in range(NP_BUF)]
        pA = [cut(2 * P).rearrange("p (h t) -> p h t", h=2) for _ in range(NP_BUF)]
        tq = [cut(2 * 512).rearrange("p (s h e) -> p s h e", s=2, h=8) for _ in range(2)]
        tk = [cut(2 * 512).rearrange("p (s h e) -> p s h e", s=2, h=8) for _ in range(2)]
        ffn_at = at[0]
        xc, sq2, rstd = ([cut(GROUP)] for _ in range(3))
        attention_at = at[0]
        qT = cut(PAIRS * SEQ).rearrange("p (a t) -> p a t", a=PAIRS)
        vv = cut(CHUNKS * INNER).rearrange("p (c n) -> p c n", c=CHUNKS)
        oT = cut(PAIRS * SEQ).rearrange("p (a t) -> p a t", a=PAIRS)
        sq = [cut(512) for _ in range(2)]
        ks = [cut(512) for _ in range(2)]
        pT = [[cut(P + WINDOW + P) for _ in range(2)] for _ in range(2)]
        at[0] = attention_at
        for buffers in (xc, sq2, rstd):
            buffers += [cut(GROUP) for _ in range(NLN - 1)]
        gl = [cut(GROUP) for _ in range(NHT)]
        hid = [[cut(GROUP) for _ in range(NHT - 1)] + [hid_last[u][:, :]] for u in range(2)]
        xtok = [cut(GROUP).rearrange("p (c f) -> p c f", f=DIM) for _ in range(2)]
        fin = [cut(GROUP) for _ in range(2)]
        ffn_end = at[0]
        at[0] = 0
        act = [cut(TOKENS) for _ in range(MT)]
        NDA, NH_BUF, NHC = 3, 3, 4
        dA = [cut(GROUP) for _ in range(NDA)]
        xz = [cut(SEQ_PER_GROUP * (SEQ + CONV - 1)).rearrange("p (s t) -> p s t", s=SEQ_PER_GROUP) for _ in range(MT)]
        assert at[0] <= ffn_at
        at[0] = ffn_at
        cacc, zabs, zexp, zpos, delta, dx, gated = ([cut(GROUP) for _ in range(MT)] for _ in range(7))
        zlog = zexp
        dbx = [cut(GROUP) for _ in range(NH_BUF)]
        hst = [cut(GROUP) for _ in range(NHC)]
        c_sb = [x.rearrange("p s t -> p (s t)")[:, 0:GROUP] for x in xz]
        hc = cacc + [cut(GROUP) for _ in range(NHC - MT)]
        r1 = cut(GROUP)
        r2 = cut(GROUP)
        bc_parts = cut(GROUP // 2).bitcast(bf16)
        assert at[0] >= ffn_end
        w_in = cut(D_INNER)
        w_gate = cut(D_INNER)
        w_delta = cut(MT * D_INNER).rearrange("p (k n) -> p k n", k=MT)
        w_bc = cut(MT * P).rearrange("p (k n) -> p k n", k=MT)
        w_out = cut(MT * DIM).rearrange("p (k n) -> p k n", k=MT)
        conv_w = cut(MT * CONV).rearrange("p (m k) -> p m k", m=MT)
        mpar = cut(8 * MT).rearrange("p (m k) -> p m k", m=MT)
        a_neg = cut(MT * D_STATE).rearrange("p (m n) -> p m n", m=MT)
        sel = cut(2 * D_STATE * P // 2).bitcast(bf16).rearrange("p (n m) -> p n m", n=2 * D_STATE)
        sgate = [xT, xnT]

        bank = [ctx.enter_context(nc.psum_tensor(f"bank{i}", [P, 512], f32)) for i in range(8)]
        QB, KB, VOB, TRB, SAB, SBB, PTB, OB = bank[0], bank[1], bank[2], bank[3], bank[4], bank[5], bank[6], bank[7]

        const_in = sem("const_in")
        lpar_in = sem("lpar_in")
        cleared = sem("cleared")
        x_in = [sem(f"x_in{u}", 0) for u in range(2)]
        x_turned = sem("x_turned", 2)
        x_kept = sem("x_kept", 2)
        ln_in = sem("ln_in")
        ln_mean = sem("ln_mean")
        ln_xc = sem("ln_xc", NLN)
        ln_sq = sem("ln_sq")
        ln_var = sem("ln_var")
        ln_log = sem("ln_log", NLN)
        ln_rstd = sem("ln_rstd")
        ln_aff = sem("ln_aff")
        ln_out = sem("ln_out", NLN)
        in_done = sem("in_done")
        in_used = [sem(f"in_used{n}", 1) for n in range(2 * MT)]
        conv_step = sem("conv_step")
        conv_done = sem("conv_done", MT)
        act_done = sem("act_done", MT)
        sg_done = sem("sg_done")
        a_done = sem("a_done")
        d_done = sem("d_done")
        z_abs = sem("z_abs")
        z_exp = sem("z_exp")
        z_log = sem("z_log")
        z_pos = sem("z_pos")
        delta_done = sem("delta_done")
        dx_done = sem("dx_done")
        bc_done = sem("bc_done")
        bc_step = sem("bc_step")
        bc_split = sem("bc_split", 1)
        b_ready = sem("b_ready")
        c_ready = sem("c_ready")
        dA_done = sem("dA_done")
        dbx_done = sem("dbx_done", 2 * MT)
        scan_done = sem("scan_done", NDA)
        c_kept = sem("c_kept", 2)
        hc0_done = sem("hc0_done", 2)
        hc1_done = sem("hc1_done", 2)
        y_step = sem("y_step", NHC)
        y_skip = sem("y_skip", MT)
        g_done = sem("g_done")
        mo_done = sem("mo_done", 1)
        mo_used = sem("mo_used", 1)
        wqkv_in = sem("wqkv_in")
        wo_in = sem("wo_in")
        w1_in = sem("w1_in")
        w2_in = sem("w2_in")
        tabs_done = sem("tabs_done")
        xs_ready = sem("xs_ready")
        proj_done = sem("proj_done")
        vproj_done = sem("vproj_done", 2 * NV)
        sq_ready = sem("sq_ready")
        sq_reduced = sem("sq_reduced", 2)
        ssq_ready = sem("ssq_ready")
        ln_done = sem("ln_done")
        r_done = sem("r_done")
        rope_q = sem("rope_q", 1)
        rope_k = sem("rope_k", 1)
        v_ready = sem("v_ready", 1)
        q_summed = sem("q_summed")
        k_summed = sem("k_summed", 2)
        k_scaled = sem("k_scaled")
        tr_done = sem("tr_done", 4)
        tr_act = sem("tr_act", 1)
        tr_dve = sem("tr_dve", 1)
        sA_done = sem("sA_done")
        sB_done = sem("sB_done", PAIRS)
        mx_step = sem("mx_step")
        nb_ready = sem("nb_ready")
        expA = sem("expA", 2)
        expB = sem("expB", 2)
        rinv_ready = sem("rinv_ready")
        normed = sem("normed")
        pt_done = sem("pt_done", 2 * NP_BUF)
        pt_evac0 = sem("pt_evac0")
        pt_evac1 = sem("pt_evac1", 1)
        pv_done = sem("pv_done", 2 * PAIRS)
        o_evac = sem("o_evac", 1)
        wo_done = sem("wo_done", NWO)
        x_added = sem("x_added", NWO)
        ag_done = sem("ag_done")
        gelu_done = sem("gelu_done")
        hid_done = sem("hid_done", NHT)
        y_done = sem("y_done", 2)
        x_next = sem("x_next", 2)
        f_sum = sem("f_sum")
        f_turned = sem("f_turned", 2)
        f_ready = sem("f_ready", 2)
        f_out = [sem(f"f_out{u}") for u in range(2)]

        block = ctx.enter_context(nc.Block())

        OUT_AT, D_AT, Z_AT, BC_AT = 2, 5, 9, 13

        def scan_loop(e, body):
            body(0, True, False)
            with e.Fori(1, GROUPS - 1) as g:
                body(g, False, False)
            body(GROUPS - 1, False, True)

        def group_loop(e, first, last, body):
            with e.Fori(first, last) as i:
                body(i)

        def swapped(a):
            return a.rearrange("p h (s e) -> p h s e", s=2)[:, :, ::-1, :]

        B_IN, B_GATE, CONV_B, B_DELTA, D_SK, B_OUT = range(6)

        @block.sync
        def _(sp):
            small = [
                (ident[:], t["ident"]), (ident16[:], t["ident16"]), (mask_a[:], t["mask_a"]), (mask_b[:], t["mask_b"]),
                (base_q[:], t["rope_q"]), (base_k[:], t["rope_k"]), (sel, t["sel"]),
                (w_in, t["L0_attn_W_in"]), (w_gate, t["L0_attn_W_gate"]),
                (w_delta, t["L0_attn_W_delta"].rearrange("(k p) n -> p k n", p=P)),
                (w_out, t["L0_attn_W_out"].rearrange("(k p) n -> p k n", p=P)),
                (conv_w, t["L0_attn_conv_w"].rearrange("(m p) o k -> p m (o k)", p=P)),
                (a_neg, t["L0_attn_A_log"].rearrange("(m p) n -> p m n", p=P)),
                (mpar[:, 0, B_OUT:B_OUT + 1], t["L0_attn_b_out"].rearrange("(p o) -> p o", o=1)),
            ]
            for col, name in ((B_IN, "b_in"), (B_GATE, "b_gate"), (CONV_B, "conv_b"), (B_DELTA, "b_delta"), (D_SK, "D_skip")):
                small.append((mpar[:, :, col], t[f"L0_attn_{name}"].rearrange("(m p) -> p m", p=P)))
            for copy in range(4):
                w = w_bc[:, :, 32 * copy:32 * copy + 32]
                small.append((w[:, :, 0:D_STATE], t["L0_attn_W_B"].rearrange("(k p) n -> p k n", p=P)))
                small.append((w[:, :, D_STATE:2 * D_STATE], t["L0_attn_W_C"].rearrange("(k p) n -> p k n", p=P)))
            with nc.allow_non_contiguous_dma("small parameters, once"):
                for dst, src in small:
                    sp.dma_start(dst, src).then_inc(const_in[0], 16)
            x_rows = t["L0_attn_x"].rearrange("s n f -> (s n) f")

            def load_pair(i):
                for u in range(2):
                    slot(sp, x_turned, i * 2 + u)
                    sp.dma_start(xtok[u], x_rows[ds((i * 2 + u) * GROUP, GROUP), :].rearrange("(c p) f -> p c f", p=P)) \
                        .then_inc(x_in[u][0], 16)
            group_loop(sp, 0, GROUPS // 2, load_pair)

            vectors = [(lpar_all[:, :, 0], t["L0_ffn_ln_g"]), (lpar_all[:, :, 1], t["L0_ffn_ln_b"]),
                       (lpar_all[:, :, 2], t["L0_ffn_b2"])]
            for m, (h0, hn) in enumerate(HT):
                vectors.append((lpar_all[0:hn, :, 3 + m], t["L0_ffn_b1"][:, h0:h0 + hn]))
                vectors.append((lpar_all[0:hn, :, 3 + NHT + m], t["L0_ffn_b1"][:, HID + h0:HID + h0 + hn]))
            sp.wait_ge(cleared[0], 1)
            with nc.allow_non_contiguous_dma("small parameters, once"):
                for dst, src in vectors:
                    sp.dma_start(dst, src.rearrange("l p -> p l")).then_inc(lpar_in[0], 16)
                for dst, src in ((scale_q, t["L0_ffn_q_scale"]), (scale_k, t["L0_ffn_k_scale"])):
                    sp.dma_start(dst[:], src.unsqueeze(0).to_broadcast([P, DEPTH, HEAD])).then_inc(lpar_in[0], 16)

            def load_layer_front(l):
                sp.dma_start(wqkv[:], t["L0_ffn_Wqkv"][ds(l, 1), :, :].rearrange("o p n -> p (o n)")).then_inc(wqkv_in[0], 16)
                sp.dma_start(wo[:], t["L0_ffn_Wo"][ds(l, 1), :, :].rearrange("o (a p) n -> p (o a) n", p=P)).then_inc(wo_in[0], 16)

            def load_layer_back(l):
                sp.dma_start(w1[:], t["L0_ffn_W1"][ds(l, 1), :, :].rearrange("o p n -> p (o n)")).then_inc(w1_in[0], 16)
                sp.dma_start(w2[:, 0:NHT - 1, :], t["L0_ffn_W2"][ds(l, 1), 0:(NHT - 1) * P, :].rearrange("o (a p) n -> p (o a) n", p=P)) \
                    .then_inc(w2_in[0], 16)
                h0, hn = HT[-1]
                sp.dma_start(w2[0:hn, NHT - 1:NHT, :], t["L0_ffn_W2"][ds(l, 1), h0:HID, :].rearrange("o p n -> p o n")).then_inc(w2_in[0], 16)

            load_layer_front(0)
            load_layer_back(0)
            with sp.Fori(1, DEPTH) as l:
                sp.wait_ge(wo_done[0], l * (BATCH * NWO) + wo_done[1])
                load_layer_front(l)
                sp.wait_ge(y_done[0], l * GROUPS + y_done[1])
                load_layer_back(l)

            out_rows = out.rearrange("s n f -> (s n) f")

            def store_pair(i):
                for u in range(2):
                    item(sp, f_ready, i * 2 + u)
                    sp.dma_start(out_rows[ds((i * 2 + u) * GROUP, GROUP), :].rearrange("(c p) f -> p c f", p=P), xtok[u]) \
                        .then_inc(f_out[u][0], 16)
            group_loop(sp, 0, GROUPS // 2, store_pair)
            for u in range(2):
                sp.wait_ge(f_out[u][0], 16 * (GROUPS // 2))

        N_CONST = 16 * (14 + 5 + 8)
        N_LPAR = 16 * (3 + 2 * NHT + 2)

        @block.gpsimd
        def _(pool):
            give_credits(pool, [k_summed, hc1_done])
            nc.gpsimd.memset(meanw[:], 1.0 / P)
            nc.gpsimd.memset(lpar_all[:], 0.0)
            nc.gpsimd.memset(eps[:], LN_EPS)
            nc.gpsimd.memset(w2[:, NHT - 1, :], 0.0)
            for u in range(2):
                nc.gpsimd.memset(hid_last[u][:], 0.0)
                nc.gpsimd.memset(xs[u][:, 0:1], 0.0)
            for m in range(MT):
                nc.gpsimd.memset(xz[m][:, :, 0:CONV - 1], 0.0)
            for n in range(NDA):
                last = nc.gpsimd.memset(dA[n].rearrange("p (s t) -> p s t", t=SEQ)[:, :, 0:1], 0.0)
            last.then_inc(cleared[0], 1)

            def scan_group(g):
                for n in range(D_STATE):
                    k = n * MT + 1
                    item(pool, c_kept, g * D_STATE + n)
                    item(pool, scan_done, g * (D_STATE * MT) + k)
                    slot(pool, y_step, g * (D_STATE * MT) + k)
                    nc.gpsimd.tensor_tensor(hc[k % NHC], hst[k % NHC], c_sb[n % 2], ALU.mult).then_inc(hc1_done[0], 1)
            group_loop(pool, 0, GROUPS, scan_group)

            item(pool, mo_used, GROUPS - 1)
            nc.gpsimd.memset(kT, 0.0)
            for n in range(NP_BUF):
                last = nc.gpsimd.memset(pB[n][:, :, 0:FIRST_B], 0.0)
            last.then_inc(cleared[0], 1)

            def k_unit(B, qn):
                ki = qn // 2
                b = ki % 2
                item(pool, rope_k, B * (NQK // 2) + ki)
                slot(pool, tr_done, B * NQK + qn)
                k2 = ks[b].rearrange("p (h e) -> p h e", h=8)
                nc.gpsimd.tensor_tensor(k2, tk[b][:, 0], tk[b][:, 1], ALU.add).then_inc(k_summed[0], 1)
                item(pool, k_summed, B * (NQK // 2) + ki)
                item(pool, r_done, B * NQK + qn)
                nc.gpsimd.tensor_tensor(k2, k2, rk[b][:, :].unsqueeze(2).to_broadcast([P, 8, HEAD]), ALU.mult).then_inc(k_scaled[0], 1)

            def q_unit(B, qn):
                b = qn // 2 % 2
                item(pool, rope_q, B * (NQK // 2) + qn // 2)
                nc.gpsimd.tensor_tensor(tq[b][:, 0], tq[b][:, 0], tq[b][:, 1], ALU.add).then_inc(q_summed[0], 1)

            def normalise(s, n):
                item(pool, rinv_ready, s)
                nc.gpsimd.tensor_tensor(pA[n], pA[n], rinv[n][:, 0:2].unsqueeze(2).to_broadcast([P, 2, P]), ALU.mult) \
                    .then_inc(normed[0], 1)
                pb = pB[n][:, :, FIRST_B:SEQ]
                nc.gpsimd.tensor_tensor(pb, pb, rinv[n][:, 2:4].unsqueeze(2).to_broadcast([P, 2, KEYS_B]), ALU.mult) \
                    .then_inc(normed[0], 1)

            def attention_slot(l, i, k, first, last):
                at_ = pair_at(l, i, k, LAG_NORMALISE, first, last)
                if at_:
                    normalise(at_[0], at_[4] % NP_BUF)
                at_ = unit_at(l, i, k, LAG_NORM, first, last)
                if at_:
                    (k_unit if at_[2] % 2 else q_unit)(at_[0], at_[2])

            with pool.Fori(0, DEPTH) as l:
                attention_slots(pool, l, attention_slot)

        @block.scalar
        def _(act_e):
            A = nc.scalar.activation
            give_credits(act_e, [pt_evac1, c_kept, ln_log, act_done, f_ready, v_ready, tr_act, expA, expB, o_evac] + in_used)
            act_e.wait_ge(const_in[0], N_CONST)
            act_e.wait_ge(cleared[0], 1)
            act_e.preload_act_table_set(EXP_LN_SET)
            A(a_neg, a_neg, ACT.Exp).then_inc(a_done[0], 1)

            def norms_of(g0):
                for u in range(NLN):
                    item(act_e, ln_xc, g0 + u)
                    A(sq2[u], xc[u], ACT.Square).then_inc(ln_sq[0], 1)
                for u in range(NLN):
                    item(act_e, ln_var, g0 + u)
                    slot(act_e, ln_out, g0 + u)
                    A(rstd[u], bank[NLN + u][:], ACT.Ln, bias=eps[:, 0:1]).then_inc(ln_log[0], 1)
                    item(act_e, ln_log, g0 + u)
                    A(rstd[u], rstd[u], ACT.Exp, scale=-0.5).then_inc(ln_rstd[0], 1)

            group_loop(act_e, 0, GROUPS // NLN, lambda i: norms_of(i * NLN))

            def mamba_in(g):
                for m in range(MT):
                    item(act_e, in_done, g * (2 * MT) + m)
                    slot(act_e, conv_done, g * MT + m)
                    A(xz[m][:, :, CONV - 1:], bank[m].rearrange("p (s t) -> p s t", t=SEQ), ACT.Identity,
                      bias=mpar[:, m, B_IN:B_IN + 1]).then_inc(in_used[m][0], 1)
                for m in range(MT):
                    item(act_e, in_done, g * (2 * MT) + (MT + m))
                    A(sgate[m][:, ds(g * GROUP, GROUP)], bank[MT + m][:], ACT.Silu, bias=mpar[:, m, B_GATE:B_GATE + 1]) \
                        .then_inc(in_used[MT + m][0], 1)
                for m in range(MT):
                    item(act_e, conv_done, g * MT + m)
                    A(act[m][:, ds(g * GROUP, GROUP)], cacc[m], ACT.Silu).then_inc(act_done[0], 1)

            act_e.preload_act_table(ACT.Silu)
            group_loop(act_e, 0, GROUPS, mamba_in)
            act_e.preload_act_table_set(EXP_LN_SET)

            def prepare(g, piece):
                step, m = divmod(piece, MT)
                if step == 0:
                    item(act_e, d_done, g * MT + m)
                    A(zabs[m], bank[6 + m][:], ACT.Abs, bias=mpar[:, m, B_DELTA:B_DELTA + 1]).then_inc(z_abs[0], 1)
                elif step == 1:
                    item(act_e, z_abs, g * MT + m)
                    A(zexp[m], zabs[m], ACT.Exp, scale=-1.0).then_inc(z_exp[0], 1)
                elif step == 2:
                    A(zpos[m], bank[6 + m][:], ACT.Relu, bias=mpar[:, m, B_DELTA:B_DELTA + 1]).then_inc(z_pos[0], 1)
                else:
                    item(act_e, z_exp, g * MT + m)
                    A(zlog[m], zexp[m], ACT.Ln, bias=1.0).then_inc(z_log[0], 1)

            def scan_group(g, first, last):
                for k in range(D_STATE * MT):
                    n, m = divmod(k, MT)
                    b = k % NDA
                    if 0 <= k - Z_AT * MT < 4 * MT and not last:
                        prepare(g + 1, k - Z_AT * MT)
                    if k < MT:
                        item(act_e, delta_done, g * MT + m)
                    act_e.wait_ge(scan_done[0], g * (D_STATE * MT) + (k + 1 if k >= NDA else NDA))
                    d3 = delta[m].rearrange("p (s t) -> p s t", t=SEQ)
                    a3 = dA[b].rearrange("p (s t) -> p s t", t=SEQ)
                    A(a3[:, :, 1:], d3[:, :, 1:], ACT.Exp, scale=a_neg[:, m, n:n + 1]).then_inc(dA_done[0], 1)
                    if m == 0:
                        item(act_e, c_ready, g * D_STATE + n)
                        slot(act_e, hc1_done, g * D_STATE + n)
                        A(c_sb[n % 2], bank[2 + n % 2][:], ACT.Copy).then_inc(c_kept[0], 1)

            item(act_e, a_done, 1)
            for piece in range(4 * MT):
                prepare(0, piece)
            scan_loop(act_e, scan_group)
            group_loop(act_e, 0, GROUPS // NLN, lambda i: norms_of(i * NLN + GROUPS))

            def norms(B, u, qn):
                c, j = QK_UNITS[qn]
                item(act_e, ssq_ready, B * NQK + qn)
                A(lnv[qn % 2][:], ssqc[qn % 2][:], ACT.Ln, scale=LN_SCALE).then_inc(ln_done[0], 1)
                item(act_e, ln_done, B * NQK + qn)
                dst = rq[u][:, c, 8 * j:8 * j + 8] if j < 2 else rk[qn // 2 % 2][:]
                A(dst, lnv[qn % 2][:], ACT.Exp, scale=-0.5).then_inc(r_done[0], 1)

            def evacuate(B, u, qn):
                c, j = QK_UNITS[qn]
                item(act_e, tr_done, B * NQK + qn)
                act_e.wait_ge(sB_done[0], B * PAIRS + (qn // 4 * 4 + 4))
                src = TRB.rearrange("p (a t) -> p a t", a=4)
                if j < 2:
                    A(qT[:, 4 * j:4 * j + 4, c * P:c * P + P], src, ACT.Copy).then_inc(tr_act[0], 1)
                else:
                    A(kT[64:P, 4 * (j - 2):4 * (j - 2) + 4, 1, c * P:c * P + P], src[64:P], ACT.Copy).then_inc(tr_act[0], 1)

            def squares(B, u, qn):
                item(act_e, proj_done, B * NQK + qn)
                slot(act_e, sq_reduced, B * NQK + qn)
                A(sq[qn % 2], (QB, KB)[qn % 2][:], ACT.Square).then_inc(sq_ready[0], 1)

            def v_evac(B, u, vn):
                c, j = V_UNITS[vn]
                item(act_e, vproj_done, B * NV + vn)
                act_e.wait_ge(pv_done[0], B * PAIRS + (vn // 2 * 4 + 4 + pv_done[1] - PAIRS))
                A(vv[:, c, 512 * (j - 4):512 * (j - 4) + 512], VOB[:], ACT.Copy).then_inc(v_ready[0], 1)

            def exps(s, n, u, p, blk):
                item(act_e, nb_ready, s * 2 + blk)
                if blk == 0:
                    act_e.wait_ge(pt_done[0], s * 2 + 2)
                for h in range(2):
                    if blk == 0:
                        src, dst, done = SAB[:, h * P:h * P + P], pA[n][:, h, :], expA
                    else:
                        src, dst, done = SBB[:, h * KEYS_B:(h + 1) * KEYS_B], pB[n][:, h, FIRST_B:SEQ], expB
                    A(dst, src, ACT.Exp, bias=nbias[n][:, 2 * blk + h:2 * blk + h + 1],
                      scale=rq[u][:, blk, 2 * p + h:2 * p + h + 1],
                      accum_out=rsum[n][:, 2 * blk + h:2 * blk + h + 1]).then_inc(done[0], 1)

            def probs_evac(s, b):
                item(act_e, pt_done, s * 2 + 1)
                act_e.wait_ge(pv_done[0], s + (2 * PAIRS - 1))
                A(pT[b][1], PTB[:, 0:P + WINDOW + P], ACT.Copy).then_inc(pt_evac1[0], 1)

            def out_evac(s, B, u, p):
                item(act_e, pv_done, s)
                act_e.wait_ge(wo_done[0], B * NWO + (p // 2 + 1))
                A(oT[:, p, :], OB[:, 0:SEQ], ACT.Copy).then_inc(o_evac[0], 1)

            def attention_slot(l, i, k, first, last):
                at_ = pair_at(l, i, k, LAG_OUT, first, last)
                if at_:
                    out_evac(*at_[:4])
                at_ = v_at(l, i, k, 1, first, last)
                if at_:
                    v_evac(*at_)
                at_ = unit_at(l, i, k, LAG_UNIT_OUT, first, last)
                if at_:
                    evacuate(*at_)
                at_ = unit_at(l, i, k, LAG_NORM, first, last)
                if at_:
                    norms(*at_)
                pair = pair_at(l, i, k, 0, first, last)
                if pair:
                    exps(pair[0], pair[4] % NP_BUF, pair[2], pair[3], 0)
                at_ = norm_at(l, i, k, LAG_VAR, first, last)
                if at_:
                    item(act_e, ln_var, at_[1])
                    item(act_e, ln_out, at_[1] + -1)
                    A(rstd[0], OB[:], ACT.Ln, bias=eps[:, 0:1]).then_inc(ln_log[0], 1)
                    item(act_e, ln_log, at_[1])
                    A(rstd[0], rstd[0], ACT.Exp, scale=-0.5).then_inc(ln_rstd[0], 1)
                if pair:
                    exps(pair[0], pair[4] % NP_BUF, pair[2], pair[3], 1)
                at_ = pair_at(l, i, k, LAG_TURN, first, last)
                if at_:
                    probs_evac(at_[0], at_[4] % 2)
                at_ = norm_at(l, i, k, LAG_MEAN, first, last)
                if at_:
                    item(act_e, ln_xc, at_[1])
                    A(sq2[0], xc[0], ACT.Square).then_inc(ln_sq[0], 1)
                at_ = unit_at(l, i, k, 0, first, last)
                if at_:
                    squares(*at_)

            def gelu_group(g, u):
                for m, (h0, hn) in enumerate(HT):
                    item(act_e, ag_done, g * NHT + m)
                    A(gl[m][0:hn], bank[NHT + m][0:hn, :], ACT.Gelu, bias=lpar[0:hn, 3 + NHT + m:4 + NHT + m]).then_inc(gelu_done[0], 1)

            act_e.wait_ge(cleared[0], 2)
            with act_e.Fori(0, DEPTH) as l:
                act_e.preload_act_table_set(EXP_LN_SET)
                attention_slots(act_e, l, attention_slot)
                act_e.preload_act_table(ACT.Gelu)
                with act_e.Fori(0, GROUPS // 2) as i:
                    for u in range(2):
                        gelu_group(l * GROUPS + i * 2 + u, u)

            def finish(i):
                for u in range(2):
                    item(act_e, f_turned, i * 2 + u)
                    act_e.wait_ge(f_out[u][0], i * 16) if not isinstance(i, int) or i else None
                    A(xtok[u], bank[u].rearrange("p (c f) -> p c f", f=DIM), ACT.Copy).then_inc(f_ready[0], 1)
            finish(0)
            group_loop(act_e, 1, GROUPS // 2, finish)

        @block.vector
        def _(dve):
            V = nc.vector
            give_credits(dve, [x_kept, ln_xc, ln_out, bc_split, dbx_done, scan_done, hc0_done, y_skip, mo_used,
                               sq_reduced, rope_q, rope_k, tr_dve, x_added, hid_done, x_next, conv_done])
            dve.wait_ge(const_in[0], N_CONST)
            dve.wait_ge(cleared[0], 1)

            def keep(i):
                for u in range(2):
                    item(dve, x_turned, i * 2 + u)
                    V.tensor_copy(x1T[:, ds((i * 2 + u) * GROUP, GROUP)], bank[u][:]).then_inc(x_kept[0], 1)
            group_loop(dve, 0, GROUPS // 2, keep)

            def plain_norm(g0, dst):
                def body(i):
                    for u in range(NLN):
                        item(dve, ln_mean, i * NLN + (g0 + u))
                        slot(dve, ln_out, i * NLN + (g0 + u))
                        V.tensor_tensor(xc[u], x1T[:, ds((i * NLN + u) * GROUP, GROUP)], bank[u][:], ALU.subtract).then_inc(ln_xc[0], 1)
                    for u in range(NLN):
                        item(dve, ln_rstd, i * NLN + (g0 + u))
                        V.tensor_tensor(dst[:, ds((i * NLN + u) * GROUP, GROUP)], xc[u], rstd[u], ALU.mult).then_inc(ln_out[0], 1)
                group_loop(dve, 0, GROUPS // NLN, body)

            item(dve, x_kept, GROUPS - 1)
            plain_norm(0, xnT)

            item(dve, a_done, 0)
            V.tensor_scalar(a_neg, a_neg, -1.0, None, ALU.mult).then_inc(a_done[0], 1)

            def conv_group(g):
                for m in range(MT):
                    item(dve, in_used[m], g)
                    slot(dve, act_done, g * MT + m)
                    c3 = cacc[m].rearrange("p (s t) -> p s t", t=SEQ)
                    V.tensor_scalar(c3, xz[m][:, :, CONV - 1:], conv_w[:, m, CONV - 1:CONV], mpar[:, m, CONV_B:CONV_B + 1],
                                    ALU.mult, ALU.add).then_inc(conv_step[0], 1)
                for tap in range(CONV - 2, -1, -1):
                    for m in range(MT):
                        step = (CONV - 2 - tap) * MT + m
                        item(dve, conv_step, g * ((CONV - 1) * MT) + step)
                        c3 = cacc[m].rearrange("p (s t) -> p s t", t=SEQ)
                        op = V.scalar_tensor_tensor(out=c3, in0=xz[m][:, :, tap:tap + SEQ], scalar=conv_w[:, m, tap:tap + 1],
                                                    in1=c3, op0=ALU.mult, op1=ALU.add)
                        op.then_inc(conv_step[0] if tap else conv_done[0], 1)
            group_loop(dve, 0, GROUPS, conv_group)

            steps = D_STATE * MT

            def inputs(g):
                cols = ds(g * GROUP, GROUP)
                item(dve, bc_done, g)
                V.tensor_copy(bc_parts, bank[6][:]).then_inc(bc_step[0], 1)
                for m in range(MT):
                    item(dve, z_log, g * MT + m)
                    item(dve, z_pos, g * MT + m)
                    V.tensor_tensor(delta[m], zpos[m], zlog[m], ALU.add).then_inc(delta_done[0], 1)
                item(dve, bc_step, g * 4)
                V.tensor_tensor(r1, bank[6][:], bc_parts, ALU.subtract).then_inc(bc_step[0], 1)
                item(dve, delta_done, g * MT)
                V.tensor_tensor(dx[0], delta[0], act[0][:, cols], ALU.mult).then_inc(dx_done[0], 1)
                item(dve, bc_step, g * 4 + 1)
                V.tensor_copy(bc_parts[32:64], r1[32:64])
                V.tensor_copy(bc_parts[64:P], r1[64:P]).then_inc(bc_step[0], 1)
                item(dve, bc_step, g * 4 + 2)
                V.tensor_tensor(r2[64:96], r1[64:96], bc_parts[64:96], ALU.subtract).then_inc(bc_step[0], 1)
                item(dve, bc_step, g * 4 + 3)
                V.tensor_copy(bc_parts[64:96], r2[64:96]).then_inc(bc_split[0], 1)
                item(dve, delta_done, g * MT + 1)
                V.tensor_tensor(dx[1], delta[1], act[1][:, cols], ALU.mult).then_inc(dx_done[0], 1)

            def gate(g):
                cols = ds(g * GROUP, GROUP)
                slot(dve, mo_done, g)
                for m in range(MT):
                    item(dve, y_step, g * steps + (steps - MT + m))
                    V.scalar_tensor_tensor(out=gated[m], in0=act[m][:, cols], scalar=mpar[:, m, D_SK:D_SK + 1], in1=bank[4 + m][:],
                                           op0=ALU.mult, op1=ALU.add).then_inc(y_skip[0], 1)
                for m in range(MT):
                    item(dve, y_skip, g * MT + m)
                    V.tensor_tensor(gated[m], gated[m], sgate[m][:, cols], ALU.mult).then_inc(g_done[0], 1)

            def add_output(g):
                cols = ds(g * GROUP, GROUP)
                item(dve, mo_done, g)
                V.scalar_tensor_tensor(out=x1T[:, cols], in0=bank[7][:], scalar=mpar[:, 0, B_OUT:B_OUT + 1], in1=x1T[:, cols],
                                       op0=ALU.add, op1=ALU.add).then_inc(mo_used[0], 1)

            def scan_group(g, first, last):
                for k in range(steps + 2):
                    if k == (OUT_AT + 3) * MT and not first:
                        add_output(g + -1)
                    if k < steps:
                        n, m = divmod(k, MT)
                        if k < MT:
                            item(dve, dx_done, g * MT + m)
                        item(dve, b_ready, g * D_STATE + n)
                        if k >= NH_BUF:
                            item(dve, scan_done, g * steps + (k - NH_BUF))
                        V.tensor_tensor(dbx[k % NH_BUF], dx[m], bank[n % 2][:], ALU.mult).then_inc(dbx_done[0], 1)
                    if 0 <= k - 1 < steps:
                        q = k - 1
                        item(dve, dA_done, g * steps + q)
                        item(dve, dbx_done, g * steps + q)
                        slot(dve, hc1_done if q % MT else hc0_done, g * D_STATE + q // MT)
                        V.tensor_tensor_scan(hst[q % NHC], dA[q % NDA], dbx[q % NH_BUF], 0.0, ALU.mult, ALU.add).then_inc(scan_done[0], 1)
                    if 0 <= k - 2 and k % MT == 0:
                        q = k - 2
                        n = q // MT
                        item(dve, c_kept, g * D_STATE + n)
                        item(dve, scan_done, g * steps + q)
                        slot(dve, y_step, g * steps + q)
                        V.tensor_tensor(hc[q % NHC], hst[q % NHC], bank[2 + n % 2][:], ALU.mult).then_inc(hc0_done[0], 1)
                if not last:
                    inputs(g + 1)
                gate(g)

            inputs(0)
            scan_loop(dve, scan_group)
            add_output(GROUPS - 1)

            item(dve, mo_used, GROUPS - 1)
            plain_norm(GROUPS, xT)

            def layer_tables(l):
                for c in range(CHUNKS):
                    for tab, base, sc in ((tab_q, base_q, scale_q), (tab_k, base_k, scale_k)):
                        V.tensor_tensor(tab[:, c], base[:, c], sc[:, ds(l, 1), :].to_broadcast([P, 2, HEAD]), ALU.mult) \
                            .then_inc(tabs_done[0], 1)
                V.tensor_copy(lpar[:], lpar_all[:, ds(l, 1), :].rearrange("p o n -> p (o n)")).then_inc(tabs_done[0], 1)

            def stage_x(B, u, col):
                dve.wait_ge(vproj_done[0], B * NV + NV)
                V.tensor_copy(xs[u][0:64, :], xT[0:64, ds(col, SEQ)])
                V.tensor_copy(xs[u][64:P, 1:SEQ], xT[64:P, ds(col, SEQ - 1)]).then_inc(xs_ready[0], 1)

            def evacuate(B, u, qn):
                c, j = QK_UNITS[qn]
                if j < 2:
                    return
                item(dve, tr_done, B * NQK + qn)
                dve.wait_ge(sB_done[0], B * PAIRS + (qn // 4 * 4 + 4))
                V.tensor_copy(kT[0:64, 4 * (j - 2):4 * (j - 2) + 4, 0, c * P:c * P + P],
                              TRB.rearrange("p (a t) -> p a t", a=4)[0:64]).then_inc(tr_dve[0], 1)

            def rope(B, u, qn):
                c, j = QK_UNITS[qn]
                item(dve, sq_ready, B * NQK + qn)
                V.tensor_reduce(ssq[qn % 2][:], sq[qn % 2].rearrange("p (h e) -> p h e", h=8), op=ALU.add, axis=AX.X) \
                    .then_inc(sq_reduced[0], 1)
                b = qn // 2 % 2
                tab, dst, done = (tab_q, tq[b], rope_q) if j < 2 else (tab_k, tk[b], rope_k)
                if j < 2:
                    slot(dve, tr_done, B * NQK + qn)
                else:
                    slot(dve, k_summed, B * (NQK // 2) + qn // 2)
                src = (QB, KB)[qn % 2].rearrange("p (h e) -> p h e", h=8)
                V.tensor_tensor(dst[:, 0], src, tab[:, c, 0:1, :].to_broadcast([P, 8, HEAD]), ALU.mult)
                V.tensor_tensor(swapped(dst[:, 1]), src.rearrange("p h (s e) -> p h s e", s=2),
                                tab[:, c, 1:2, :].rearrange("p o (s e) -> p o s e", s=2).to_broadcast([P, 8, 2, HALF]),
                                ALU.mult).then_inc(done[0], 1)
                item(dve, sq_reduced, B * NQK + qn)
                V.tensor_scalar(ssqc[qn % 2][:], ssq[qn % 2][:], NORM_FLOOR, None, ALU.max).then_inc(ssq_ready[0], 1)

            def maxima(s, n, u, p, blk):
                bank_, keys, done = (SAB, P, sA_done) if blk == 0 else (SBB, KEYS_B, sB_done)
                item(dve, done, s)
                V.reduce_max(mx[n][:, 2 * blk:2 * blk + 2], bank_[:, 0:2 * keys].rearrange("p (h t) -> p h t", h=2), AX.X).then_inc(mx_step[0], 1)

            def biases(s, n, u, p, blocks):
                item(dve, mx_step, s * 2 + blocks[-1])
                c = slice(blocks[0], blocks[-1] + 1)
                V.scalar_tensor_tensor(out=nbias[n].rearrange("p (c h) -> p c h", h=2)[:, c], in0=mx[n].rearrange("p (c h) -> p c h", h=2)[:, c],
                                       scalar=-1.0, in1=rq[u][:, c, 2 * p:2 * p + 2], op0=ALU.mult, op1=ALU.mult) \
                    .then_inc(nb_ready[0], len(blocks))

            def probs_evac(s, b):
                item(dve, pt_done, s * 2)
                dve.wait_ge(pv_done[0], s + (2 * PAIRS - 1))
                V.tensor_copy(pT[b][0], PTB[:, 0:P + WINDOW + P]).then_inc(pt_evac0[0], 1)

            def add_x(B, place, u, pc, more):
                item(dve, wo_done, B * NWO + pc)
                if pc:
                    item(dve, x_added, B * NWO + (pc - 1))
                cols = ds(place * SEQ, SEQ)
                V.tensor_tensor(xT[:, cols], VOB[:, 0:SEQ], xT[:, cols], ALU.add).then_inc(x_added[0], 1)

            def inverse(s, n):
                item(dve, expA, s * 2 + 1)
                item(dve, expB, s * 2 + 1)
                V.reciprocal(rinv[n][:], rsum[n][:]).then_inc(rinv_ready[0], 1)

            def stage_norm(group, n):
                item(dve, x_added, n * (SEQ_PER_GROUP * NWO) + (SEQ_PER_GROUP * NWO - 1 - 2 * GROUPS * SEQ_PER_GROUP * NWO))
                x3 = xT[:, ds(group * GROUP, GROUP)].rearrange("p (s t) -> p s t", t=SEQ)
                V.tensor_copy(xs2[0:64], x3[0:64])
                V.tensor_copy(xs2[64:P, :, 1:SEQ], x3[64:P, :, 0:SEQ - 1]).then_inc(ln_in[0], 1)

            def attention_slot(l, i, k, first, last):
                at_ = pair_at(l, i, k, LAG_NORMALISE, first, last)
                if at_:
                    inverse(at_[0], at_[4] % NP_BUF)
                at_ = wo_at(l, i, k, 1, first, last)
                if at_:
                    add_x(*at_)
                at_ = unit_at(l, i, k, LAG_UNIT_OUT, first, last)
                if at_:
                    evacuate(*at_)
                at_ = pair_at(l, i, k, 0, first, last)
                if at_:
                    s, B, u, p, t_ = at_
                    if p % 4 == 0:
                        item(dve, r_done, B * NQK + (p + 2))
                    maxima(s, t_ % NP_BUF, u, p, 0)
                    alone = last and t_ >= PAIRS
                    if alone:
                        biases(s, t_ % NP_BUF, u, p, [0])
                    maxima(s, t_ % NP_BUF, u, p, 1)
                    biases(s, t_ % NP_BUF, u, p, [1] if alone else [0, 1])
                at_ = norm_at(l, i, k, LAG_MEAN, first, last)
                if at_:
                    item(dve, ln_mean, at_[1])
                    V.tensor_tensor(xc[0], xs2.rearrange("p s t -> p (s t)"), OB[:], ALU.subtract).then_inc(ln_xc[0], 1)
                turned = pair_at(l, i, k, LAG_TURN, first, last)
                if turned:
                    probs_evac(turned[0], turned[4] % 2)
                at_ = unit_at(l, i, k, LAG_ROPE, first, last)
                if at_:
                    rope(*at_)
                at_ = unit_at(l, i, k, -1, first, last)
                if at_ and at_[2] == 0 and k >= -1:
                    stage_x(at_[0], at_[1], i * (2 * SEQ) + ((k + 1) // PAIRS + 1) * SEQ)
                at_ = norm_at(l, i, k, 0, first, last)
                if at_:
                    stage_norm(*at_[:2])
                at_ = norm_at(l, i, k, LAG_RSTD, first, last)
                if at_:
                    item(dve, ln_rstd, at_[1])
                    V.scalar_tensor_tensor(out=xc[0], in0=xc[0], scalar=lpar[:, 0:1], in1=rstd[0], op0=ALU.mult, op1=ALU.mult) \
                        .then_inc(ln_aff[0], 1)
                at_ = norm_at(l, i, k, LAG_NORMED, first, last)
                if at_:
                    item(dve, ln_aff, at_[1] + -2 * GROUPS)
                    V.tensor_scalar(xnT[:, ds(at_[0] * GROUP, GROUP)], xc[0], lpar[:, 1:2], None, ALU.add).then_inc(ln_out[0], 1)

            dve.wait_ge(lpar_in[0], N_LPAR)
            dve.wait_ge(cleared[0], 2)
            item(dve, ln_out, 2 * GROUPS - 1)
            V.memset(xs2[:, :, 0:1], 0.0)
            with dve.Fori(0, DEPTH) as l:
                layer_tables(l)
                item(dve, tabs_done, l * (2 * CHUNKS + 1) + 2 * CHUNKS)
                stage_x(l * BATCH, 0, 0)
                attention_slots(dve, l, attention_slot)

                with dve.Fori(0, GROUPS // 2) as i:
                    for u in range(2):
                        g = l * GROUPS + i * 2 + u
                        slot(dve, y_done, g)
                        for m, (h0, hn) in enumerate(HT):
                            item(dve, gelu_done, g * NHT + m)
                            V.scalar_tensor_tensor(out=hid[u][m][0:hn], in0=bank[m][0:hn, :], scalar=lpar[0:hn, 3 + m:4 + m],
                                                   in1=gl[m][0:hn], op0=ALU.add, op1=ALU.mult).then_inc(hid_done[0], 1)
                        item(dve, y_done, g)
                        cols = ds((i * 2 + u) * GROUP, GROUP)
                        V.scalar_tensor_tensor(out=xT[:, cols], in0=bank[2 * NHT + u][:], scalar=lpar[:, 2:3], in1=xT[:, cols],
                                               op0=ALU.add, op1=ALU.add).then_inc(x_next[0], 1)
                item(dve, x_next, l * GROUPS + (GROUPS - 1))

            def finish(i):
                for u in range(2):
                    cols = ds((i * 2 + u) * GROUP, GROUP)
                    slot(dve, f_turned, i * 2 + u)
                    V.tensor_tensor(fin[u], x1T[:, cols], xT[:, cols], ALU.add).then_inc(f_sum[0], 1)
            group_loop(dve, 0, GROUPS // 2, finish)

        @block.tensor
        def _(pe):
            give_credits(pe, [x_turned, y_step, mo_done, vproj_done, tr_done, sB_done, pt_done, pv_done, wo_done, y_done, f_turned])
            MM = nc.tensor.matmul

            def turn(out_, in_, **kw):
                k = in_.shape[0]
                return MM(out_, lhsT=in_, rhs=ident[0:k, 0:k], is_transpose=True, **kw)

            pe.wait_ge(const_in[0], N_CONST)
            pe.wait_ge(cleared[0], 1)

            def load_pair(i):
                for u in range(2):
                    pe.wait_ge(x_in[u][0], i * 16 + 16)
                    slot(pe, x_kept, i * 2 + u)
                    for c in range(GROUP // P):
                        last = turn(bank[u][:, c * P:(c + 1) * P], xtok[u][:, c, :], start=True, stop=True)
                    last.then_inc(x_turned[0], 1)
            group_loop(pe, 0, GROUPS // 2, load_pair)

            def norms_of(i, g0):
                for u in range(NLN):
                    slot(pe, ln_xc, i * NLN + (g0 + u))
                    MM(bank[u][:], lhsT=meanw[:], rhs=x1T[:, ds((i * NLN + u) * GROUP, GROUP)], start=True, stop=True).then_inc(ln_mean[0], 1)
                for u in range(NLN):
                    item(pe, ln_sq, i * NLN + (g0 + u))
                    slot(pe, ln_log, i * NLN + (g0 + u))
                    MM(bank[NLN + u][:], lhsT=meanw[:], rhs=sq2[u], start=True, stop=True).then_inc(ln_var[0], 1)

            item(pe, x_kept, GROUPS - 1)
            group_loop(pe, 0, GROUPS // NLN, lambda i: norms_of(i, 0))

            def mamba_in(g):
                rhs = xnT[:, ds(g * GROUP, GROUP)]
                for n in range(2 * MT):
                    slot(pe, in_used[n], g)
                    w = (w_in, w_gate)[n // MT]
                    m = n % MT
                    MM(bank[n][:], lhsT=w[:, m * P:(m + 1) * P], rhs=rhs, start=True, stop=True).then_inc(in_done[0], 1)

            item(pe, ln_out, GROUPS - 1)
            group_loop(pe, 0, GROUPS, mamba_in)

            steps = D_STATE * MT

            def delta_product(g, m, k, after=None):
                if m == 0 and k == 0:
                    slot(pe, bc_split, g)
                if m == 1 and k == 0 and after is not None:
                    item(pe, mo_used, after)
                mm = MM(bank[6 + m][:], lhsT=w_delta[:, k, m * P:(m + 1) * P], rhs=act[k][:, ds(g * GROUP, GROUP)], start=k == 0, stop=k == MT - 1)
                if k == MT - 1:
                    mm.then_inc(d_done[0], 1)

            def bc_product(g, k):
                if k == 0:
                    item(pe, z_pos, g * MT)
                mm = MM(bank[6][:], lhsT=w_bc[:, k, :], rhs=act[k][:, ds(g * GROUP, GROUP)], start=k == 0, stop=k == MT - 1)
                if k == MT - 1:
                    mm.then_inc(bc_done[0], 1)

            def output_product(g, m, after):
                if m == 0:
                    item(pe, z_pos, after * MT + 1)
                item(pe, g_done, g * MT + m)
                mm = MM(bank[7][:], lhsT=w_out[:, m, :], rhs=gated[m], start=m == 0, stop=m == MT - 1)
                if m == MT - 1:
                    mm.then_inc(mo_done[0], 1)

            def scan_group(g, first, last):
                def spread_b(n):
                    pe.wait_ge(dbx_done[0], g * steps + (n + 1) * MT)
                    MM(bank[n % 2][:], lhsT=sel[:, n, :], rhs=bc_parts, start=True, stop=True).then_inc(b_ready[0], 1)

                def spread_c(n):
                    slot(pe, hc0_done, g * D_STATE + n)
                    slot(pe, c_kept, g * D_STATE + n)
                    MM(bank[2 + n % 2][:], lhsT=sel[:, D_STATE + n, :], rhs=bc_parts, start=True, stop=True).then_inc(c_ready[0], 1)

                item(pe, bc_split, g)
                spread_b(0)
                spread_c(0)
                for n in range(D_STATE + 1):
                    if n + 1 < D_STATE:
                        spread_b(n + 1)
                    for m in range(MT):
                        k = (n - 1) * MT + m
                        if k >= 0:
                            item(pe, (hc0_done, hc1_done)[m], g * D_STATE + (n - 1))
                            if n == 1:
                                slot(pe, y_skip, g * MT + m)
                            MM(bank[4 + m][:], lhsT=ident[:], rhs=hc[k % NHC], start=n == 1, stop=n == D_STATE).then_inc(y_step[0], 1)
                    if n + 1 < D_STATE:
                        spread_c(n + 1)
                    if 0 <= n - OUT_AT < MT and not first:
                        output_product(g + -1, n - OUT_AT, g)
                    if 0 <= n - D_AT < MT * MT and not last:
                        delta_product(g + 1, (n - D_AT) // MT, (n - D_AT) % MT, None if first else g + -1)
                    if 0 <= n - BC_AT < MT and not last:
                        bc_product(g + 1, n - BC_AT)

            item(pe, act_done, GROUPS * MT - 1)
            for n in range(2 * MT):
                item(pe, in_used[n], GROUPS - 1)
            for m in range(MT):
                for k in range(MT):
                    delta_product(0, m, k)
            for k in range(MT):
                bc_product(0, k)
            scan_loop(pe, scan_group)
            for m in range(MT):
                output_product(GROUPS - 1, m, GROUPS - 1)
            item(pe, mo_used, GROUPS - 1)
            group_loop(pe, 0, GROUPS // NLN, lambda i: norms_of(i, GROUPS))
            item(pe, ln_out, 2 * GROUPS - 1)

            def transposes(B, u, qn):
                c, j = QK_UNITS[qn]
                b = qn // 2 % 2
                slot(pe, tr_act, B * NQK + qn)
                if j < 2:
                    slot(pe, tr_dve, B * (NQK // 2) + qn // 2)
                    item(pe, q_summed, B * (NQK // 2) + qn // 2)
                    for a in range(4):
                        last = turn(TRB[:, a * P:(a + 1) * P], tq[b][:, 0, 2 * a:2 * a + 2, :].rearrange("p h e -> p (h e)"), start=True, stop=True)
                else:
                    item(pe, k_scaled, B * (NQK // 2) + qn // 2)
                    for a in range(4):
                        last = turn(TRB[:, a * P:(a + 1) * P], ks[b][:, a * P:(a + 1) * P], start=True, stop=True)
                last.then_inc(tr_done[0], 1)

            def projection(dst, u, c, j):
                return MM(dst[:], lhsT=xs[u][:, c * P:(c + 1) * P], rhs=wqkv[:, j * 512:(j + 1) * 512], start=True, stop=True)

            def unit(B, u, qn):
                c, j = QK_UNITS[qn]
                if qn == 0:
                    item(pe, xs_ready, B)
                slot(pe, rope_q if j < 2 else rope_k, B * (NQK // 2) + qn // 2)
                projection((QB, KB)[qn % 2], u, c, j).then_inc(proj_done[0], 1)

            def v_unit(B, u, vn):
                c, j = V_UNITS[vn]
                slot(pe, v_ready, B * NV + vn)
                slot(pe, x_added, B * NWO + vn)
                projection(VOB, u, c, j).then_inc(vproj_done[0], 1)

            def scores(s, B, u, p):
                if p % 4 == 0:
                    item(pe, tr_act, B * NQK + (p + 3))
                    item(pe, tr_dve, B * (NQK // 2) + (p // 2 + 1))
                for bank_, first, keys, mask, free, done, q0 in (
                        (SAB, 0, P, mask_a, expA, sA_done, 0), (SBB, FIRST_B, KEYS_B, mask_b, expB, sB_done, P)):
                    pe.wait_ge(free[0], s * 2 + 2)
                    dst = bank_[:, 0:2 * keys]
                    MM(dst, lhsT=ident16[:], rhs=mask[:, :].unsqueeze(1).to_broadcast([P, 2, keys]), start=True, stop=False)
                    MM(dst, lhsT=qT[:, p, q0:q0 + P], rhs=kT[:, p, :, first:first + keys], start=False, stop=True) \
                        .then_inc(done[0], 1)

            def probs_turn(s, n, h):
                if h == 0:
                    slot(pe, pt_evac1, s)
                else:
                    item(pe, pt_evac0, s)
                if h == 0:
                    item(pe, normed, s * 2 + 1)
                turn(PTB[:, 0:P], pA[n][:, h, :], start=True, stop=True)
                turn(PTB[:, P:P + WINDOW], pB[n][0:WINDOW, h, 0:P], start=True, stop=True)
                turn(PTB[:, P + WINDOW:2 * P + WINDOW], pB[n][:, h, P:SEQ], start=True, stop=True).then_inc(pt_done[0], 1)

            def values(s, B, u, p, b):
                item(pe, pt_evac1, s)
                slot(pe, o_evac, s)
                if p % 4 == 0:
                    item(pe, v_ready, B * NV + (p // 4 * 2 + 1))
                for c, q0, t0, n in ((0, 0, 0, P + WINDOW), (1, P, P + WINDOW, P)):
                    for h in range(2):
                        col = (2 * p + h) * HEAD
                        last = MM(OB[64 * h:64 * h + 64, q0:q0 + n], lhsT=vv[:, c, col:col + HEAD], rhs=pT[b][h][:, t0:t0 + n],
                                  start=c == 0, stop=c == 1, skip_group_check=True)
                last.then_inc(pv_done[0], 1)

            def project(B, place, u, pc, more):
                item(pe, o_evac, B * PAIRS + (2 * pc + 1))
                pe.wait_ge(x_added[0], B * NWO + (pc + x_added[1]))
                if more or pc == 0:
                    item(pe, v_ready, B * NV + (NV - 1 + pc))
                for a in (2 * pc, 2 * pc + 1):
                    last = MM(VOB[:, 0:SEQ], lhsT=wo[:, a, :], rhs=oT[:, a, :], start=a % 2 == 0, stop=a % 2 == 1)
                last.then_inc(wo_done[0], 1)

            def attention_slot(l, i, k, first, last):
                at_ = pair_at(l, i, k, 0, first, last)
                if at_:
                    scores(*at_[:4])
                mean = norm_at(l, i, k, LAG_MEAN, first, last)
                if mean:
                    item(pe, ln_in, mean[1] + -2 * GROUPS)
                    item(pe, o_evac, mean[2])
                    MM(OB[:], lhsT=meanw[:], rhs=xs2.rearrange("p s t -> p (s t)"), start=True, stop=True).then_inc(ln_mean[0], 1)
                var = norm_at(l, i, k, LAG_VAR, first, last)
                if var:
                    item(pe, ln_sq, var[1])
                    item(pe, o_evac, var[2])
                    MM(OB[:], lhsT=meanw[:], rhs=sq2[0], start=True, stop=True).then_inc(ln_var[0], 1)
                turned = pair_at(l, i, k, LAG_TURN, first, last)
                if turned:
                    probs_turn(turned[0], turned[4] % NP_BUF, 0)
                at_ = unit_at(l, i, k, 0, first, last)
                if at_:
                    unit(*at_)
                at_ = v_at(l, i, k, 0, first, last)
                if at_:
                    v_unit(*at_)
                at_ = wo_at(l, i, k, 0, first, last)
                if at_:
                    project(*at_)
                if turned:
                    probs_turn(turned[0], turned[4] % NP_BUF, 1)
                at_ = unit_at(l, i, k, LAG_UNIT_TURN, first, last)
                if at_:
                    transposes(*at_)
                at_ = pair_at(l, i, k, LAG_VALUES, first, last)
                if at_:
                    s, B, u, p, t_ = at_
                    if mean:
                        item(pe, ln_xc, mean[1])
                    if var:
                        item(pe, ln_log, var[1])
                    values(s, B, u, p, t_ % 2)

            with pe.Fori(0, DEPTH) as l:
                pe.wait_ge(wqkv_in[0], l * 16 + 16)
                pe.wait_ge(wo_in[0], l * 16 + 16)
                attention_slots(pe, l, attention_slot)

                with pe.Fori(0, GROUPS // 2) as i:
                    pe.wait_ge(w1_in[0], l * 16 + 16)
                    pe.wait_ge(w2_in[0], l * 32 + 32)
                    item(pe, ln_out, l * GROUPS + (3 * GROUPS - 1))

                    def up(u, m):
                        g = l * GROUPS + i * 2 + u
                        h0, hn = HT[m]
                        rhs = xnT[:, ds((i * 2 + u) * GROUP, GROUP)]
                        slot(pe, hid_done, g * NHT + m)
                        MM(bank[m][0:hn, :], lhsT=w1[:, h0:h0 + hn], rhs=rhs, start=True, stop=True)
                        MM(bank[NHT + m][0:hn, :], lhsT=w1[:, HID + h0:HID + h0 + hn], rhs=rhs, start=True, stop=True) \
                            .then_inc(ag_done[0], 1)

                    def down(u):
                        g = l * GROUPS + i * 2 + u
                        slot(pe, x_next, g)
                        for m in range(NHT):
                            item(pe, hid_done, g * NHT + m)
                            last = MM(bank[2 * NHT + u][:], lhsT=w2[:, m, :], rhs=hid[u][m], start=m == 0, stop=m == NHT - 1)
                        last.then_inc(y_done[0], 1)

                    for m in range(NHT):
                        up(0, m)
                    up(1, 0)
                    down(0)
                    for m in range(1, NHT):
                        up(1, m)
                    down(1)

            def finish(i):
                for u in range(2):
                    item(pe, f_sum, i * 2 + u)
                    slot(pe, f_ready, i * 2 + u)
                    for c in range(GROUP // P):
                        last = turn(bank[u][:, c * P:(c + 1) * P], fin[u][:, c * P:(c + 1) * P], start=True, stop=True)
                    last.then_inc(f_turned[0], 1)
            group_loop(pe, 0, GROUPS // 2, finish)


_NAMES = ['L0_attn_x', 'L0_attn_W_in', 'L0_attn_b_in', 'L0_attn_W_gate', 'L0_attn_b_gate', 'L0_attn_conv_w',
          'L0_attn_conv_b', 'L0_attn_A_log', 'L0_attn_D_skip', 'L0_attn_W_delta', 'L0_attn_b_delta', 'L0_attn_W_B',
          'L0_attn_W_C', 'L0_attn_W_out', 'L0_attn_b_out', 'L0_ffn_Wqkv', 'L0_ffn_q_scale', 'L0_ffn_k_scale',
          'L0_ffn_Wo', 'L0_ffn_ln_g', 'L0_ffn_ln_b', 'L0_ffn_W1', 'L0_ffn_b1', 'L0_ffn_W2', 'L0_ffn_b2']


def constants():
    import numpy as np
    bf = mybir.dt.np(mybir.dt.bfloat16)
    f = np.float32
    out = {"ident": np.eye(P, dtype=f), "ident16": np.eye(P).astype(bf)}
    i, k = np.arange(P)[:, None], np.arange(P)[None, :]
    out["mask_a"] = np.where((k <= i) & (k >= i - WINDOW), 0.0, MASKED).astype(bf)
    i, k = i + P, np.arange(FIRST_B, SEQ)[None, :]
    out["mask_b"] = np.where((k <= i) & (k >= i - WINDOW), 0.0, MASKED).astype(bf)
    sel = np.zeros((P, 2 * D_STATE, P))
    for n in range(2 * D_STATE):
        sel[[n, 32 + n, 64 + n], n, :] = 1.0
    out["sel"] = sel.astype(bf)
    half = np.arange(0, HEAD, 2, dtype=f)
    inv_freq = (f(1.0) / np.power(f(10000.0), half / f(HEAD))).astype(f)
    pos = np.arange(SEQ, dtype=f)
    freqs = (pos[:, None] * inv_freq[None, :]).astype(f)
    freqs = np.concatenate([freqs, freqs], -1).astype(np.float64)
    base = ((half + f(0.4 * HEAD)) / f(1.4 * HEAD)).astype(f)
    power = ((pos - SEQ // 2) / f(WINDOW // 2)).astype(f)
    scale = np.power(base[None, :].astype(np.float64), power[:, None].astype(np.float64))
    scale = np.concatenate([scale, scale], -1)
    sign = np.where(np.arange(HEAD) < HALF, 1.0, -1.0)[None, :]
    for name, sc in (("rope_q", scale * 8.0), ("rope_k", 1.0 / scale)):
        tab = np.stack([np.cos(freqs) * sc, np.sin(freqs) * sc * sign], 1) * 2.0 ** 16
        out[name] = np.ascontiguousarray(tab.reshape(CHUNKS, P, 2, HEAD).transpose(1, 0, 2, 3)).astype(f)
    return out


def kernel(**inputs):
    import numpy as np
    import concourse.bacc as bacc
    from concourse.bass_utils import run_bass_kernel_spmd

    nc = bacc.Bacc("TRN2", target_bir_lowering=False, num_devices=1)
    arrays, aps = {}, {}
    given = {n: np.ascontiguousarray(inputs[n]) for n in _NAMES}
    given.update(constants())
    for name, a in given.items():
        arrays["in_" + name] = a
        aps[name] = nc.dram_tensor("in_" + name, a.shape, mybir.dt.from_np(a.dtype), kind="ExternalInput").ap()
    out = nc.dram_tensor("out", (BATCH, SEQ, DIM), mybir.dt.float32, kind="ExternalOutput").ap()
    build(nc, aps, out)
    r = run_bass_kernel_spmd(nc, [arrays], core_ids=[0])
    return r.results[0]["out"]
```
